# Optimizing a Trainium2 kernel written in Bass

```python
import numpy as np
import jax
import jax.numpy as jnp

def _softmax(x, axis=-1):
    return jax.nn.softmax(x, axis=axis)

def _gelu(x):
    return jax.nn.gelu(x, approximate=True)

def _silu(x):
    return jax.nn.silu(x)

def _sigmoid(x):
    return jax.nn.sigmoid(x)

def _layernorm(x, axis=-1, eps=1e-05):
    m = jnp.mean(x, axis=axis, keepdims=True)
    v = jnp.var(x, axis=axis, keepdims=True)
    return (x - m) / jnp.sqrt(v + eps)

def _scatter_add(tgt, idx, src, axis=0):
    return tgt.at[idx].add(src)

def _segment_sum(src, seg, n):
    return jax.ops.segment_sum(src, seg, n)
kernel_name = 'mk_gnn_ffn_d1_gnn_r32_94c814'

def setup_inputs(seed: int=0):
    np.random.seed(seed)
    _w = jnp.asarray

    def _rec_inputs():
        import jax
        import jax.numpy as jnp
        _gk = jax.random.key(seed)
        x = -0.0002117 + 1 * jax.random.normal(jax.random.fold_in(_gk, 1), (3125, 256), jnp.float32)
        src = jax.random.randint(jax.random.fold_in(_gk, 2), (50000,), 0, 3125, jnp.int32)
        dst = jnp.minimum((3125 * jax.random.uniform(jax.random.fold_in(_gk, 3), (50000,)) ** 2.0).astype(jnp.int32), 99999)
        _o = jnp.argsort(dst, stable=True)
        src = src[_o]
        dst = dst[_o]
        edge_weight = 0.000714719 + 1.00021 * jax.random.normal(jax.random.fold_in(_gk, 12), (50000,), jnp.float32)
        return (x, src, dst, edge_weight)
    x, src, dst, edge_weight = _rec_inputs()

    def _L0_gnn_setup():
        import jax, jax.numpy as jnp
        import numpy as np
        N = 3125
        E = 100000
        D = 256
        LN_EPS = 1e-05

        def _safe(x):
            return jnp.nan_to_num(x, nan=0.0, posinf=0.0, neginf=0.0)

        def _layernorm(h, g, b):
            mu = jnp.mean(h, axis=-1, keepdims=True)
            var = jnp.mean(jnp.square(h - mu), axis=-1, keepdims=True)
            return (h - mu) * jax.lax.rsqrt(var + LN_EPS) * g + b

        def _gcn_conv(h, row, col, ew, dis, W, b):
            xw = h @ W
            norm = dis[row] * ew * dis[col]
            msg = norm[:, None] * xw[row]
            agg = jax.ops.segment_sum(msg, col, num_segments=N)
            agg = agg + (dis * dis)[:, None] * xw
            return agg + b
        key = jax.random.key(seed)
        ks = jax.random.split(key, 8)
        x = jax.random.normal(ks[0], (N, D), dtype=jnp.float32)
        edge_index = jax.random.randint(ks[1], (2, E), 0, N, dtype=jnp.int64)
        edge_weight = jax.random.normal(ks[2], (E,), dtype=jnp.float32)
        s = 1.0 / np.sqrt(D)
        W1 = jax.random.uniform(ks[3], (D, D), jnp.float32, -s, s)
        W2 = jax.random.uniform(ks[4], (D, D), jnp.float32, -s, s)
        b1 = jax.random.uniform(ks[5], (D,), jnp.float32, -s, s)
        b2 = jax.random.uniform(ks[6], (D,), jnp.float32, -s, s)
        ln_g1 = jnp.ones((D,), jnp.float32)
        ln_b1 = jnp.zeros((D,), jnp.float32)
        ln_g2 = jnp.ones((D,), jnp.float32)
        ln_b2 = jnp.zeros((D,), jnp.float32)
        return dict(x=x, edge_index=edge_index, edge_weight=edge_weight, W1=W1, b1=b1, ln_g1=ln_g1, ln_b1=ln_b1, W2=W2, b2=b2, ln_g2=ln_g2, ln_b2=ln_b2)
    _L0_gnn_all = _L0_gnn_setup()
    _L0_gnn_in = {k: v for k, v in _L0_gnn_all.items() if k in ('W1', 'b1', 'ln_g1', 'ln_b1', 'W2', 'b2', 'ln_g2', 'ln_b2')}
    del _L0_gnn_all

    def _L0_ffn_setup():
        import jax, jax.numpy as jnp
        import numpy as np
        BN_EPS = 0.001

        def _bn(h, g, b, m, v):
            return g * (h - m) * jax.lax.rsqrt(v + BN_EPS) + b
        key = jax.random.key(seed)
        ks = jax.random.split(key, 8)
        B, F, Df = (256, 64, 256)
        E, H, D = (8, 256, 256)
        s1 = 1.0 / np.sqrt(Df)
        s2 = 1.0 / np.sqrt(H)
        return {'x': jax.random.normal(ks[0], (B, F, Df), jnp.float32), 'Wr': jax.random.normal(ks[1], (Df, E), jnp.float32) * s1, 'br': jnp.zeros((E,), jnp.float32), 'W1': jax.random.normal(ks[2], (E, Df, H), jnp.float32) * s1, 'b1': jnp.zeros((E, H), jnp.float32), 'g1': jnp.ones((E, H), jnp.float32), 'be1': jnp.zeros((E, H), jnp.float32), 'm1': jnp.zeros((E, H), jnp.float32), 'v1': jnp.ones((E, H), jnp.float32), 'W2': jax.random.normal(ks[3], (E, H, H), jnp.float32) * s2, 'b2': jnp.zeros((E, H), jnp.float32), 'g2': jnp.ones((E, H), jnp.float32), 'be2': jnp.zeros((E, H), jnp.float32), 'm2': jnp.zeros((E, H), jnp.float32), 'v2': jnp.ones((E, H), jnp.float32), 'Wo': jax.random.normal(ks[4], (E, H, D), jnp.float32) * s2, 'bo': jnp.zeros((E, D), jnp.float32)}
    _L0_ffn_all = _L0_ffn_setup()
    _L0_ffn_in = {k: v for k, v in _L0_ffn_all.items() if k in ('Wr', 'br', 'W1', 'b1', 'g1', 'be1', 'm1', 'v1', 'W2', 'b2', 'g2', 'be2', 'm2', 'v2', 'Wo', 'bo')}
    del _L0_ffn_all
    return {'x': x, 'src': src, 'dst': dst, 'edge_weight': edge_weight, 'L0_gnn_W1': _L0_gnn_in['W1'], 'L0_gnn_b1': _L0_gnn_in['b1'], 'L0_gnn_ln_g1': _L0_gnn_in['ln_g1'], 'L0_gnn_ln_b1': _L0_gnn_in['ln_b1'], 'L0_gnn_W2': _L0_gnn_in['W2'], 'L0_gnn_b2': _L0_gnn_in['b2'], 'L0_gnn_ln_g2': _L0_gnn_in['ln_g2'], 'L0_gnn_ln_b2': _L0_gnn_in['ln_b2'], 'L0_ffn_Wr': _L0_ffn_in['Wr'], 'L0_ffn_br': _L0_ffn_in['br'], 'L0_ffn_W1': _L0_ffn_in['W1'], 'L0_ffn_b1': _L0_ffn_in['b1'], 'L0_ffn_g1': _L0_ffn_in['g1'], 'L0_ffn_be1': _L0_ffn_in['be1'], 'L0_ffn_m1': _L0_ffn_in['m1'], 'L0_ffn_v1': _L0_ffn_in['v1'], 'L0_ffn_W2': _L0_ffn_in['W2'], 'L0_ffn_b2': _L0_ffn_in['b2'], 'L0_ffn_g2': _L0_ffn_in['g2'], 'L0_ffn_be2': _L0_ffn_in['be2'], 'L0_ffn_m2': _L0_ffn_in['m2'], 'L0_ffn_v2': _L0_ffn_in['v2'], 'L0_ffn_Wo': _L0_ffn_in['Wo'], 'L0_ffn_bo': _L0_ffn_in['bo']}

def reference(x, src, dst, edge_weight, L0_gnn_W1, L0_gnn_b1, L0_gnn_ln_g1, L0_gnn_ln_b1, L0_gnn_W2, L0_gnn_b2, L0_gnn_ln_g2, L0_gnn_ln_b2, L0_ffn_Wr, L0_ffn_br, L0_ffn_W1, L0_ffn_b1, L0_ffn_g1, L0_ffn_be1, L0_ffn_m1, L0_ffn_v1, L0_ffn_W2, L0_ffn_b2, L0_ffn_g2, L0_ffn_be2, L0_ffn_m2, L0_ffn_v2, L0_ffn_Wo, L0_ffn_bo):
    import jax
    import jax.numpy as jnp

    def _L0_gnn_ref(x, edge_index, edge_weight, W1, b1, ln_g1, ln_b1, W2, b2, ln_g2, ln_b2):
        import jax, jax.numpy as jnp
        import numpy as np
        N = 3125
        E = 100000
        D = 256
        LN_EPS = 1e-05

        def _safe(x):
            return jnp.nan_to_num(x, nan=0.0, posinf=0.0, neginf=0.0)

        def _layernorm(h, g, b):
            mu = jnp.mean(h, axis=-1, keepdims=True)
            var = jnp.mean(jnp.square(h - mu), axis=-1, keepdims=True)
            return (h - mu) * jax.lax.rsqrt(var + LN_EPS) * g + b

        def _gcn_conv(h, row, col, ew, dis, W, b):
            xw = h @ W
            norm = dis[row] * ew * dis[col]
            msg = norm[:, None] * xw[row]
            agg = jax.ops.segment_sum(msg, col, num_segments=N)
            agg = agg + (dis * dis)[:, None] * xw
            return agg + b
        row, col = (edge_index[0], edge_index[1])
        h = _safe(x)
        ew = jnp.clip(jnp.abs(_safe(edge_weight.reshape(-1))), 1e-06, None)
        deg = jax.ops.segment_sum(ew, col, num_segments=N) + 1.0
        dis = jax.lax.rsqrt(deg)
        for W, b, g, be in ((W1, b1, ln_g1, ln_b1), (W2, b2, ln_g2, ln_b2)):
            h_res = h
            h = _gcn_conv(h, row, col, ew, dis, W, b)
            h = _safe(h)
            h = _safe(_layernorm(h, g, be))
            h = jax.nn.relu(h)
            h = _safe(h)
            h = _safe(h + h_res)
        return h

    def _L0_ffn_ref(x, Wr, br, W1, b1, g1, be1, m1, v1, W2, b2, g2, be2, m2, v2, Wo, bo):
        import jax, jax.numpy as jnp
        import numpy as np
        BN_EPS = 0.001

        def _bn(h, g, b, m, v):
            return g * (h - m) * jax.lax.rsqrt(v + BN_EPS) + b
        feat = jnp.mean(x, axis=0)
        w = jax.nn.softmax(feat @ Wr + br, axis=-1)
        h = jnp.einsum('bfd,edh->bfeh', x, W1) + b1
        h = jax.nn.relu(_bn(h, g1, be1, m1, v1))
        h = jnp.einsum('bfeh,ehk->bfek', h, W2) + b2
        h = jax.nn.relu(_bn(h, g2, be2, m2, v2))
        y = jnp.einsum('bfeh,ehd->bfed', h, Wo) + bo
        return jnp.einsum('bfed,fe->bfd', y, w)
    edge_index = jnp.stack([src, dst])
    x = x + _L0_gnn_ref(_layernorm(x, axis=-1), edge_index, edge_weight, L0_gnn_W1, L0_gnn_b1, L0_gnn_ln_g1, L0_gnn_ln_b1, L0_gnn_W2, L0_gnn_b2, L0_gnn_ln_g2, L0_gnn_ln_b2)
    x = x + _L0_ffn_ref(_layernorm(x, axis=-1)[None], L0_ffn_Wr, L0_ffn_br, L0_ffn_W1, L0_ffn_b1, L0_ffn_g1, L0_ffn_be1, L0_ffn_m1, L0_ffn_v1, L0_ffn_W2, L0_ffn_b2, L0_ffn_g2, L0_ffn_be2, L0_ffn_m2, L0_ffn_v2, L0_ffn_Wo, L0_ffn_bo)[0]
    return x

_drawn_inputs = setup_inputs


def setup_inputs(seed=0):
    import zlib

    import numpy as np

    out = dict(_drawn_inputs(seed))
    spreads = {'L0_gnn_ln_g1': (1.0, 0.2),
     'L0_gnn_ln_b1': (0.0, 0.1),
     'L0_gnn_ln_g2': (1.0, 0.2),
     'L0_gnn_ln_b2': (0.0, 0.1),
     'L0_ffn_br': (0.0, 0.567),
     'L0_ffn_b1': (0.0, 0.728),
     'L0_ffn_g1': (1.0, 0.6),
     'L0_ffn_be1': (0.0, 0.749),
     'L0_ffn_m1': (0.0, 0.729),
     'L0_ffn_v1': (1.0, 0.6),
     'L0_ffn_b2': (0.0, 0.516),
     'L0_ffn_g2': (1.0, 0.6),
     'L0_ffn_be2': (0.0, 0.536),
     'L0_ffn_m2': (0.0, 0.528),
     'L0_ffn_v2': (1.0, 0.6),
     'L0_ffn_bo': (0.0, 0.388)}
    factors = {}
    for name, (base, spread) in spreads.items():
        noise = np.random.default_rng([zlib.crc32(name.encode()), seed]).standard_normal(out[name].shape)
        drawn = base * np.exp(spread * noise) if base else spread * noise
        out[name] = jnp.asarray(drawn.astype(out[name].dtype))
    for name, factor in factors.items():
        out[name] = (out[name] * factor).astype(out[name].dtype)
    return out
```

```python
from contextlib import ExitStack

import concourse.bass as bass
from concourse import mybir

F32 = mybir.dt.float32
F32R = mybir.dt.float32r
BF16 = mybir.dt.bfloat16
I32 = mybir.dt.int32
U8 = mybir.dt.uint8
ALU = mybir.AluOpType
ACT = mybir.ActivationFunctionType
AX = mybir.AxisListType

FINITE_MAX = 3.4028234663852886e38
LN_EPS = 1e-5
BN_EPS = 1e-3
EDGE_MIN = 1e-6

N, D = 3125, 256
E = 50000
NE = 8
HALF = D // 128
CHUNK = 128
GROUP = 2
GROUPS = 7
MC = GROUP * GROUPS
PAIRS = 14
CHUNKS = PAIRS * 2 * MC
NG = CHUNKS // GROUP
WIN = 64
STRETCH = 448
TILE = 112
BT = 4
BLOCK = TILE * BT
BLOCKS = 7
NP = BLOCK * BLOCKS
TILES = NP // TILE
PASSES = NP // WIN
AGG = NP + STRETCH
NOWHERE = 8192.0
LROWS, LCH = CHUNKS // 4, 4
META = 8
LAST_ROWS = N - (TILES - 1) * TILE
LROW = LCH * CHUNK
REST = E - (LROWS - 1) * LROW
HALVES = 4 * NE
PIECES = 3 * NE // 2
SLOT_A, SLOT_B, SLOT_C, SLOT_D, SLOT_E, SLOT_F = 2, 3, 4, 5, 6, 7
ADVANCES = 3 * PASSES
CHAIN1, CHAIN2 = 12, 24


def build_program(nc, x, src, dst, edge_weight, gW, gb, gg, gbe, Wr, br, par1, par2, W1, W2, Wo, bo, out):
    ctx = ExitStack()
    with ctx:
        build_inside(ctx, nc, x, src, dst, edge_weight, gW, gb, gg, gbe, Wr, br, par1, par2,
                     W1, W2, Wo, bo, out)


def build_inside(ctx, nc, x, src, dst, edge_weight, gW, gb, gg, gbe, Wr, br, par1, par2,
                 W1, W2, Wo, bo, out):
    def sb(name, shape, dt=F32):
        return ctx.enter_context(nc.sbuf_tensor(name, shape, dt))

    def pb(name, shape, dt=F32):
        return ctx.enter_context(nc.psum_tensor(name, shape, dt))

    def sem(name):
        return ctx.enter_context(nc.semaphore(name))

    ds = bass.ds

    table = [nc.dram_tensor(f"table{n}", [NP, D], F32, kind="Internal").ap() for n in range(2)]
    resid = [nc.dram_tensor(f"resid{n}", [NP, D], F32, kind="Internal").ap() for n in range(2)]

    w_hi = [sb(f"w_hi{n}", [128, NE, HALF, D], F32R) for n in range(3)]
    w_lo = [sb(f"w_lo{n}", [128, NE, HALF, D], F32R) for n in range(3)]
    ring = sb("ring", [128, MC, D])
    onehot = sb("onehot", [128, 2, MC, WIN])
    onehot_b = onehot[:, :, :, :].bitcast(BF16)[:, :, :, 0:WIN]
    aggT = sb("aggT", [128, HALF, AGG])
    srcs = sb("srcs", [128, CHUNKS], I32)
    rel = sb("rel", [128, CHUNKS])
    ew = sb("ew", [128, CHUNKS])
    hnT_hi = [sb(f"hnT_hi{n}", [128, HALF, BLOCK], F32R) for n in range(2)]
    hnT_lo = [sb(f"hnT_lo{n}", [128, HALF, BLOCK], F32R) for n in range(2)]
    hid_hi = [sb(f"hid_hi{n}", [128, HALF, BLOCK], F32R) for n in range(2)]
    hid_lo = [sb(f"hid_lo{n}", [128, HALF, BLOCK], F32R) for n in range(2)]
    hid = sb("hid", [128, HALF, BLOCK])
    acc = [sb(f"acc{n}", [128, BT, D]) for n in range(2)]
    g_blk = sb("g_blk", [128, BT, D])
    h_res = sb("h_res", [128, BT, D])
    hc = sb("hc", [128, BT, D])
    aggst = sb("aggst", [128, HALF, BLOCK])
    bad = sb("bad", [TILE, BT * D], U8)
    gW_sb = sb("gW_sb", [128, HALF, D])
    gvec = sb("gvec", [TILE, 3, D])
    bo_meta = sb("bo_meta", [33, D])
    bo_sb = bo_meta[0:NE, :]
    meta = bo_meta[32:33, 0:2 * PAIRS * META].bitcast(I32)
    ident = sb("ident", [128, 128])
    iota = sb("iota", [128, WIN])
    zeros_b = sb("zeros_b", [128, STRETCH], BF16)
    zero1 = sb("zero1", [128, 1])
    ones1 = sb("ones1", [128, 1])
    br_bc = sb("br_bc", [TILE, NE])
    hid_s = sb("hid_s", [128, 2, NE * HALF])
    hid_b = sb("hid_b", [128, 2, NE * HALF])
    dis = sb("dis", [TILE, TILES])
    stats = sb("stats", [TILE, BT, 6])
    mv = sb("mv", [TILE, TILES, 2])
    rstd = sb("rstd", [TILE, TILES])
    nmr = sb("nmr", [TILE, TILES])
    logit = sb("logit", [TILE, BT, NE])
    lmax = sb("lmax", [TILE, BT])
    lsum = sb("lsum", [TILE, BT])
    gate = [sb(f"gate{n}", [TILE, BT, NE]) for n in range(2)]
    wr_f = sb("wr_f", [128, HALF, NE])
    wr_hi = sb("wr_hi", [128, HALF, NE], F32R)
    wr_lo = sb("wr_lo", [128, HALF, NE], F32R)
    small = sb("small", [128, 2 * PAIRS])
    place = sb("place", [128, 2 * PAIRS])
    bmv = sb("bmv", [TILE, BT, 2])
    newton = sb("newton", [TILE, TILES])
    eps = sb("eps", [128, 2])
    brstd = sb("brstd", [TILE, BT])
    bnmr = sb("bnmr", [TILE, BT])
    odd = sb("odd", [TILE, TILES], U8)
    ctrl = sb("ctrl", [1, 4], I32)
    idx_st = sb("idx_st", [128, 2, MC], I32)

    ew_st = sb("ew_st", [128, 2, MC, 3], BF16)
    scal = sb("scal", [128, 8])
    gext = sb("gext", [LROWS, 2, GROUP])

    gateT = aggst[0:NE, 0, :]

    def flat(t):
        return t[:, :, :].rearrange("p a b -> p (a b)")

    x_all = flat(aggT)[0:TILE, :].rearrange("p (t d) -> p t d", d=D)
    degrow = flat(ring)[0:3, :]
    ew3 = flat(hid).bitcast(BF16)[:, 0:3 * CHUNKS].rearrange("p (c k) -> p c k", k=3)
    iota_i = flat(hid)[:, 3 * CHUNKS // 2:3 * CHUNKS // 2 + WIN].bitcast(I32)
    par_T = flat(hid)[:, 704:704 + 10 * NE * HALF].rearrange("p (l i c) -> p l i c", l=2, i=5)
    ldst, lsrc, lew = (flat(t)[0:LROWS, :] for t in (hc, g_blk, h_res))
    diag = flat(acc[0])[0:LROWS, 0:4 * LROWS]
    ones_m = flat(acc[0])[0:LROWS, 512:640]
    room = flat(acc[1])
    pair_i = flat(aggst)[:, 0:NG].bitcast(I32)
    par_st = flat(aggst)[0:5 * NE * HALF, 512:768].rearrange("p (l n) -> p l n", l=2)
    stage = [acc[n][:, :, :].rearrange("p (e k) n -> p e k n", k=HALF) for n in range(2)]

    psA = pb("psA", [128, 2, 512])
    psN = pb("psN", [128, 2, 512])
    psH = pb("psH", [128, 2, 512])
    psY = pb("psY", [128, 2, 512])

    s_pad = sem("s_pad")
    s_pool = sem("s_pool")
    s_wr_hi = sem("s_wr_hi")
    s_wr_lo = sem("s_wr_lo")
    s_acc_pad = sem("s_acc_pad")
    s_x_last = sem("s_x_last")
    s_degrow = sem("s_degrow")
    s_carried = sem("s_carried")
    s_moved = sem("s_moved")
    s_dst_in = sem("s_dst_in")
    s_src_in = sem("s_src_in")
    s_ew_in = sem("s_ew_in")
    s_x_in = [sem(f"s_x_in{b}") for b in range(BLOCKS)]
    s_const_in = sem("s_const_in")
    s_par_in = sem("s_par_in")
    s_pre = sem("s_pre")
    s_prep = sem("s_prep")
    s_prep_pe = sem("s_prep_pe")
    s_meta = sem("s_meta")
    s_srcs = sem("s_srcs")
    s_var_x = sem("s_var_x")
    s_sqrt_x = sem("s_sqrt_x")
    s_var_par = sem("s_var_par")
    s_sqrt_par = sem("s_sqrt_par")
    s_sqrt_deg = sem("s_sqrt_deg")
    s_var = sem("s_var")
    s_sqrt = sem("s_sqrt")
    s_stat_x = sem("s_stat_x")
    s_h0 = sem("s_h0")
    s_h0_out = [sem(f"s_h0_out{b}") for b in range(BLOCKS)]
    s_dis = sem("s_dis")
    s_g1 = sem("s_g1")
    s_g1_out = sem("s_g1_out")
    s_deg_oh = sem("s_deg_oh")
    s_deg_mm = sem("s_deg_mm")
    s_deg_free = sem("s_deg_free")
    s_degT = sem("s_degT")
    s_wst_in = [sem(f"s_wst_in{n}") for n in range(2)]
    s_w_hi = sem("s_w_hi")
    s_w_lo = sem("s_w_lo")
    s_par = sem("s_par")
    s_cleared = sem("s_cleared")
    s_gath = [sem(f"s_gath{s}") for s in range(MC)]
    s_used = sem("s_used")
    s_oh = sem("s_oh")
    s_agg_free = sem("s_agg_free")
    s_idx = sem("s_idx")
    s_ohc = sem("s_ohc")
    s_adv = sem("s_adv")
    s_g_in = sem("s_g_in")
    s_hres_in = sem("s_hres_in")
    s_x_blk = [sem(f"s_x_blk{n}") for n in range(2)]
    s_gvec_in = sem("s_gvec_in")
    s_gT = sem("s_gT")
    s_aggst = sem("s_aggst")
    s_conv = sem("s_conv")
    s_conv_ev = sem("s_conv_ev")
    s_stat = sem("s_stat")
    s_norm = sem("s_norm")
    s_h = sem("s_h")
    s_g2 = sem("s_g2")
    s_h_out = sem("s_h_out")
    s_g2_out = sem("s_g2_out")
    s_ch1 = sem("s_ch1")
    s_ch2 = sem("s_ch2")
    s_stat2 = sem("s_stat2")
    s_hn = sem("s_hn")
    s_hnT = sem("s_hnT")
    s_hnT_hi = sem("s_hnT_hi")
    s_hnT_lo = sem("s_hnT_lo")
    s_logit = sem("s_logit")
    s_lsub = sem("s_lsub")
    s_exp = sem("s_exp")
    s_gate = sem("s_gate")
    s_gateT = sem("s_gateT")
    s_gateT_sb = sem("s_gateT_sb")
    s_gbo = sem("s_gbo")
    s_acc0 = sem("s_acc0")
    s_hid = sem("s_hid")
    s_hid_free = sem("s_hid_free")
    s_hid_hi = sem("s_hid_hi")
    s_hid_lo = sem("s_hid_lo")
    s_y = sem("s_y")
    s_y_free = sem("s_y_free")
    s_out = [sem(f"s_out{n}") for n in range(2)]

    def within(value, low, high):
        return value if isinstance(value, int) else value.with_bounds(min_val=low, max_val=high)

    def carry(eng):
        eng.sem_inc(s_carried, 1)

    def control(eng):
        eng.wait_ge(s_meta, 1)
        extra = eng.value_load(ctrl[0:1, 0:1], min_val=0, max_val=PASSES - 1)
        lead = eng.value_load(ctrl[0:1, 1:2], min_val=3, max_val=PAIRS)
        return extra, lead

    def extra_passes(eng, extra, base, pair, after=None):
        with eng.If(extra > 0):
            with eng.Fori(0, PASSES - 1) as p:
                with eng.Fori(0, PAIRS) as i:
                    pair(base + p * PAIRS + i, PAIRS - 1 - i)
                if after is not None:
                    after(p)

    block = ctx.enter_context(nc.Block())

    @block.sync
    def _(sp):
        sp.wait_ge(s_pad, 3)
        for tile, array, s_in in ((ldst, dst, s_dst_in), (lew, edge_weight, s_ew_in), (lsrc, src, s_src_in)):
            t = tile[:, 0:LROW] if array is edge_weight else tile[:, 0:LROW].bitcast(I32)
            sp.dma_start(t[0:96, :], array[0:96 * LROW].rearrange("(p n) -> p n", n=LROW)).then_inc(s_in, 16)
            sp.dma_start(t[96:97, :], array[96 * LROW:97 * LROW].rearrange("(p n) -> p n", n=LROW)).then_inc(s_in, 16)
            sp.dma_start(t[97:98, 0:REST], array[97 * LROW:E].rearrange("(p n) -> p n", p=1)).then_inc(s_in, 16)
        for b in range(BLOCKS):
            full = BT if b < BLOCKS - 1 else BT - 1
            sp.dma_start(x_all[:, b * BT:b * BT + full, :],
                         x[b * BLOCK:b * BLOCK + full * TILE, :].rearrange("(t p) d -> p t d", p=TILE)
                         ).then_inc(s_x_in[b], 16)
        sp.wait_ge(s_pad, 4)
        sp.dma_start(x_all[0:LAST_ROWS, TILES - 1, :], x[N - LAST_ROWS:N, :]).then_inc(s_x_in[BLOCKS - 1], 16)
        for l, arrays in enumerate((par1, par2)):
            for i, a in enumerate(arrays):
                rows16 = NE * HALF
                sp.dma_start(par_st[i * rows16:(i + 1) * rows16, l, :], a.rearrange("e (m p) -> (e m) p", p=128)).then_inc(s_par_in, 16)
        sp.dma_start(bo_sb[:, :], bo).then_inc(s_const_in, 16)
        sp.dma_start(br_bc[:, :], br.unsqueeze(0).broadcast_to([TILE, NE])).then_inc(s_const_in, 16)
        sp.dma_start(wr_f[:, :, :], Wr.rearrange("(k p) e -> p k e", p=128)).then_inc(s_const_in, 16)

        def rows(t, b):
            return t[ds(within(b * BLOCK, 0, t.shape[0] - BLOCK), BLOCK), :].rearrange("(t p) d -> p t d", p=TILE)

        def static_rows(t, b):
            return t[b * BLOCK:(b + 1) * BLOCK, :].rearrange("(t p) d -> p t d", p=TILE)

        def layer_consts(layer):
            sp.dma_start(gW_sb[:, :, :], gW[layer].rearrange("(k p) n -> p k n", p=128)).then_inc(s_gvec_in, 16)
            for i, v in enumerate((gb[layer], gg[layer], gbe[layer])):
                sp.dma_start(gvec[:, i, :], v.unsqueeze(0).broadcast_to([TILE, D])).then_inc(s_gvec_in, 16)

        layer_consts(0)
        sp.wait_ge(s_meta, 1)
        for piece in range(PIECES):
            w, e, u = (W1, W2, Wo)[piece // 4], 2 * (piece % 4), piece % 2
            if piece >= 2:
                sp.wait_ge(s_w_lo, piece - 1)
            for i in range(2):
                sp.dma_start(stage[u][:, i, :, :], w[e + i].rearrange("(k p) n -> p k n", p=128)).then_inc(s_wst_in[u], 16)
        for b in range(BLOCKS):
            sp.wait_ge(s_h0, BT * (b + 1))
            sp.dma_start(static_rows(resid[0], b), x_all[:, b * BT:(b + 1) * BT, :]).then_inc(s_h0_out[b], 16)
        for b in range(BLOCKS):
            sp.wait_ge(s_g1, BT * (b + 1))
            sp.dma_start(static_rows(table[0], b), x_all[:, b * BT:(b + 1) * BT, :]).then_inc(s_g1_out, 16)

        def load_table_block(layer, j):
            sp.dma_start(g_blk[0:TILE, :, :], rows(table[layer], BLOCKS - 1 - j)).then_inc(s_g_in, 16)

        def load_resid_block(layer, j):
            sp.dma_start(h_res[0:TILE, :, :], rows(resid[layer], BLOCKS - 1 - j)).then_inc(s_hres_in, 16)

        def store_layer1(j):
            b = BLOCKS - 1 - j
            sp.wait_ge(s_h, j + 1)
            carry(sp)
            sp.dma_start(rows(resid[1], b), hc[0:TILE, :, :]).then_inc(s_h_out, 16)
            sp.wait_ge(s_g2, BT * (j + 1))
            carry(sp)
            sp.dma_start(rows(table[1], b), h_res[0:TILE, :, :]).then_inc(s_g2_out, 16)

        def store_out(k, par, last_piece=True):
            first = (BLOCKS - 1 - k) * BLOCK
            sp.dma_start(out[ds(first, (BT - 1) * TILE), :].rearrange("(t p) d -> p t d", p=TILE),
                         acc[par][0:TILE, 0:BT - 1, :]).then_inc(s_out[par], 16)
            sp.dma_start(out[ds(first + (BT - 1) * TILE, LAST_ROWS), :],
                         acc[par][0:LAST_ROWS, BT - 1, :]).then_inc(s_out[par], 16)
            if last_piece:
                sp.dma_start(out[ds(first + (BT - 1) * TILE + LAST_ROWS, TILE - LAST_ROWS), :],
                             acc[par][LAST_ROWS:TILE, BT - 1, :]).then_inc(s_out[par], 16)

        sp.wait_ge(s_g1_out, 16 * BLOCKS)
        for b in range(BLOCKS):
            sp.wait_ge(s_h0_out[b], 16)
        sp.wait_ge(s_srcs, 1)
        load_table_block(0, 0)
        load_resid_block(0, 0)
        store_layer1(0)
        with sp.Fori(1, BLOCKS) as j:
            sp.wait_ge(s_gT, j)
            carry(sp)
            load_table_block(0, j)
            sp.wait_ge(s_g2_out, 16 * j)
            carry(sp)
            load_resid_block(0, j)
            store_layer1(j)
        sp.wait_ge(s_g2_out, 16 * BLOCKS)
        sp.wait_ge(s_h_out, 16 * BLOCKS)
        layer_consts(1)
        load_table_block(1, 0)
        load_resid_block(1, 0)
        tail = (BLOCKS - 1) * BLOCK
        sp.dma_start(acc[0][0:TILE, 0:BT - 1, :],
                     x[tail:tail + (BT - 1) * TILE, :].rearrange("(t p) d -> p t d", p=TILE)).then_inc(s_x_blk[0], 16)
        sp.dma_start(acc[0][0:LAST_ROWS, BT - 1, :], x[N - LAST_ROWS:N, :]).then_inc(s_x_last, 16)
        sp.wait_ge(s_gT, BLOCKS + 1)
        load_table_block(1, 1)
        sp.wait_ge(s_acc0, 1)
        load_resid_block(1, 1)
        sp.dma_start(acc[1][0:TILE, :, :], rows(x, BLOCKS - 2)).then_inc(s_x_blk[1], 16)
        with sp.Fori(0, (BLOCKS - 1) // 2) as kk:
            for par in range(2):
                k = 2 * kk + par
                with sp.If(k + 2 < BLOCKS):
                    sp.wait_ge(s_gT, BLOCKS + k + 2)
                    carry(sp)
                    load_table_block(1, k + 2)
                    sp.wait_ge(s_acc0, k + 2)
                    carry(sp)
                    load_resid_block(1, k + 2)
                sp.wait_ge(s_y_free, 2 * NE * (k + 1) + 2)
                carry(sp)
                if par == 0:
                    store_out(k, 0, last_piece=False)
                    with sp.If(kk > 0):
                        first = within((BLOCKS - 1 - k) * BLOCK, 0, (BLOCKS - 3) * BLOCK)
                        sp.dma_start(out[ds(first + (BT - 1) * TILE + LAST_ROWS, TILE - LAST_ROWS), :],
                                     acc[0][LAST_ROWS:TILE, BT - 1, :]).then_inc(s_out[0], 16)
                    with sp.Else():
                        sp.dma_start(resid[0][0:TILE - LAST_ROWS, :],
                                     acc[0][LAST_ROWS:TILE, BT - 1, :]).then_inc(s_out[0], 16)
                else:
                    store_out(k, 1)
                sp.wait_ge(s_out[par], 48 * (kk + 1))
                carry(sp)
                with sp.If(k + 2 < BLOCKS):
                    sp.dma_start(acc[par][0:TILE, :, :], rows(x, BLOCKS - 3 - k)).then_inc(s_x_blk[par], 16)
                sp.nop()
        sp.wait_ge(s_y_free, 2 * NE * BLOCKS + 2)
        store_out(BLOCKS - 1, 0)
        sp.wait_ge(s_out[0], 48 * 4)
        sp.wait_ge(s_out[1], 48 * 3)

    @block.gpsimd
    def _(pool):
        nc.gpsimd.memset(ldst[:, 0:LROW].bitcast(I32), int(NOWHERE)).then_inc(s_pad, 1)
        nc.gpsimd.memset(lew[:, 0:LROW], 0.0).then_inc(s_pad, 1)
        nc.gpsimd.memset(lsrc[:, 0:LROW].bitcast(I32), 0).then_inc(s_pad, 1)
        nc.gpsimd.memset(x_all[:, TILES - 1, :], 0.0).then_inc(s_pad, 1)
        nc.gpsimd.memset(ident[:, :], 0.0).then_inc(s_pool, 1)
        nc.gpsimd.memset(zeros_b[:, :], 0.0).then_inc(s_pool, 1)
        nc.gpsimd.memset(ones_m[:, :], 1.0).then_inc(s_pool, 1)
        nc.gpsimd.memset(ones1[:, :], 1.0).then_inc(s_pool, 1)
        nc.gpsimd.memset(zero1[:, :], 0.0).then_inc(s_pool, 1)
        nc.gpsimd.iota(iota_i[:, :], [[1, WIN]], base=0, channel_multiplier=0).then_inc(s_pool, 1)
        nc.gpsimd.iota(pair_i, [[1, PAIRS], [0, NG // PAIRS]], base=0, channel_multiplier=0).then_inc(s_pool, 1)
        nc.gpsimd.memset(eps[:, 0:1], LN_EPS).then_inc(s_pool, 1)
        nc.gpsimd.memset(eps[:, 1:2], BN_EPS).then_inc(s_pool, 1)
        pool.wait_ge(s_pool, 9)
        nc.gpsimd.affine_select(out=ident[:, :], in_=ident[:, :], compare_op=ALU.not_equal, fill=1.0, base=0,
                                pattern=[[-1, 128]], channel_multiplier=1).then_inc(s_pool, 1)
        for piece in range(PIECES):
            t, e, u = piece // 4, 2 * (piece % 4), piece % 2
            pool.wait_ge(s_w_hi, piece + 1)
            nc.gpsimd.tensor_tensor(w_lo[t][:, e:e + 2, :, :], stage[u], w_hi[t][:, e:e + 2, :, :].bitcast(F32),
                                    ALU.subtract).then_inc(s_w_lo, 1)
        pool.wait_ge(s_wr_hi, 1)
        nc.gpsimd.tensor_tensor(wr_lo[:, :, :], wr_f[:, :, :], wr_hi[:, :, :].bitcast(F32), ALU.subtract).then_inc(s_wr_lo, 1)
        pool.wait_ge(s_w_lo, PIECES)
        nc.gpsimd.memset(acc[0][0:TILE, BT - 1, :], 0.0).then_inc(s_acc_pad, 1)

        extra, _ = control(pool)
        pool.wait_ge(s_srcs, 1)

        def gathers(layer, g, pb):
            for h in range(2):
                m = 2 * g + h
                nc.gpsimd.tensor_copy(idx_st[:, h, :], srcs[:, ds(pb * (2 * MC) + h * MC, MC)]).then_inc(s_idx, 1)
                pool.wait_ge(s_idx, m + 1)
                for s in range(MC):
                    if s % GROUP == 0:
                        pool.wait_ge(s_used, m * GROUPS + s // GROUP + 1)
                        carry(pool)
                    nc.gpsimd.indirect_dma_start(
                        ring[:, s, :], None, table[layer],
                        bass.IndirectOffsetOnAxis(ap=idx_st[:, h, s:s + 1], axis=0)).then_inc(s_gath[s], 16)

        pool.wait_ge(s_g1_out, 16 * BLOCKS)
        pool.wait_ge(s_degT, 1)
        extra_passes(pool, extra, 0, lambda g, pb: gathers(0, g, pb))
        with pool.Fori(0, PAIRS) as i:
            gathers(0, extra * PAIRS + i, PAIRS - 1 - i)
        pool.wait_ge(s_g2_out, 16 * BLOCKS)
        extra_passes(pool, extra, extra * PAIRS + PAIRS, lambda g, pb: gathers(1, g, pb))
        with pool.Fori(0, PAIRS) as i:
            gathers(1, extra * (2 * PAIRS) + PAIRS + i, PAIRS - 1 - i)

    @block.scalar
    def _(act):
        act.sem_inc(s_hid_free, 2)

        def split_piece(piece):
            t, e, u = piece // 4, 2 * (piece % 4), piece % 2
            act.wait_ge(s_wst_in[u], 32 * (piece // 2 + 1))
            nc.scalar.activation(w_hi[t][:, e:e + 2, :, :], stage[u], ACT.Copy).then_inc(s_w_hi, 1)

        act.wait_ge(s_const_in, 48)
        nc.scalar.activation(wr_hi[:, :, :], wr_f[:, :, :], ACT.Copy).then_inc(s_wr_hi, 1)
        for piece in range(PIECES // 2):
            split_piece(piece)
        act.wait_ge(s_pool, 10)
        act.wait_ge(s_var_x, 1)
        nc.scalar.activation(rstd[:, :], mv[:, :, 1], ACT.Sqrt, bias=eps[0:TILE, 0:1]).then_inc(s_sqrt_x, 1)
        act.wait_ge(s_stat_x, 1)
        for t in range(TILES):
            nc.scalar.activation(x_all[:, t, :], x_all[:, t, :], ACT.Identity,
                                 bias=nmr[:, t:t + 1], scale=rstd[:, t:t + 1]).then_inc(s_h0, 1)
        for piece in range(PIECES // 2, PIECES):
            split_piece(piece)
        act.wait_ge(s_var_par, 1)
        nc.scalar.activation(hid_s[:, :, :], par_T[:, :, 4, :], ACT.Sqrt, bias=eps[:, 1:2]).then_inc(s_sqrt_par, 1)
        act.wait_ge(s_degT, 1)
        nc.scalar.activation(dis[:, :], psN[0:TILE, 1, 0:TILES], ACT.Sqrt, bias=ones1[0:TILE, :]).then_inc(s_sqrt_deg, 1)
        act.wait_ge(s_dis, 1)
        for b in range(BLOCKS):
            act.wait_ge(s_h0_out[b], 16)
            for t in range(b * BT, (b + 1) * BT):
                nc.scalar.activation(x_all[:, t, :], x_all[:, t, :], ACT.Copy, scale=dis[:, t:t + 1]).then_inc(s_g1, 1)

        def root(nth):
            act.wait_ge(s_var, nth)
            nc.scalar.activation(brstd[:, :], bmv[:, :, 1], ACT.Sqrt, bias=eps[0:TILE, 0:1]).then_inc(s_sqrt, 1)

        def norm(layer, j):
            root(j + 1 if layer == 0 else BLOCKS + 2 * j + 1)
            act.wait_ge(s_stat, layer * BLOCKS + j + 1)
            for t in range(BT):
                nc.scalar.activation(hc[0:TILE, t, :], hc[0:TILE, t, :], ACT.Identity,
                                     bias=bnmr[:, t:t + 1], scale=brstd[:, t:t + 1]).then_inc(s_norm, 1)

        def second_table(j):
            act.wait_ge(s_h, j + 1)
            for t in range(BT):
                nc.scalar.activation(h_res[0:TILE, t, :], hc[0:TILE, t, :], ACT.Copy,
                                     scale=dis[:, ds((BLOCKS - 1 - j) * BT + t, 1)]).then_inc(s_g2, 1)

        def norm_x1(j, par):
            root(BLOCKS + 2 * j + 2)
            act.wait_ge(s_stat2, j + 1)
            for t in range(BT):
                nc.scalar.activation(hc[0:TILE, t, :], acc[par][0:TILE, t, :], ACT.Identity,
                                     bias=bnmr[:, t:t + 1], scale=brstd[:, t:t + 1]).then_inc(s_hn, 1)

        def hnT_high(j, par):
            act.wait_ge(s_hnT, j + 1)
            nc.scalar.activation(hnT_hi[par][:, :, :], psN[:, :, 0:BLOCK], ACT.Copy).then_inc(s_hnT_hi, 1)

        def exponentials(j):
            act.wait_ge(s_lsub, j + 1)
            nc.scalar.activation(logit[:, :, :], logit[:, :, :], ACT.Exp).then_inc(s_exp, 1)

        def gates_T(j):
            act.wait_ge(s_gateT, j + 1)
            nc.scalar.activation(gateT[:, :], psN[0:NE, 1, 0:BLOCK], ACT.Copy).then_inc(s_gateT_sb, 1)

        def hidden_half(k, idx, l, e, m):
            n = k * HALVES + idx
            act.wait_ge(s_hid, n + 1)
            act.wait_ge(s_hid_lo, n + 1)
            col = e * HALF + m
            nc.scalar.activation(hid[:, m, :], psH[:, m, 0:BLOCK], ACT.Relu, bias=hid_b[:, l, col:col + 1],
                                 scale=hid_s[:, l, col:col + 1]).then_inc(s_hid_free, 1)
            act.wait_ge(s_hid_free, n + 3)
            nc.scalar.activation(hid_hi[l][:, m, :], hid[:, m, :], ACT.Copy).then_inc(s_hid_hi, 1)

        def expert(k, e):
            for m in range(HALF):
                hidden_half(k, 4 * e + 2 + m, 1, e, m)
            if e + 1 < NE:
                for m in range(HALF):
                    hidden_half(k, 4 * (e + 1) + m, 0, e + 1, m)

        norm(0, 0)
        second_table(0)
        with act.Fori(1, BLOCKS) as j:
            norm(0, j)
            second_table(j)
        norm(1, 0)
        norm_x1(0, 0)
        hnT_high(0, 0)
        exponentials(0)
        gates_T(0)

        def experts(k, par, node):
            act.wait_ge(s_par, 1)
            for m in range(HALF):
                hidden_half(k, m, 0, 0, m)
            for e in range(NE):
                if node and e == SLOT_D:
                    norm_x1(k + 1, 1 - par)
                if node and e == SLOT_C:
                    norm(1, k + 1)
                if node and e == SLOT_F:
                    exponentials(k + 1)
                expert(k, e)
                if node and e == SLOT_D:
                    hnT_high(k + 1, 1 - par)
                if node and e == SLOT_F:
                    gates_T(k + 1)

        with act.Fori(0, (BLOCKS - 1) // 2) as kk:
            for par in range(2):
                experts(2 * kk + par, par, True)
        experts(BLOCKS - 1, 0, False)

    @block.tensor
    def _(pe):
        pe.sem_inc(s_used, GROUPS)
        pe.wait_ge(s_pool, 10)
        pe.wait_ge(s_prep, 1)
        for c in range(LCH):
            nc.tensor.transpose(psH[:, 0, c * LROWS:(c + 1) * LROWS], ldst[:, LROW + c * CHUNK:LROW + (c + 1) * CHUNK],
                                ident[0:LROWS, 0:LROWS]).then_inc(s_prep_pe, 1)
        pe.wait_ge(s_prep, 2)
        nc.tensor.matmul(psN[:, 0, 0:4 * LROWS], ones_m, diag, start=True, stop=True).then_inc(s_prep_pe, 1)
        pe.wait_ge(s_prep, 3)
        for c in range(LCH):
            nc.tensor.transpose(psY[:, 0, c * LROWS:(c + 1) * LROWS], lew[:, LROW + c * CHUNK:LROW + (c + 1) * CHUNK],
                                ident[0:LROWS, 0:LROWS]).then_inc(s_prep_pe, 1)
        pe.wait_ge(s_prep, 4)
        for c in range(LCH):
            nc.tensor.transpose(psH[:, 1, c * LROWS:(c + 1) * LROWS], lsrc[:, LROW + c * CHUNK:LROW + (c + 1) * CHUNK],
                                ident[0:LROWS, 0:LROWS]).then_inc(s_prep_pe, 1)
        pe.wait_ge(s_par_in, 16 * 10)
        rows80 = 5 * NE * HALF
        for l in range(2):
            nc.tensor.transpose(psY[:, 1, l * rows80:(l + 1) * rows80], par_st[:, l, :],
                                ident[0:rows80, 0:rows80]).then_inc(s_prep_pe, 1)

        extra, lead = control(pe)

        places = []

        def window_regs(pb, h):
            places.append(None)
            regs = [pe.alloc_register(f"win{len(places)}_{n}") for n in range(GROUPS)]
            pe.load(regs, meta[0:1, ds(pb * (2 * META) + h * META, GROUPS)])
            return regs, [pe.snap(r, min_val=0, max_val=STRETCH - WIN) for r in regs]

        def degree_pair(g, pb):
            for h in range(2):
                m = 2 * g + h
                pe.wait_ge(s_deg_free, m + 1)
                nc.tensor.matmul(psA[0:3, 0, 0:STRETCH], zeros_b[:, 0:3], zeros_b[:, :], start=True, stop=True)
                regs, offs = window_regs(pb, h)
                pe.wait_ge(s_deg_oh, 2 * (m + 1))
                for s in range(MC):
                    last = nc.tensor.matmul(psA[0:3, 0, ds(offs[s // GROUP], WIN)], ew_st[:, h, s, :],
                                            onehot_b[:, h, s, :], start=False, stop=True, skip_group_check=True)
                last.then_inc(s_deg_mm, 1)
                for r in regs:
                    pe.free_register(r)

        extra_passes(pe, extra, 0, degree_pair)
        with pe.Fori(0, PAIRS) as i:
            degree_pair(extra * PAIRS + i, PAIRS - 1 - i)
        pe.wait_ge(s_degrow, 1)
        for t in range(TILES):
            last = nc.tensor.matmul(psN[0:TILE, 1, t:t + 1], degrow[:, t * TILE:(t + 1) * TILE], ones1[0:3, :],
                                    start=True, stop=True)
        last.then_inc(s_degT, 1)

        def macro(g, pb, h):
            m = 2 * g + h
            pe.wait_ge(s_agg_free, m + 1)
            for f in range(HALF):
                nc.tensor.matmul(psA[:, f, 0:STRETCH], zeros_b[:, 0:128], zeros_b[:, :], start=True, stop=True)
            regs, offs = window_regs(pb, h)
            pe.wait_ge(s_oh, m + 1)
            for s in range(MC):
                pe.wait_ge(s_gath[s], (m + 1) * 16)
                for f in range(HALF):
                    last = nc.tensor.matmul(psA[:, f, ds(offs[s // GROUP], WIN)], ring[:, s, f * 128:(f + 1) * 128],
                                            onehot[:, h, s, :], start=False, stop=True, skip_group_check=True)
                if s % GROUP == GROUP - 1:
                    last.then_inc(s_used, 1)
            for r in regs:
                pe.free_register(r)

        def pair(g, pb):
            macro(g, pb, 0)
            macro(g, pb, 1)

        def node_A(layer, j, first=False):
            n = layer * BLOCKS + j
            pe.wait_ge(s_g_in, (n + 1) * 16)
            if layer == 0:
                if not first:
                    pe.wait_ge(s_conv_ev, n)
            elif first:
                pe.wait_ge(s_conv_ev, n)
            else:
                pe.wait_ge(s_acc0, j)
            for f in range(HALF):
                for t in range(BT):
                    last = nc.tensor.transpose(psN[:, f, t * TILE:(t + 1) * TILE],
                                               g_blk[0:TILE, t, f * 128:(f + 1) * 128], ident[0:TILE, 0:TILE])
            last.then_inc(s_gT, 1)

        def node_B(layer, j):
            pe.wait_ge(s_gvec_in, 64 * (layer + 1))
            pe.wait_ge(s_aggst, layer * BLOCKS + j + 1)
            for t in range(BT):
                for f in range(HALF):
                    last = nc.tensor.matmul(psN[0:TILE, t // 2, (t % 2) * D:(t % 2 + 1) * D],
                                            aggst[:, f, t * TILE:(t + 1) * TILE], gW_sb[:, f, :],
                                            start=(f == 0), stop=(f == HALF - 1))
            last.then_inc(s_conv, 1)

        def node_D(j):
            pe.wait_ge(s_hn, (j + 1) * BT)
            for f in range(HALF):
                for t in range(BT):
                    last = nc.tensor.transpose(psN[:, f, t * TILE:(t + 1) * TILE],
                                               hc[0:TILE, t, f * 128:(f + 1) * 128], ident[0:TILE, 0:TILE])
            last.then_inc(s_hnT, 1)

        def three(ps, hi, lo, whi, wlo, weights_stationary, start, stop):
            for i, (a, w) in enumerate(((hi, whi), (hi, wlo), (lo, whi))):
                lhsT, rhs = (w, a) if weights_stationary else (a, w)
                last = nc.tensor.matmul(ps, lhsT, rhs, start=start and i == 0, stop=stop and i == 2)
            return last

        def node_E(j, par):
            pe.wait_ge(s_hnT_lo, j + 1)
            for t in range(BT):
                ts = slice(t * TILE, (t + 1) * TILE)
                for f in range(HALF):
                    last = three(psN[0:TILE, 0, t * NE:(t + 1) * NE], hnT_hi[par][:, f, ts], hnT_lo[par][:, f, ts],
                                 wr_hi[:, f, :], wr_lo[:, f, :], False, f == 0, f == HALF - 1)
            last.then_inc(s_logit, 1)

        def node_F(j, par):
            pe.wait_ge(s_gate, j + 1)
            for t in range(BT):
                last = nc.tensor.transpose(psN[0:NE, 1, t * TILE:(t + 1) * TILE], gate[par][:, t, :], ident[0:TILE, 0:TILE])
            last.then_inc(s_gateT, 1)
            pe.wait_ge(s_gateT_sb, j + 1)
            for t in range(BT):
                last = nc.tensor.matmul(psN[0:TILE, t // 2, (t % 2) * D:(t % 2 + 1) * D],
                                        gateT[:, t * TILE:(t + 1) * TILE], bo_sb[:, :], start=True, stop=True)
            last.then_inc(s_gbo, 1)

        def hidden(k, idx, l, e, m):
            n = k * HALVES + idx
            pe.wait_ge(s_hid_free, n + 1)
            src_hi, src_lo = (hnT_hi[k_par[0]], hnT_lo[k_par[0]]) if l == 0 else (hid_hi[0], hid_lo[0])
            ms = slice(m * 128, (m + 1) * 128)
            for f in range(HALF):
                last = three(psH[:, m, 0:BLOCK], src_hi[:, f, :], src_lo[:, f, :], w_hi[l][:, e, f, ms],
                             w_lo[l][:, e, f, ms], True, f == 0, f == HALF - 1)
            last.then_inc(s_hid, 1)

        k_par = [0]

        def experts_start(k, par):
            k_par[0] = par
            pe.wait_ge(s_hnT_lo, k + 1)
            for m in range(HALF):
                hidden(k, m, 0, 0, m)

        def expert(k, e):
            pe.wait_ge(s_hid_lo, k * HALVES + 4 * e + 2 + 2)
            for m in range(HALF):
                hidden(k, 4 * e + 2 + m, 1, e, m)
            if e + 1 < NE:
                for m in range(HALF):
                    hidden(k, 4 * (e + 1) + m, 0, e + 1, m)
            pe.wait_ge(s_hid_lo, k * HALVES + 4 * e + 4 + 2)
            for u in range(2):
                n = (k * NE + e) * 2 + u
                pe.wait_ge(s_y_free, n + 1)
                for t in (2 * u, 2 * u + 1):
                    ts = slice(t * TILE, (t + 1) * TILE)
                    for f in range(HALF):
                        last = three(psY[0:TILE, u, (t % 2) * D:(t % 2 + 1) * D], hid_hi[1][:, f, ts],
                                     hid_lo[1][:, f, ts], w_hi[2][:, e, f, :], w_lo[2][:, e, f, :], False,
                                     f == 0, f == HALF - 1)
                last.then_inc(s_y, 1)

        for layer in range(2):
            first = extra * (PAIRS * (layer + 1)) + PAIRS * layer
            extra_passes(pe, extra, extra * (PAIRS * layer) + PAIRS * layer, pair)
            with pe.Fori(0, lead) as i:
                pair(first + i, PAIRS - 1 - i)
            node_A(layer, 0, first=True)
            node_B(layer, 0)
            if layer == 0:
                with pe.Fori(0, BLOCKS - 1) as k:
                    for a in range(2):
                        with pe.If(lead + 2 * k + a < PAIRS):
                            pair(first + lead + 2 * k + a, within(PAIRS - 1 - lead - 2 * k - a, 0, PAIRS - 4))
                        if a == 0:
                            node_A(0, k + 1)
                            node_B(0, k + 1)
                    pe.nop()
            else:
                pe.wait_ge(s_w_lo, PIECES)
                pe.wait_ge(s_wr_lo, 1)
                node_D(0)
                node_E(0, 0)
                node_F(0, 0)

                def experts(k, par, node):
                    experts_start(k, par)
                    for e in range(NE):
                        if node and e % 2 == 0:
                            a, h = e // 4, (e // 2) % 2
                            with pe.If(lead + 2 * k + a < PAIRS):
                                macro(first + lead + 2 * k + a, within(PAIRS - 1 - lead - 2 * k - a, 0, PAIRS - 4), h)
                        expert(k, e)
                        if node:
                            if e == SLOT_A:
                                node_A(1, k + 1)
                            if e == SLOT_B:
                                node_B(1, k + 1)
                            if e == SLOT_D:
                                node_D(k + 1)
                            if e == SLOT_E:
                                node_E(k + 1, 1 - par)
                            if e == SLOT_F:
                                node_F(k + 1, 1 - par)

                with pe.Fori(0, (BLOCKS - 1) // 2) as kk:
                    for par in range(2):
                        experts(2 * kk + par, par, True)
                experts(BLOCKS - 1, 0, False)

    @block.vector
    def _(dve):
        v = nc.vector
        dve.sem_inc(s_deg_free, 1)
        dve.sem_inc(s_agg_free, 1)
        dve.sem_inc(s_hid_lo, 2)
        dve.sem_inc(s_y_free, 2)
        count = [0]

        def pre(ins):
            count[0] += 1
            ins.then_inc(s_pre, 1)
            dve.wait_ge(s_pre, count[0])

        def rsqrt(step, y, var, eps, t):
            step(v.reciprocal(y, y))
            step(v.scalar_tensor_tensor(t, var, eps, y, ALU.add, ALU.mult))
            step(v.scalar_tensor_tensor(t, t, -0.5, y, ALU.mult, ALU.mult))
            step(v.tensor_scalar(t, t, -0.75, 1.5, ALU.max, ALU.add))
            step(v.tensor_tensor(y, y, t, ALU.mult))

        dve.wait_ge(s_dst_in, 48)
        dstf = ldst[:, LROW:2 * LROW]
        pre(v.tensor_copy(dstf, ldst[:, 0:LROW].bitcast(I32)))
        dve.sem_inc(s_prep, 1)
        groups = dstf.rearrange("p (h n) -> p h n", h=GROUP)
        pre(v.tensor_reduce(gext[:, 0, :], groups, AX.X, ALU.min))
        inside = ldst[:, 0:LROW]
        pre(v.scalar_tensor_tensor(inside, dstf, NOWHERE - 1, dstf, ALU.is_lt, ALU.mult))
        pre(v.tensor_reduce(gext[:, 1, :], inside.rearrange("p (h n) -> p h n", h=GROUP), AX.X, ALU.max))
        dve.wait_ge(s_pool, 10)
        for q in range(2):
            for h in range(2):
                pre(v.tensor_scalar(diag[:, (2 * q + h) * LROWS:(2 * q + h + 1) * LROWS], ident[0:LROWS, 0:LROWS],
                                    gext[:, q, h:h + 1], None, ALU.mult))
        dve.sem_inc(s_prep, 1)
        dve.wait_ge(s_ew_in, 48)
        ewf = lew[:, LROW:2 * LROW]
        pre(v.scalar_tensor_tensor(ewf, lew[:, 0:LROW], -1.0, lew[:, 0:LROW], ALU.mult, ALU.max))
        pre(v.scalar_tensor_tensor(ewf, ewf, FINITE_MAX, ewf, ALU.is_le, ALU.mult))
        pre(v.tensor_scalar(ewf, ewf, EDGE_MIN, None, ALU.max))
        pre(v.scalar_tensor_tensor(ewf, dstf, NOWHERE - 1, ewf, ALU.is_lt, ALU.mult))
        dve.sem_inc(s_prep, 1)
        dve.wait_ge(s_src_in, 48)
        pre(v.tensor_copy(lsrc[:, LROW:2 * LROW], lsrc[:, 0:LROW].bitcast(I32)))
        dve.sem_inc(s_prep, 1)
        def num(n):
            return room[:, n * NG:(n + 1) * NG]

        gmin, gmax, off, blk, pairf = (num(n) for n in range(5))
        dve.wait_ge(s_prep_pe, LCH + 1)
        for q, t in ((0, gmin), (1, gmax)):
            pre(v.tensor_copy(t.rearrange("p (n h) -> p h n", h=2),
                              psN[:, 0, q * 2 * LROWS:(q + 1) * 2 * LROWS].rearrange("p (h n) -> p h n", h=2)))
        mmin = small[:, 0:2 * PAIRS]
        pre(v.tensor_reduce(mmin, gmin.rearrange("p (m g) -> p m g", g=GROUPS), AX.X, ALU.min))
        pre(v.tensor_tensor(off.rearrange("p (m g) -> p m g", g=GROUPS), gmin.rearrange("p (m g) -> p m g", g=GROUPS),
                            mmin.unsqueeze(2).broadcast_to([128, 2 * PAIRS, GROUPS]), ALU.subtract))
        pre(v.tensor_reduce(scal[:, 0:1], off, AX.X, ALU.max))
        pre(v.tensor_tensor(blk, gmax, gmin, ALU.subtract))
        pre(v.tensor_reduce(scal[:, 1:2], blk, AX.X, ALU.max))
        pre(v.tensor_scalar(scal[:, 2:3], scal[:, 0:1], float(STRETCH - WIN), None, ALU.is_le))
        pre(v.scalar_tensor_tensor(scal[:, 2:3], scal[:, 1:2], float(WIN - 1), scal[:, 2:3], ALU.is_le, ALU.mult))
        pre(v.tensor_scalar(scal[:, 3:4], scal[:, 2:3], -float(PASSES - 1), float(PASSES - 1), ALU.mult, ALU.add))
        pre(v.tensor_scalar(blk, gmax, float(BLOCK), None, ALU.is_ge))
        for b in range(2, BLOCKS):
            pre(v.scalar_tensor_tensor(blk, gmax, float(b * BLOCK), blk, ALU.is_ge, ALU.add))
        pre(v.tensor_scalar(blk, blk, 2.0, 3.0, ALU.mult, ALU.add))
        pre(v.tensor_copy(pairf, pair_i))
        pre(v.scalar_tensor_tensor(blk, blk, float(PAIRS), pairf, ALU.min, ALU.subtract))
        pre(v.tensor_reduce(scal[:, 4:5], blk, AX.X, ALU.max))
        pre(v.tensor_copy(ctrl[0:1, 0:2], scal[0:1, 3:5]))
        pre(v.tensor_scalar(gmin, gmin, scal[:, 2:3], None, ALU.mult))
        pre(v.tensor_scalar(off, off, scal[:, 2:3], None, ALU.mult))
        pre(v.tensor_scalar(place[:, :], mmin, scal[:, 2:3], None, ALU.mult))
        metav = meta[:, :].rearrange("p (m w) -> p m w", w=META)
        pre(v.tensor_copy(metav[0:1, :, 0:GROUPS], off[32:33, :].rearrange("p (m g) -> p m g", g=GROUPS)))
        pre(v.tensor_copy(metav[0:1, :, GROUPS], place[32:33, :]))
        pre(v.tensor_tensor(rel[:, :].rearrange("p (n a b) -> p n a b", a=2, b=2),
                            psH[:, 0, 0:CHUNKS].rearrange("p (a b n) -> p n a b", a=2, b=2),
                            gmin.rearrange("p (n a) -> p n a", a=2).unsqueeze(3).broadcast_to([128, LROWS, 2, 2]),
                            ALU.subtract))
        dve.wait_ge(s_prep_pe, 2 * LCH + 1)
        pre(v.tensor_copy(ew[:, :].rearrange("p (n c) -> p n c", c=LCH),
                          psY[:, 0, 0:CHUNKS].rearrange("p (c n) -> p n c", c=LCH)))
        rest = room[:, 0:CHUNKS]
        pre(v.tensor_copy(ew3[:, :, 0], ew[:, :]))
        pre(v.tensor_tensor(rest, ew[:, :], ew3[:, :, 0], ALU.subtract))
        pre(v.tensor_copy(ew3[:, :, 1], rest))
        pre(v.tensor_tensor(ew3[:, :, 2], rest, ew3[:, :, 1], ALU.subtract))
        pre(v.tensor_copy(iota[:, :], iota_i[:, :]))
        dve.sem_inc(s_meta, 1)
        pre(v.memset(degrow, 0.0))
        dve.wait_ge(s_prep_pe, 3 * LCH + 1)
        v.tensor_copy(srcs[:, :].rearrange("p (n c) -> p n c", c=LCH),
                      psH[:, 1, 0:CHUNKS].rearrange("p (c n) -> p n c", c=LCH)).then_inc(s_srcs, 1)
        for b in range(BLOCKS):
            dve.wait_ge(s_x_in[b], 16 if b < BLOCKS - 1 else 32)
            for t in range(BT):
                last = v.bn_stats(stats[:, t, :], x_all[:, b * BT + t, :])
            pre(last)
            for t in range(BT):
                last = v.bn_aggr(mv[:, b * BT + t, :], stats[:, t, :])
            pre(last)
            pre(v.tensor_scalar(x_all[:, b * BT:(b + 1) * BT, :], x_all[:, b * BT:(b + 1) * BT, :],
                                -FINITE_MAX, FINITE_MAX, ALU.max, ALU.min))
        dve.sem_inc(s_var_x, 1)
        dve.wait_ge(s_sqrt_x, 1)
        rsqrt(pre, rstd[:, :], mv[:, :, 1], LN_EPS, newton[:, :])
        pre(v.scalar_tensor_tensor(nmr[:, :], mv[:, :, 0], -1.0, rstd[:, :], ALU.mult, ALU.mult))
        pre(v.tensor_scalar(odd[:, :], nmr[:, :], 0.0, 0.0, ALU.mult, ALU.not_equal))
        nil = zero1[0:TILE, :].broadcast_to([TILE, TILES])
        pre(v.copy_predicated(rstd[:, :], odd[:, :], nil))
        v.copy_predicated(nmr[:, :], odd[:, :], nil).then_inc(s_stat_x, 1)

        dve.wait_ge(s_prep_pe, 3 * LCH + 3)
        pre(v.tensor_copy(par_T, psY[:, 1, 0:10 * NE * HALF].rearrange("p (l i c) -> p l i c", l=2, i=5)))
        b_, g_, be_, m_, v_ = (par_T[:, :, i, :] for i in range(5))
        dve.sem_inc(s_var_par, 1)
        dve.wait_ge(s_sqrt_par, 1)
        rsqrt(pre, hid_s[:, :, :], v_, BN_EPS, hid_b[:, :, :])
        pre(v.tensor_tensor(hid_s[:, :, :], hid_s[:, :, :], g_, ALU.mult))
        pre(v.tensor_tensor(hid_b[:, :, :], b_, m_, ALU.subtract))
        pre(v.tensor_tensor(hid_b[:, :, :], hid_b[:, :, :], hid_s[:, :, :], ALU.mult))
        v.tensor_tensor(hid_b[:, :, :], hid_b[:, :, :], be_, ALU.add).then_inc(s_par, 1)
        extra, lead = control(dve)

        def columns(pb, h):
            return ds(pb * (2 * MC) + h * MC, MC)

        def over_window(t):
            return t.unsqueeze(2).broadcast_to([128, MC, WIN])

        iota_bc = iota[:, :].unsqueeze(1).broadcast_to([128, MC, WIN])

        def stretch_place(pb, h):
            return dve.value_load(meta[0:1, ds(pb * (2 * META) + h * META + GROUPS, 1)], min_val=0, max_val=NP)

        def degree_pair(g, pb):
            for h in range(2):
                v.tensor_tensor(onehot_b[:, h, :, :], iota_bc, over_window(rel[:, columns(pb, h)]),
                                ALU.is_equal).then_inc(s_deg_oh, 1)
                v.tensor_copy(ew_st[:, h, :, :], ew3[:, columns(pb, h), :]).then_inc(s_deg_oh, 1)
            for h in range(2):
                m = 2 * g + h
                part = degrow[:, ds(stretch_place(pb, h), STRETCH)]
                dve.wait_ge(s_deg_mm, m + 1)
                v.tensor_tensor(part, part, psA[0:3, 0, 0:STRETCH], ALU.add).then_inc(s_deg_free, 1)
                dve.wait_ge(s_deg_free, m + 2)
                carry(dve)

        def advance(nth):
            def after(p):
                v.tensor_scalar(rel[:, :], rel[:, :], -float(WIN), None, ALU.add).then_inc(s_adv, 1)
                v.tensor_scalar(place[:, :], place[:, :], float(WIN), None, ALU.add).then_inc(s_adv, 1)
                dve.wait_ge(s_adv, p * 3 + nth * ADVANCES + 2)
                v.tensor_copy(metav[0:1, :, GROUPS], place[32:33, :]).then_inc(s_adv, 1)
                dve.wait_ge(s_adv, p * 3 + nth * ADVANCES + 3)
                dve.sem_inc(s_moved, 1)
            return after

        def rewind(nth):
            at = nth * ADVANCES + 3 * (PASSES - 1)
            with dve.If(extra > 0):
                v.tensor_scalar(rel[:, :], rel[:, :], float(WIN * (PASSES - 1)), None, ALU.add).then_inc(s_adv, 1)
                v.tensor_scalar(place[:, :], place[:, :], -float(WIN * (PASSES - 1)), None, ALU.add).then_inc(s_adv, 1)
                dve.wait_ge(s_adv, at + 2)
                v.tensor_copy(metav[0:1, :, GROUPS], place[32:33, :]).then_inc(s_adv, 1)
                dve.wait_ge(s_adv, at + 3)
            dve.nop()

        extra_passes(dve, extra, 0, degree_pair, advance(0))
        with dve.Fori(0, PAIRS) as i:
            degree_pair(extra * PAIRS + i, PAIRS - 1 - i)
        dve.sem_inc(s_degrow, 1)
        rewind(0)
        dve.wait_ge(s_degT, 1)
        dve.wait_ge(s_sqrt_deg, 1)
        rsqrt(pre, dis[:, :], psN[0:TILE, 1, 0:TILES], 1.0, newton[:, :])
        dve.sem_inc(s_dis, 1)
        dve.wait_ge(s_g1_out, 16 * BLOCKS)
        pre(v.memset(aggT[:, :, :], 0.0))

        def onehots(g, pb, h):
            m = 2 * g + h
            v.tensor_tensor(onehot[:, h, :, :], iota_bc, over_window(rel[:, columns(pb, h)]),
                            ALU.is_equal).then_inc(s_ohc, 1)
            dve.wait_ge(s_ohc, m + 1)
            v.tensor_tensor(onehot[:, h, :, :], onehot[:, h, :, :], over_window(ew[:, columns(pb, h)]),
                            ALU.mult).then_inc(s_oh, 1)

        def take(g, pb, h):
            m = 2 * g + h
            part = aggT[:, :, ds(stretch_place(pb, h), STRETCH)]
            dve.wait_ge(s_used, (m + 1) * GROUPS + GROUPS)
            v.tensor_tensor(part, part, psA[:, :, 0:STRETCH], ALU.add).then_inc(s_agg_free, 1)
            dve.wait_ge(s_agg_free, m + 2)
            carry(dve)

        def pair(g, pb):
            onehots(g, pb, 0)
            onehots(g, pb, 1)
            take(g, pb, 0)
            take(g, pb, 1)

        steps = {0: (s_ch1, CHAIN1), 1: (s_ch2, CHAIN2)}
        place_in = [0]

        def chain(layer, j, ins):
            s, per = steps[layer]
            place_in[0] += 1
            ins.then_inc(s, 1)
            dve.wait_ge(s, j * per + place_in[0])

        def block_stats(layer, j, src_t, done, nth):
            for t in range(BT):
                last = v.bn_stats(stats[:, t, :], src_t[0:TILE, t, :])
            chain(layer, j, last)
            carry(dve)
            for t in range(BT):
                last = v.bn_aggr(bmv[:, t, :], stats[:, t, :])
            last.then_inc(s_var, 1)
            dve.wait_ge(s_sqrt, nth)
            rsqrt(lambda ins: chain(layer, j, ins), brstd[:, :], bmv[:, :, 1], LN_EPS, newton[:, 0:BT])
            v.scalar_tensor_tensor(bnmr[:, :], bmv[:, :, 0], -1.0, brstd[:, :], ALU.mult, ALU.mult).then_inc(done, 1)

        def node_A(layer, j):
            n = layer * BLOCKS + j
            place_in[0] = 0
            own = aggT[:, :, ds((BLOCKS - 1 - j) * BLOCK, BLOCK)]
            dve.wait_ge(s_gT, n + 1)
            carry(dve)
            v.tensor_tensor(aggst[:, :, :], own, psN[:, :, 0:BLOCK], ALU.add).then_inc(s_aggst, 1)
            if layer == 0:
                dve.wait_ge(s_aggst, n + 1)
                carry(dve)
                chain(layer, j, v.tensor_tensor(own.bitcast(I32), own.bitcast(I32), own.bitcast(I32), ALU.bitwise_xor))

        def node_B(layer, j, first=False):
            n = layer * BLOCKS + j
            dve.wait_ge(s_conv, n + 1)
            if layer == 0 and not first:
                dve.wait_ge(s_h_out, 16 * j)
            if layer == 1 and first:
                dve.wait_ge(s_h_out, 16 * BLOCKS)
            for t in range(BT):
                last = v.scalar_tensor_tensor(hc[0:TILE, t, :], psN[0:TILE, t // 2, (t % 2) * D:(t % 2 + 1) * D],
                                              dis[:, ds((BLOCKS - 1 - j) * BT + t, 1)], gvec[:, 0, :],
                                              ALU.mult, ALU.add)
            last.then_inc(s_conv_ev, 1)
            dve.wait_ge(s_conv_ev, n + 1)
            hcf = hc[0:TILE, :, :].rearrange("p t d -> p (t d)")
            chain(layer, j, v.tensor_scalar(bad[:, :], hcf, 0.0, 0.0, ALU.mult, ALU.not_equal))
            carry(dve)
            chain(layer, j, v.copy_predicated(hcf, bad[:, :], zero1[0:TILE, :].broadcast_to([TILE, BT * D])))
            block_stats(layer, j, hc, s_stat, j + 1 if layer == 0 else BLOCKS + 2 * j + 1)

        def node_C(layer, j, par=0, xlast=False):
            n = layer * BLOCKS + j
            h = hc[0:TILE, :, :]

            def bc(i):
                return gvec[:, i, :].unsqueeze(1).broadcast_to([TILE, BT, D])

            dve.wait_ge(s_norm, (n + 1) * BT)
            chain(layer, j, v.tensor_tensor(h, h, bc(1), ALU.mult))
            chain(layer, j, v.tensor_tensor(h, h, bc(2), ALU.add))
            chain(layer, j, v.scalar_tensor_tensor(h, h, FINITE_MAX, h, ALU.is_le, ALU.mult))
            dve.wait_ge(s_hres_in, (n + 1) * 16)
            v.scalar_tensor_tensor(h, h, 0.0, h_res[0:TILE, :, :], ALU.max, ALU.add).then_inc(s_h, 1)
            dve.wait_ge(s_h, n + 1)
            if layer == 1:
                keep = h_res[0:TILE, :, :].bitcast(I32)
                hi32 = hc[0:TILE, :, :].bitcast(I32)
                chain(layer, j, v.tensor_scalar(keep, h, FINITE_MAX, -1.0, ALU.is_le, ALU.mult))
                chain(layer, j, v.tensor_tensor(hi32, hi32, keep, ALU.bitwise_and))
                dve.wait_ge(s_x_blk[par], 16 * (j // 2 + 1) if isinstance(j, int) else x_count(j))
                if xlast:
                    dve.wait_ge(s_x_last, 16)
                a = acc[par][0:TILE, :, :]
                chain(layer, j, v.tensor_tensor(a, a, h, ALU.add))
                block_stats(layer, j, acc[par], s_stat2, BLOCKS + 2 * j + 2)

        kk_now = [None]

        def x_count(j):
            return kk_now[0]

        def node_D(j, par):
            dve.wait_ge(s_hnT_hi, j + 1)
            v.tensor_tensor(hnT_lo[par][:, :, :], psN[:, :, 0:BLOCK], hnT_hi[par][:, :, :].bitcast(F32),
                            ALU.subtract).then_inc(s_hnT_lo, 1)

        def node_E(j):
            dve.wait_ge(s_logit, j + 1)
            chain(1, j, v.tensor_tensor(logit[:, :, :], psN[0:TILE, 0, 0:BT * NE].rearrange("p (t e) -> p t e", e=NE),
                                        br_bc[:, :].unsqueeze(1).broadcast_to([TILE, BT, NE]), ALU.add))
            chain(1, j, v.tensor_reduce(lmax[:, :], logit[:, :, :], AX.X, ALU.max))
            v.tensor_tensor(logit[:, :, :], logit[:, :, :], lmax[:, :].unsqueeze(2).broadcast_to([TILE, BT, NE]),
                            ALU.subtract).then_inc(s_lsub, 1)

        def node_F(j, par):
            dve.wait_ge(s_exp, j + 1)
            chain(1, j, v.tensor_reduce(lsum[:, :], logit[:, :, :], AX.X, ALU.add))
            chain(1, j, v.reciprocal(lsum[:, :], lsum[:, :]))
            v.tensor_tensor(gate[par][:, :, :], logit[:, :, :], lsum[:, :].unsqueeze(2).broadcast_to([TILE, BT, NE]),
                            ALU.mult).then_inc(s_gate, 1)

        def node_G(j, par):
            dve.wait_ge(s_gbo, j + 1)
            a = acc[par][0:TILE, :, :].rearrange("p (u t) d -> p u (t d)", u=2)
            v.tensor_tensor(a, a, psN[0:TILE, :, :], ALU.add).then_inc(s_acc0, 1)

        def low_half(k, idx, l, m):
            n = k * HALVES + idx
            dve.wait_ge(s_hid_hi, n + 1)
            v.tensor_tensor(hid_lo[l][:, m, :], hid[:, m, :], hid_hi[l][:, m, :].bitcast(F32),
                            ALU.subtract).then_inc(s_hid_lo, 1)

        def expert(k, e, par):
            for m in range(HALF):
                low_half(k, 4 * e + 2 + m, 1, m)
            if e + 1 < NE:
                for m in range(HALF):
                    low_half(k, 4 * (e + 1) + m, 0, m)
            for u in range(2):
                n = (k * NE + e) * 2 + u
                if e == 0:
                    dve.wait_ge(s_acc0, k + 1)
                else:
                    dve.wait_ge(s_y_free, n - 2 + 1 + 2)
                dve.wait_ge(s_y, n + 1)
                for t in (2 * u, 2 * u + 1):
                    last = v.scalar_tensor_tensor(acc[par][0:TILE, t, :], psY[0:TILE, u, (t % 2) * D:(t % 2 + 1) * D],
                                                  gate[par][:, t, e:e + 1], acc[par][0:TILE, t, :], ALU.mult, ALU.add)
                last.then_inc(s_y_free, 1)

        for layer in range(2):
            first = extra * (PAIRS * (layer + 1)) + PAIRS * layer
            extra_passes(dve, extra, extra * (PAIRS * layer) + PAIRS * layer, pair, advance(layer + 1))
            with dve.Fori(0, lead) as i:
                pair(first + i, PAIRS - 1 - i)
            node_A(layer, 0)
            if layer == 0:
                node_B(0, 0, first=True)
                node_C(0, 0)
                with dve.Fori(0, BLOCKS - 1) as k:
                    for a in range(2):
                        with dve.If(lead + 2 * k + a < PAIRS):
                            pair(first + lead + 2 * k + a, within(PAIRS - 1 - lead - 2 * k - a, 0, PAIRS - 4))
                        if a == 0:
                            node_A(0, k + 1)
                            node_B(0, k + 1)
                            node_C(0, k + 1)
                    dve.nop()
                rewind(1)
            else:
                dve.wait_ge(s_gvec_in, 128)
                dve.wait_ge(s_acc_pad, 1)
                node_B(1, 0, first=True)
                node_C(1, 0, par=0, xlast=True)
                node_D(0, 0)
                node_E(0)
                node_F(0, 0)
                node_G(0, 0)

                def experts(k, par, node):
                    for m in range(HALF):
                        low_half(k, m, 0, m)
                    for e in range(NE):
                        if node and e % 2 == 0:
                            a, h = e // 4, (e // 2) % 2
                            with dve.If(lead + 2 * k + a < PAIRS):
                                g, pb = first + lead + 2 * k + a, within(PAIRS - 1 - lead - 2 * k - a, 0, PAIRS - 4)
                                if h == 0:
                                    onehots(g, pb, 0)
                                    onehots(g, pb, 1)
                                take(g, pb, h)
                        if node and e == SLOT_F:
                            node_F(k + 1, 1 - par)
                        expert(k, e, par)
                        if node:
                            if e == SLOT_A:
                                node_A(1, k + 1)
                            if e == SLOT_B:
                                node_B(1, k + 1)
                            if e == SLOT_C:
                                node_C(1, k + 1, par=1 - par)
                            if e == SLOT_D:
                                node_D(k + 1, 1 - par)
                            if e == SLOT_E:
                                node_E(k + 1)
                            if e == SLOT_F:
                                node_G(k + 1, 1 - par)

                with dve.Fori(0, (BLOCKS - 1) // 2) as kk:
                    for par in range(2):
                        kk_now[0] = (kk + 1) * 16 if par == 0 else (kk + 2) * 16
                        experts(2 * kk + par, par, True)
                experts(BLOCKS - 1, 0, False)


_NAMES = ["x", "src", "dst", "edge_weight"] \
    + ["L0_gnn_" + n for n in ("W1", "b1", "ln_g1", "ln_b1", "W2", "b2", "ln_g2", "ln_b2")] \
    + ["L0_ffn_" + n for n in ("Wr", "br", "W1", "b1", "g1", "be1", "m1", "v1", "W2", "b2", "g2", "be2", "m2", "v2",
                               "Wo", "bo")]


def kernel(**inputs):
    import numpy as _np
    import concourse.bacc as _bacc
    from concourse import mybir as _mybir
    from concourse.bass_utils import run_bass_kernel_spmd as _run

    nc = _bacc.Bacc("TRN2", target_bir_lowering=False, num_devices=1, dynamic_dma_scratch_size=8192)
    arrays, a = {}, {}
    for name in _NAMES:
        host = _np.ascontiguousarray(inputs[name])
        arrays["in_" + name] = host
        a[name] = nc.dram_tensor("in_" + name, host.shape, _mybir.dt.from_np(host.dtype), kind="ExternalInput").ap()
    out = nc.dram_tensor("out_0", (N, D), F32, kind="ExternalOutput").ap()

    def g(n):
        return a["L0_gnn_" + n]

    def f(n):
        return a["L0_ffn_" + n]

    build_program(nc, a["x"], a["src"], a["dst"], a["edge_weight"], (g("W1"), g("W2")), (g("b1"), g("b2")),
                  (g("ln_g1"), g("ln_g2")), (g("ln_b1"), g("ln_b2")), f("Wr"), f("br"),
                  [f(n) for n in ("b1", "g1", "be1", "m1", "v1")], [f(n) for n in ("b2", "g2", "be2", "m2", "v2")],
                  f("W1"), f("W2"), f("Wo"), f("bo"), out)
    r = _run(nc, [arrays], core_ids=[0])
    return r.results[0]["out_0"]
```

```python
from contextlib import ExitStack

import concourse.bass as bass
from concourse import mybir

F32 = mybir.dt.float32
F32R = mybir.dt.float32r
BF16 = mybir.dt.bfloat16
I32 = mybir.dt.int32
U8 = mybir.dt.uint8
ALU = mybir.AluOpType
ACT = mybir.ActivationFunctionType
AX = mybir.AxisListType

FINITE_MAX = 3.4028234663852886e38
LN_EPS = 1e-5
BN_EPS = 1e-3
EDGE_MIN = 1e-6

N, D = 3125, 256
E = 50000
NE = 8
HALF = D // 128
CHUNK = 128
GROUP = 2
GROUPS = 7
MC = GROUP * GROUPS
PAIRS = 14
CHUNKS = PAIRS * 2 * MC
NG = CHUNKS // GROUP
WIN = 64
STRETCH = 448
TILE = 112
BT = 4
BLOCK = TILE * BT
BLOCKS = 7
NP = BLOCK * BLOCKS
TILES = NP // TILE
PASSES = NP // WIN
AGG = NP + STRETCH
NOWHERE = 8192.0
LROWS, LCH = CHUNKS // 4, 4
META = 8
LAST_ROWS = N - (TILES - 1) * TILE
LROW = LCH * CHUNK
REST = E - (LROWS - 1) * LROW
HALVES = 4 * NE
PIECES = 3 * NE // 2
STEP_B, STEP_S, STEP_R, STEP_S2 = 1, 2, 3, 5
LEAD_MIN = 2
SPLIT = 4
ADVANCES = 3 * PASSES
CHAIN1, CHAIN2 = 12, 24


def build_program(nc, x, src, dst, edge_weight, gW, gb, gg, gbe, Wr, br, par1, par2, W1, W2, Wo, bo, out):
    ctx = ExitStack()
    with ctx:
        build_inside(ctx, nc, x, src, dst, edge_weight, gW, gb, gg, gbe, Wr, br, par1, par2,
                     W1, W2, Wo, bo, out)


def build_inside(ctx, nc, x, src, dst, edge_weight, gW, gb, gg, gbe, Wr, br, par1, par2,
                 W1, W2, Wo, bo, out):
    def sb(name, shape, dt=F32):
        return ctx.enter_context(nc.sbuf_tensor(name, shape, dt))

    def pb(name, shape, dt=F32):
        return ctx.enter_context(nc.psum_tensor(name, shape, dt))

    def sem(name):
        return ctx.enter_context(nc.semaphore(name))

    ds = bass.ds

    table = [nc.dram_tensor(f"table{n}", [NP, D], F32, kind="Internal").ap() for n in range(2)]
    resid = nc.dram_tensor("resid", [NP, D], F32, kind="Internal").ap()

    w_hi = [sb(f"w_hi{n}", [128, NE, HALF, D], F32R) for n in range(3)]
    w_lo = [sb(f"w_lo{n}", [128, NE, HALF, D], F32R) for n in range(3)]
    ring = sb("ring", [128, MC, D])
    onehot = sb("onehot", [128, 2, MC, WIN])
    onehot_b = onehot[:, :, :, :].bitcast(BF16)[:, :, :, 0:WIN]
    aggT = sb("aggT", [128, HALF, AGG])
    srcs = sb("srcs", [128, CHUNKS], I32)
    rel = sb("rel", [128, CHUNKS])
    ew = sb("ew", [128, CHUNKS])
    hnT_hi = [sb(f"hnT_hi{n}", [128, HALF, BLOCK], F32R) for n in range(2)]
    hnT_lo = [sb(f"hnT_lo{n}", [128, HALF, BLOCK], F32R) for n in range(2)]
    hid_hi = [sb(f"hid_hi{n}", [128, HALF, BLOCK], F32R) for n in range(2)]
    hid_lo = [sb(f"hid_lo{n}", [128, HALF, BLOCK], F32R) for n in range(2)]
    hid = sb("hid", [128, HALF, BLOCK])
    acc = [sb(f"acc{n}", [128, BT, D]) for n in range(2)]
    g_blk = sb("g_blk", [128, BT, D])
    h_res = sb("h_res", [128, BT, D])
    hc = sb("hc", [128, BT, D])
    aggst = sb("aggst", [128, HALF, BLOCK])
    bad = sb("bad", [TILE, BT * D], U8)
    gW_sb = sb("gW_sb", [128, HALF, D])
    gvec = sb("gvec", [TILE, 3, D])
    bo_meta = sb("bo_meta", [33, D])
    bo_sb = bo_meta[0:NE, :]
    meta = bo_meta[32:33, 0:2 * PAIRS * META].bitcast(I32)
    ident = sb("ident", [128, 128])
    iota = sb("iota", [128, WIN])
    zeros_b = sb("zeros_b", [128, STRETCH], BF16)
    zero1 = sb("zero1", [128, 1])
    ones1 = sb("ones1", [128, 1])
    br_bc = sb("br_bc", [TILE, NE])
    hid_s = sb("hid_s", [128, 2, NE * HALF])
    hid_b = sb("hid_b", [128, 2, NE * HALF])
    dis = sb("dis", [TILE, TILES])
    stats = sb("stats", [TILE, BT, 6])
    mv = sb("mv", [TILE, TILES, 2])
    rstd = sb("rstd", [TILE, TILES])
    nmr = sb("nmr", [TILE, TILES])
    logit = sb("logit", [TILE, BT, NE])
    lmax = sb("lmax", [TILE, BT])
    lsum = sb("lsum", [TILE, BT])
    gate = [sb(f"gate{n}", [TILE, BT, NE]) for n in range(2)]
    wr_f = sb("wr_f", [128, HALF, NE])
    wr_hi = sb("wr_hi", [128, HALF, NE], F32R)
    wr_lo = sb("wr_lo", [128, HALF, NE], F32R)
    small = sb("small", [128, 2 * PAIRS])
    place = sb("place", [128, 2 * PAIRS])
    bmv = sb("bmv", [TILE, BT, 2])
    newton = sb("newton", [TILE, TILES])
    eps = sb("eps", [128, 2])
    brstd = sb("brstd", [TILE, BT])
    bnmr = sb("bnmr", [TILE, BT])
    drow = sb("drow", [TILE, 2, TILES])
    odd = sb("odd", [TILE, TILES], U8)
    ctrl = sb("ctrl", [1, 4], I32)
    idx_st = sb("idx_st", [128, 2, MC], I32)

    scal = sb("scal", [128, 8])
    gext = sb("gext", [LROWS, 2, GROUP])

    gateT = aggst[0:NE, 0, :]

    def flat(t):
        return t[:, :, :].rearrange("p a b -> p (a b)")

    x_all = flat(aggT)[0:TILE, :].rearrange("p (t d) -> p t d", d=D)
    degrow = flat(ring)[0:3, :]
    ew3 = flat(hid).bitcast(BF16)[:, 0:3 * CHUNKS].rearrange("p (c k) -> p c k", k=3)
    iota_i = flat(hid)[:, 3 * CHUNKS // 2:3 * CHUNKS // 2 + WIN].bitcast(I32)
    ew_st = flat(hid)[:, 656:656 + 3 * MC].bitcast(BF16).rearrange("p (h s k) -> p h s k", h=2, k=3)
    par_T = flat(hid)[:, 704:704 + 10 * NE * HALF].rearrange("p (l i c) -> p l i c", l=2, i=5)
    ldst, lsrc, lew = (flat(t)[0:LROWS, :] for t in (hc, g_blk, h_res))
    diag = flat(acc[0])[0:LROWS, 0:4 * LROWS]
    ones_m = flat(acc[0])[0:LROWS, 512:640]
    room = flat(acc[1])
    pair_i = flat(aggst)[:, 0:NG].bitcast(I32)
    par_st = flat(aggst)[0:5 * NE * HALF, 512:768].rearrange("p (l n) -> p l n", l=2)
    stage = [acc[n][:, :, :].rearrange("p (e k) n -> p e k n", k=HALF) for n in range(2)]

    psA = pb("psA", [128, 2, 512])
    psN = pb("psN", [128, 2, 512])
    psH = pb("psH", [128, 2, 512])
    psY = pb("psY", [128, 2, 512])

    s_pad = sem("s_pad")
    s_pool = sem("s_pool")
    s_wr_hi = sem("s_wr_hi")
    s_wr_lo = sem("s_wr_lo")
    s_x_last = sem("s_x_last")
    s_degrow = sem("s_degrow")
    s_carried = sem("s_carried")
    s_dst_in = sem("s_dst_in")
    s_src_in = sem("s_src_in")
    s_ew_in = sem("s_ew_in")
    s_x_in = [sem(f"s_x_in{b}") for b in range(BLOCKS)]
    s_const_in = sem("s_const_in")
    s_par_in = sem("s_par_in")
    s_pre = sem("s_pre")
    s_prep = sem("s_prep")
    s_prep_pe = sem("s_prep_pe")
    s_meta = sem("s_meta")
    s_srcs = sem("s_srcs")
    s_var_x = sem("s_var_x")
    s_sqrt_x = sem("s_sqrt_x")
    s_var_par = sem("s_var_par")
    s_sqrt_par = sem("s_sqrt_par")
    s_sqrt_deg = sem("s_sqrt_deg")
    s_var = sem("s_var")
    s_sqrt = sem("s_sqrt")
    s_h0 = sem("s_h0")
    s_clean = sem("s_clean")
    s_g1_odd = sem("s_g1_odd")
    s_dis = sem("s_dis")
    s_g1 = sem("s_g1")
    s_g1_out = sem("s_g1_out")
    s_deg_oh = sem("s_deg_oh")
    s_deg_mm = sem("s_deg_mm")
    s_deg_free = sem("s_deg_free")
    s_degT = sem("s_degT")
    s_wst_in = [sem(f"s_wst_in{n}") for n in range(2)]
    s_w_hi = sem("s_w_hi")
    s_w_lo = sem("s_w_lo")
    s_par = sem("s_par")
    s_gath = [sem(f"s_gath{s}") for s in range(MC)]
    s_used = sem("s_used")
    s_oh = sem("s_oh")
    s_agg_free = sem("s_agg_free")
    s_idx = sem("s_idx")
    s_ohc = sem("s_ohc")
    s_adv = sem("s_adv")
    s_g_in = sem("s_g_in")
    s_hres_in = sem("s_hres_in")
    s_x_blk = [sem(f"s_x_blk{n}") for n in range(2)]
    s_gvec_in = sem("s_gvec_in")
    s_gT = sem("s_gT")
    s_aggst = sem("s_aggst")
    s_conv = sem("s_conv")
    s_conv_ev = sem("s_conv_ev")
    s_stat = sem("s_stat")
    s_norm = sem("s_norm")
    s_h = sem("s_h")
    s_g2 = sem("s_g2")
    s_h_out = sem("s_h_out")
    s_g2_out = sem("s_g2_out")
    s_ch1 = sem("s_ch1")
    s_ch2 = sem("s_ch2")
    s_stat2 = sem("s_stat2")
    s_hn = sem("s_hn")
    s_hnT = sem("s_hnT")
    s_hnT_hi = sem("s_hnT_hi")
    s_hnT_lo = sem("s_hnT_lo")
    s_logit = sem("s_logit")
    s_lsub = sem("s_lsub")
    s_exp = sem("s_exp")
    s_gate = sem("s_gate")
    s_gateT = sem("s_gateT")
    s_gateT_sb = sem("s_gateT_sb")
    s_gbo = sem("s_gbo")
    s_acc0 = sem("s_acc0")
    s_hid = sem("s_hid")
    s_hid_free = sem("s_hid_free")
    s_hid_hi = sem("s_hid_hi")
    s_hid_lo = sem("s_hid_lo")
    s_y = sem("s_y")
    s_y_free = sem("s_y_free")
    s_out = [sem(f"s_out{n}") for n in range(2)]

    def within(value, low, high):
        return value if isinstance(value, int) else value.with_bounds(min_val=low, max_val=high)

    def carry(eng):
        eng.sem_inc(s_carried, 1)

    def control(eng):
        eng.wait_ge(s_meta, 1)
        extra = eng.value_load(ctrl[0:1, 0:1], min_val=0, max_val=PASSES - 1)
        lead = eng.value_load(ctrl[0:1, 1:2], min_val=LEAD_MIN, max_val=PAIRS)
        return extra, lead

    def extra_passes(eng, extra, base, pair, after=None):
        with eng.If(extra > 0):
            with eng.Fori(0, PASSES - 1) as p:
                with eng.Fori(0, PAIRS) as i:
                    pair(base + p * PAIRS + i, PAIRS - 1 - i)
                if after is not None:
                    after(p)

    block = ctx.enter_context(nc.Block())

    @block.sync
    def _(sp):
        sp.wait_ge(s_pad, 3)
        for tile, array, s_in in ((ldst, dst, s_dst_in), (lew, edge_weight, s_ew_in), (lsrc, src, s_src_in)):
            t = tile[:, 0:LROW] if array is edge_weight else tile[:, 0:LROW].bitcast(I32)
            sp.dma_start(t[0:96, :], array[0:96 * LROW].rearrange("(p n) -> p n", n=LROW)).then_inc(s_in, 16)
            sp.dma_start(t[96:97, :], array[96 * LROW:97 * LROW].rearrange("(p n) -> p n", n=LROW)).then_inc(s_in, 16)
            sp.dma_start(t[97:98, 0:REST], array[97 * LROW:E].rearrange("(p n) -> p n", p=1)).then_inc(s_in, 16)
        for b in range(BLOCKS):
            full = BT if b < BLOCKS - 1 else BT - 1
            sp.dma_start(x_all[:, b * BT:b * BT + full, :],
                         x[b * BLOCK:b * BLOCK + full * TILE, :].rearrange("(t p) d -> p t d", p=TILE)
                         ).then_inc(s_x_in[b], 16)
        sp.wait_ge(s_pad, 4)
        sp.dma_start(x_all[0:LAST_ROWS, TILES - 1, :], x[N - LAST_ROWS:N, :]).then_inc(s_x_in[BLOCKS - 1], 16)
        for l, arrays in enumerate((par1, par2)):
            for i, a in enumerate(arrays):
                rows16 = NE * HALF
                sp.dma_start(par_st[i * rows16:(i + 1) * rows16, l, :], a.rearrange("e (m p) -> (e m) p", p=128)).then_inc(s_par_in, 16)
        sp.dma_start(bo_sb[:, :], bo).then_inc(s_const_in, 16)
        sp.dma_start(br_bc[:, :], br.unsqueeze(0).broadcast_to([TILE, NE])).then_inc(s_const_in, 16)
        sp.dma_start(wr_f[:, :, :], Wr.rearrange("(k p) e -> p k e", p=128)).then_inc(s_const_in, 16)

        def rows(t, b):
            return t[ds(within(b * BLOCK, 0, t.shape[0] - BLOCK), BLOCK), :].rearrange("(t p) d -> p t d", p=TILE)

        def static_rows(t, b):
            return t[b * BLOCK:(b + 1) * BLOCK, :].rearrange("(t p) d -> p t d", p=TILE)

        def layer_consts(layer):
            sp.dma_start(gW_sb[:, :, :], gW[layer].rearrange("(k p) n -> p k n", p=128)).then_inc(s_gvec_in, 16)
            for i, v in enumerate((gb[layer], gg[layer], gbe[layer])):
                sp.dma_start(gvec[:, i, :], v.unsqueeze(0).broadcast_to([TILE, D])).then_inc(s_gvec_in, 16)

        layer_consts(0)
        sp.wait_ge(s_meta, 1)
        for piece in range(PIECES):
            w, e, u = (W1, W2, Wo)[piece // 4], 2 * (piece % 4), piece % 2
            if piece >= 2:
                sp.wait_ge(s_w_lo, piece - 1)
            for i in range(2):
                sp.dma_start(stage[u][:, i, :, :], w[e + i].rearrange("(k p) n -> p k n", p=128)).then_inc(s_wst_in[u], 16)
        for b in range(BLOCKS):
            sp.wait_ge(s_g1, BT // 2 * (b + 1))
            sp.wait_ge(s_g1_odd, BT // 2 * (b + 1))
            sp.dma_start(static_rows(table[0], b), x_all[:, b * BT:(b + 1) * BT, :]).then_inc(s_g1_out, 16)

        def load_table_block(layer, j):
            sp.dma_start(g_blk[0:TILE, :, :], rows(table[layer], BLOCKS - 1 - j)).then_inc(s_g_in, 16)

        def load_x_block(tile, s_in, k):
            sp.dma_start(tile[0:TILE, :, :], rows(x, BLOCKS - 1 - k)).then_inc(s_in, 16)

        def load_last_x_block(tile, s_in):
            tail = (BLOCKS - 1) * BLOCK
            sp.dma_start(tile[0:TILE, 0:BT - 1, :],
                         x[tail:tail + (BT - 1) * TILE, :].rearrange("(t p) d -> p t d", p=TILE)).then_inc(s_in, 16)
            sp.dma_start(tile[0:LAST_ROWS, BT - 1, :], x[N - LAST_ROWS:N, :]).then_inc(s_x_last, 16)
            sp.dma_start(tile[LAST_ROWS:TILE, BT - 1, :], x[0:TILE - LAST_ROWS, :]).then_inc(s_x_last, 16)

        def load_resid_block(j):
            sp.dma_start(h_res[0:TILE, :, :], rows(resid, BLOCKS - 1 - j)).then_inc(s_hres_in, 16)

        def store_layer1(j):
            b = BLOCKS - 1 - j
            sp.wait_ge(s_h, j + 1)
            carry(sp)
            sp.dma_start(rows(resid, b), hc[0:TILE, :, :]).then_inc(s_h_out, 16)
            sp.wait_ge(s_g2, BT * (j + 1))
            carry(sp)
            sp.dma_start(rows(table[1], b), h_res[0:TILE, :, :]).then_inc(s_g2_out, 16)

        def store_out(k, par, last_piece=True):
            first = (BLOCKS - 1 - k) * BLOCK
            sp.dma_start(out[ds(first, (BT - 1) * TILE), :].rearrange("(t p) d -> p t d", p=TILE),
                         acc[par][0:TILE, 0:BT - 1, :]).then_inc(s_out[par], 16)
            sp.dma_start(out[ds(first + (BT - 1) * TILE, LAST_ROWS), :],
                         acc[par][0:LAST_ROWS, BT - 1, :]).then_inc(s_out[par], 16)
            if last_piece:
                sp.dma_start(out[ds(first + (BT - 1) * TILE + LAST_ROWS, TILE - LAST_ROWS), :],
                             acc[par][LAST_ROWS:TILE, BT - 1, :]).then_inc(s_out[par], 16)

        sp.wait_ge(s_g1_out, 16 * BLOCKS)
        sp.wait_ge(s_srcs, 1)
        load_table_block(0, 0)
        load_last_x_block(h_res, s_hres_in)
        store_layer1(0)
        with sp.Fori(1, BLOCKS) as j:
            sp.wait_ge(s_gT, j)
            carry(sp)
            load_table_block(0, j)
            sp.wait_ge(s_g2_out, 16 * j)
            carry(sp)
            load_x_block(h_res, s_hres_in, j)
            store_layer1(j)
        sp.wait_ge(s_g2_out, 16 * BLOCKS)
        sp.wait_ge(s_h_out, 16 * BLOCKS)
        layer_consts(1)
        load_table_block(1, 0)
        load_resid_block(0)
        load_last_x_block(acc[0], s_x_blk[0])
        sp.wait_ge(s_gT, BLOCKS + 1)
        load_table_block(1, 1)
        sp.wait_ge(s_acc0, 1)
        load_resid_block(1)
        load_x_block(acc[1], s_x_blk[1], 1)
        with sp.Fori(0, (BLOCKS - 1) // 2) as kk:
            for par in range(2):
                k = 2 * kk + par
                with sp.If(k + 2 < BLOCKS):
                    sp.wait_ge(s_gT, BLOCKS + k + 2)
                    carry(sp)
                    load_table_block(1, k + 2)
                    sp.wait_ge(s_acc0, k + 2)
                    carry(sp)
                    load_resid_block(k + 2)
                sp.wait_ge(s_y_free, 2 * NE * (k + 1) + 2)
                carry(sp)
                if par == 0:
                    store_out(k, 0, last_piece=False)
                    with sp.If(kk > 0):
                        first = within((BLOCKS - 1 - k) * BLOCK, 0, (BLOCKS - 3) * BLOCK)
                        sp.dma_start(out[ds(first + (BT - 1) * TILE + LAST_ROWS, TILE - LAST_ROWS), :],
                                     acc[0][LAST_ROWS:TILE, BT - 1, :]).then_inc(s_out[0], 16)
                    with sp.Else():
                        sp.dma_start(table[0][0:TILE - LAST_ROWS, :],
                                     acc[0][LAST_ROWS:TILE, BT - 1, :]).then_inc(s_out[0], 16)
                else:
                    store_out(k, 1)
                sp.wait_ge(s_out[par], 48 * (kk + 1))
                carry(sp)
                with sp.If(k + 2 < BLOCKS):
                    load_x_block(acc[par], s_x_blk[par], k + 2)
                sp.nop()
        sp.wait_ge(s_y_free, 2 * NE * BLOCKS + 2)
        store_out(BLOCKS - 1, 0)
        sp.wait_ge(s_out[0], 48 * 4)
        sp.wait_ge(s_out[1], 48 * 3)

    @block.gpsimd
    def _(pool):
        nc.gpsimd.memset(ldst[:, 0:LROW].bitcast(I32), int(NOWHERE)).then_inc(s_pad, 1)
        nc.gpsimd.memset(lew[:, 0:LROW], 0.0).then_inc(s_pad, 1)
        nc.gpsimd.memset(lsrc[:, 0:LROW].bitcast(I32), 0).then_inc(s_pad, 1)
        nc.gpsimd.memset(x_all[:, TILES - 1, :], 0.0).then_inc(s_pad, 1)
        nc.gpsimd.memset(ident[:, :], 0.0).then_inc(s_pool, 1)
        nc.gpsimd.memset(zeros_b[:, :], 0.0).then_inc(s_pool, 1)
        nc.gpsimd.memset(ones_m[:, :], 1.0).then_inc(s_pool, 1)
        nc.gpsimd.memset(ones1[:, :], 1.0).then_inc(s_pool, 1)
        nc.gpsimd.memset(zero1[:, :], 0.0).then_inc(s_pool, 1)
        nc.gpsimd.iota(iota_i[:, :], [[1, WIN]], base=0, channel_multiplier=0).then_inc(s_pool, 1)
        nc.gpsimd.iota(pair_i, [[1, PAIRS], [0, NG // PAIRS]], base=0, channel_multiplier=0).then_inc(s_pool, 1)
        nc.gpsimd.memset(eps[:, 0:1], LN_EPS).then_inc(s_pool, 1)
        nc.gpsimd.memset(eps[:, 1:2], BN_EPS).then_inc(s_pool, 1)
        pool.wait_ge(s_pool, 9)
        nc.gpsimd.affine_select(out=ident[:, :], in_=ident[:, :], compare_op=ALU.not_equal, fill=1.0, base=0,
                                pattern=[[-1, 128]], channel_multiplier=1).then_inc(s_pool, 1)
        pool.wait_ge(s_wr_hi, 1)
        nc.gpsimd.tensor_tensor(wr_lo[:, :, :], wr_f[:, :, :], wr_hi[:, :, :].bitcast(F32), ALU.subtract).then_inc(s_wr_lo, 1)
        for piece in range(PIECES):
            t, e, u = piece // 4, 2 * (piece % 4), piece % 2
            pool.wait_ge(s_w_hi, piece + 1)
            nc.gpsimd.tensor_tensor(w_lo[t][:, e:e + 2, :, :], stage[u], w_hi[t][:, e:e + 2, :, :].bitcast(F32),
                                    ALU.subtract).then_inc(s_w_lo, 1)
        extra, _ = control(pool)
        pool.wait_ge(s_srcs, 1)

        def gathers(layer, g, pb):
            for h in range(2):
                m = 2 * g + h
                nc.gpsimd.tensor_copy(idx_st[:, h, :], srcs[:, ds(pb * (2 * MC) + h * MC, MC)]).then_inc(s_idx, 1)
                pool.wait_ge(s_idx, m + 1)
                for s in range(MC):
                    if s % GROUP == 0:
                        pool.wait_ge(s_used, m * GROUPS + s // GROUP + 1)
                        carry(pool)
                    nc.gpsimd.indirect_dma_start(
                        ring[:, s, :], None, table[layer],
                        bass.IndirectOffsetOnAxis(ap=idx_st[:, h, s:s + 1], axis=0)).then_inc(s_gath[s], 16)

        pool.wait_ge(s_g1_out, 16 * BLOCKS)
        pool.wait_ge(s_degT, 1)
        extra_passes(pool, extra, 0, lambda g, pb: gathers(0, g, pb))
        with pool.Fori(0, PAIRS) as i:
            gathers(0, extra * PAIRS + i, PAIRS - 1 - i)
        pool.wait_ge(s_g2_out, 16 * BLOCKS)
        extra_passes(pool, extra, extra * PAIRS + PAIRS, lambda g, pb: gathers(1, g, pb))
        with pool.Fori(0, PAIRS) as i:
            gathers(1, extra * (2 * PAIRS) + PAIRS + i, PAIRS - 1 - i)

    @block.scalar
    def _(act):
        act.sem_inc(s_hid_free, 2)

        def split_piece(piece):
            t, e, u = piece // 4, 2 * (piece % 4), piece % 2
            act.wait_ge(s_wst_in[u], 32 * (piece // 2 + 1))
            nc.scalar.activation(w_hi[t][:, e:e + 2, :, :], stage[u], ACT.Copy).then_inc(s_w_hi, 1)

        act.wait_ge(s_const_in, 48)
        nc.scalar.activation(wr_hi[:, :, :], wr_f[:, :, :], ACT.Copy).then_inc(s_wr_hi, 1)
        for piece in range(PIECES):
            split_piece(piece)
        act.wait_ge(s_pool, 10)
        act.wait_ge(s_degT, 1)
        nc.scalar.activation(dis[:, :], psN[0:TILE, 1, 0:TILES], ACT.Sqrt, bias=ones1[0:TILE, :]).then_inc(s_sqrt_deg, 1)
        act.wait_ge(s_var_x, 1)
        nc.scalar.activation(rstd[:, :], mv[:, :, 1], ACT.Sqrt, bias=eps[0:TILE, 0:1]).then_inc(s_sqrt_x, 1)
        act.wait_ge(s_dis, 1)
        for t in range(0, TILES, 2):
            nc.scalar.activation(x_all[:, t, :], x_all[:, t, :], ACT.Identity,
                                 bias=drow[:, 1, t:t + 1], scale=drow[:, 0, t:t + 1]).then_inc(s_g1, 1)
        act.wait_ge(s_var_par, 1)
        nc.scalar.activation(hid_s[:, :, :], par_T[:, :, 4, :], ACT.Sqrt, bias=eps[:, 1:2]).then_inc(s_sqrt_par, 1)
        def root(nth):
            act.wait_ge(s_var, nth)
            nc.scalar.activation(brstd[:, :], bmv[:, :, 1], ACT.Sqrt, bias=eps[0:TILE, 0:1]).then_inc(s_sqrt, 1)

        def norm(layer, j):
            act.wait_ge(s_stat, layer * BLOCKS + j + 1)
            for t in range(BT):
                nc.scalar.activation(hc[0:TILE, t, :], hc[0:TILE, t, :], ACT.Identity,
                                     bias=bnmr[:, t:t + 1], scale=brstd[:, t:t + 1]).then_inc(s_norm, 1)

        def first_residual(j):
            act.wait_ge(s_clean, j + 1)
            for t in range(BT):
                col = ds((BLOCKS - 1 - j) * BT + t, 1)
                nc.scalar.activation(h_res[0:TILE, t, :], h_res[0:TILE, t, :], ACT.Identity,
                                     bias=nmr[:, col], scale=rstd[:, col]).then_inc(s_h0, 1)

        def second_table(j):
            act.wait_ge(s_h, j + 1)
            for t in range(BT):
                nc.scalar.activation(h_res[0:TILE, t, :], hc[0:TILE, t, :], ACT.Copy,
                                     scale=dis[:, ds((BLOCKS - 1 - j) * BT + t, 1)]).then_inc(s_g2, 1)

        def norm_x1(j, par):
            act.wait_ge(s_stat2, j + 1)
            for t in range(BT):
                nc.scalar.activation(hc[0:TILE, t, :], acc[par][0:TILE, t, :], ACT.Identity,
                                     bias=bnmr[:, t:t + 1], scale=brstd[:, t:t + 1]).then_inc(s_hn, 1)

        def hnT_high(j, par):
            act.wait_ge(s_hnT, j + 1)
            nc.scalar.activation(hnT_hi[par][:, :, :], psN[:, :, 0:BLOCK], ACT.Copy).then_inc(s_hnT_hi, 1)

        def exponentials(j):
            act.wait_ge(s_lsub, j + 1)
            nc.scalar.activation(logit[:, :, :], logit[:, :, :], ACT.Exp).then_inc(s_exp, 1)

        def gates_T(j):
            act.wait_ge(s_gateT, j + 1)
            nc.scalar.activation(gateT[:, :], psN[0:NE, 1, 0:BLOCK], ACT.Copy).then_inc(s_gateT_sb, 1)

        def hidden_half(k, idx, l, e, m):
            n = k * HALVES + idx
            act.wait_ge(s_hid, n + 1)
            act.wait_ge(s_hid_lo, n + 1)
            col = e * HALF + m
            nc.scalar.activation(hid[:, m, :], psH[:, m, 0:BLOCK], ACT.Relu, bias=hid_b[:, l, col:col + 1],
                                 scale=hid_s[:, l, col:col + 1]).then_inc(s_hid_free, 1)
            act.wait_ge(s_hid_free, n + 3)
            nc.scalar.activation(hid_hi[l][:, m, :], hid[:, m, :], ACT.Copy).then_inc(s_hid_hi, 1)

        def expert(k, e, between):
            for m in range(HALF):
                hidden_half(k, 4 * e + 2 + m, 1, e, m)
            between()
            if e + 1 < NE:
                for m in range(HALF):
                    hidden_half(k, 4 * (e + 1) + m, 0, e + 1, m)

        def node_layer1(j):
            first_residual(j)
            root(j + 1)
            norm(0, j)
            second_table(j)

        node_layer1(0)
        with act.Fori(1, BLOCKS) as j:
            node_layer1(j)
        root(BLOCKS + 1)
        norm(1, 0)
        root(BLOCKS + 2)
        norm_x1(0, 0)
        hnT_high(0, 0)

        def experts(k, par, node):
            exponentials(k)
            for m in range(HALF):
                hidden_half(k, m, 0, 0, m)
            gates_T(k)
            for e in range(NE):
                def between():
                    if node and e == STEP_S + 1:
                        root(BLOCKS + 2 * (k + 1) + 1)
                    if node and e == STEP_R + 1:
                        norm(1, k + 1)
                    if node and e == STEP_S2 + 1:
                        root(BLOCKS + 2 * (k + 1) + 2)
                    if node and e == STEP_S2 + 2:
                        norm_x1(k + 1, 1 - par)
                        hnT_high(k + 1, 1 - par)

                expert(k, e, between)

        act.wait_ge(s_par, 1)
        with act.Fori(0, (BLOCKS - 1) // 2) as kk:
            for par in range(2):
                experts(2 * kk + par, par, True)
        experts(BLOCKS - 1, 0, False)

    @block.tensor
    def _(pe):
        pe.sem_inc(s_used, GROUPS)
        pe.wait_ge(s_pool, 10)
        pe.wait_ge(s_prep, 1)
        for c in range(LCH):
            nc.tensor.transpose(psH[:, 0, c * LROWS:(c + 1) * LROWS], ldst[:, LROW + c * CHUNK:LROW + (c + 1) * CHUNK],
                                ident[0:LROWS, 0:LROWS]).then_inc(s_prep_pe, 1)
        pe.wait_ge(s_prep, 2)
        nc.tensor.matmul(psN[:, 0, 0:4 * LROWS], ones_m, diag, start=True, stop=True).then_inc(s_prep_pe, 1)
        pe.wait_ge(s_prep, 3)
        for c in range(LCH):
            nc.tensor.transpose(psY[:, 0, c * LROWS:(c + 1) * LROWS], lew[:, LROW + c * CHUNK:LROW + (c + 1) * CHUNK],
                                ident[0:LROWS, 0:LROWS]).then_inc(s_prep_pe, 1)
        pe.wait_ge(s_prep, 4)
        for c in range(LCH):
            nc.tensor.transpose(psH[:, 1, c * LROWS:(c + 1) * LROWS], lsrc[:, LROW + c * CHUNK:LROW + (c + 1) * CHUNK],
                                ident[0:LROWS, 0:LROWS]).then_inc(s_prep_pe, 1)
        pe.wait_ge(s_par_in, 16 * 10)
        rows80 = 5 * NE * HALF
        for l in range(2):
            nc.tensor.transpose(psY[:, 1, l * rows80:(l + 1) * rows80], par_st[:, l, :],
                                ident[0:rows80, 0:rows80]).then_inc(s_prep_pe, 1)

        extra, lead = control(pe)

        places = []

        def window_regs(pb, h, first, last):
            places.append(None)
            regs = [pe.alloc_register(f"win{len(places)}_{n}") for n in range(first, last)]
            pe.load(regs, meta[0:1, ds(pb * (2 * META) + h * META + first, last - first)])
            return regs, [pe.snap(r, min_val=0, max_val=STRETCH - WIN) for r in regs]

        def degree_pair(g, pb):
            for h in range(2):
                m = 2 * g + h
                pe.wait_ge(s_deg_free, m + 1)
                nc.tensor.matmul(psA[0:3, h, 0:STRETCH], zeros_b[:, 0:3], zeros_b[:, :], start=True, stop=True)
                regs, offs = window_regs(pb, h, 0, GROUPS)
                pe.wait_ge(s_deg_oh, 2 * m + 2)
                for s in range(MC):
                    last = nc.tensor.matmul(psA[0:3, h, ds(offs[s // GROUP], WIN)], ew_st[:, h, s, :],
                                            onehot_b[:, h, s, :], start=False, stop=True, skip_group_check=True)
                last.then_inc(s_deg_mm, 1)
                for r in regs:
                    pe.free_register(r)

        extra_passes(pe, extra, 0, degree_pair)
        with pe.Fori(0, PAIRS) as i:
            degree_pair(extra * PAIRS + i, PAIRS - 1 - i)
        pe.wait_ge(s_degrow, 1)
        for t in range(TILES):
            last = nc.tensor.matmul(psN[0:TILE, 1, t:t + 1], degrow[:, t * TILE:(t + 1) * TILE], ones1[0:3, :],
                                    start=True, stop=True)
        last.then_inc(s_degT, 1)

        def macro(g, pb, h, part):
            m = 2 * g + h
            first, last = ((0, SPLIT), (SPLIT, GROUPS))[part]
            if part == 0:
                pe.wait_ge(s_agg_free, m + 1)
                for f in range(HALF):
                    nc.tensor.matmul(psA[:, f, 0:STRETCH], zeros_b[:, 0:128], zeros_b[:, :], start=True, stop=True)
            regs, offs = window_regs(pb, h, first, last)
            if part == 0:
                pe.wait_ge(s_oh, m + 1)
            for s in range(first * GROUP, last * GROUP):
                pe.wait_ge(s_gath[s], (m + 1) * 16)
                for f in range(HALF):
                    ins = nc.tensor.matmul(psA[:, f, ds(offs[s // GROUP - first], WIN)], ring[:, s, f * 128:(f + 1) * 128],
                                           onehot[:, h, s, :], start=False, stop=True, skip_group_check=True)
                if s % GROUP == GROUP - 1:
                    ins.then_inc(s_used, 1)
            for r in regs:
                pe.free_register(r)

        def pair(g, pb):
            for h in range(2):
                for part in range(2):
                    macro(g, pb, h, part)

        def node_A(layer, j, first=False):
            n = layer * BLOCKS + j
            pe.wait_ge(s_g_in, (n + 1) * 16)
            if layer == 0:
                if not first:
                    pe.wait_ge(s_conv_ev, n)
            elif first:
                pe.wait_ge(s_conv_ev, n)
            else:
                pe.wait_ge(s_acc0, j)
            for f in range(HALF):
                for t in range(BT):
                    last = nc.tensor.transpose(psN[:, f, t * TILE:(t + 1) * TILE],
                                               g_blk[0:TILE, t, f * 128:(f + 1) * 128], ident[0:TILE, 0:TILE])
            last.then_inc(s_gT, 1)

        def node_B(layer, j):
            pe.wait_ge(s_gvec_in, 64 * (layer + 1))
            pe.wait_ge(s_aggst, layer * BLOCKS + j + 1)
            for t in range(BT):
                for f in range(HALF):
                    last = nc.tensor.matmul(psN[0:TILE, t // 2, (t % 2) * D:(t % 2 + 1) * D],
                                            aggst[:, f, t * TILE:(t + 1) * TILE], gW_sb[:, f, :],
                                            start=(f == 0), stop=(f == HALF - 1))
            last.then_inc(s_conv, 1)

        def node_D(j):
            pe.wait_ge(s_hn, (j + 1) * BT)
            for f in range(HALF):
                for t in range(BT):
                    last = nc.tensor.transpose(psN[:, f, t * TILE:(t + 1) * TILE],
                                               hc[0:TILE, t, f * 128:(f + 1) * 128], ident[0:TILE, 0:TILE])
            last.then_inc(s_hnT, 1)

        def three(ps, hi, lo, whi, wlo, weights_stationary, start, stop):
            for i, (a, w) in enumerate(((hi, whi), (hi, wlo), (lo, whi))):
                lhsT, rhs = (w, a) if weights_stationary else (a, w)
                last = nc.tensor.matmul(ps, lhsT, rhs, start=start and i == 0, stop=stop and i == 2)
            return last

        def node_E(j, par):
            pe.wait_ge(s_hnT_lo, j + 1)
            for t in range(BT):
                ts = slice(t * TILE, (t + 1) * TILE)
                for f in range(HALF):
                    last = three(psN[0:TILE, 0, t * NE:(t + 1) * NE], hnT_hi[par][:, f, ts], hnT_lo[par][:, f, ts],
                                 wr_hi[:, f, :], wr_lo[:, f, :], False, f == 0, f == HALF - 1)
            last.then_inc(s_logit, 1)

        def node_F(j, par):
            pe.wait_ge(s_gate, j + 1)
            for t in range(BT):
                last = nc.tensor.transpose(psN[0:NE, 1, t * TILE:(t + 1) * TILE], gate[par][:, t, :], ident[0:TILE, 0:TILE])
            last.then_inc(s_gateT, 1)

        def node_G(j):
            pe.wait_ge(s_gateT_sb, j + 1)
            for t in range(BT):
                last = nc.tensor.matmul(psN[0:TILE, t // 2, (t % 2) * D:(t % 2 + 1) * D],
                                        gateT[:, t * TILE:(t + 1) * TILE], bo_sb[:, :], start=True, stop=True)
            last.then_inc(s_gbo, 1)

        def hidden(k, idx, l, e, m):
            n = k * HALVES + idx
            pe.wait_ge(s_hid_free, n + 1)
            src_hi, src_lo = (hnT_hi[k_par[0]], hnT_lo[k_par[0]]) if l == 0 else (hid_hi[0], hid_lo[0])
            ms = slice(m * 128, (m + 1) * 128)
            for f in range(HALF):
                last = three(psH[:, m, 0:BLOCK], src_hi[:, f, :], src_lo[:, f, :], w_hi[l][:, e, f, ms],
                             w_lo[l][:, e, f, ms], True, f == 0, f == HALF - 1)
            last.then_inc(s_hid, 1)

        k_par = [0]

        def experts_start(k, par):
            k_par[0] = par
            pe.wait_ge(s_hnT_lo, k + 1)
            for m in range(HALF):
                hidden(k, m, 0, 0, m)

        def expert(k, e, between):
            pe.wait_ge(s_hid_lo, k * HALVES + 4 * e + 2 + 2)
            for m in range(HALF):
                hidden(k, 4 * e + 2 + m, 1, e, m)
            if e + 1 < NE:
                for m in range(HALF):
                    hidden(k, 4 * (e + 1) + m, 0, e + 1, m)
            between()
            pe.wait_ge(s_hid_lo, k * HALVES + 4 * e + 4 + 2)
            for u in range(2):
                n = (k * NE + e) * 2 + u
                pe.wait_ge(s_y_free, n + 1)
                for t in (2 * u, 2 * u + 1):
                    ts = slice(t * TILE, (t + 1) * TILE)
                    for f in range(HALF):
                        last = three(psY[0:TILE, u, (t % 2) * D:(t % 2 + 1) * D], hid_hi[1][:, f, ts],
                                     hid_lo[1][:, f, ts], w_hi[2][:, e, f, :], w_lo[2][:, e, f, :], False,
                                     f == 0, f == HALF - 1)
                last.then_inc(s_y, 1)

        for layer in range(2):
            first = extra * (PAIRS * (layer + 1)) + PAIRS * layer
            extra_passes(pe, extra, extra * (PAIRS * layer) + PAIRS * layer, pair)
            with pe.Fori(0, lead) as i:
                pair(first + i, PAIRS - 1 - i)

            def part_of(j, a, h, part, first=first):
                with pe.If(lead + 2 * j + a < PAIRS):
                    macro(first + lead + 2 * j + a, within(PAIRS - 1 - lead - 2 * j - a, 0, PAIRS - 1 - LEAD_MIN), h, part)

            if layer == 0:
                def node(j, first=False, edges=True):
                    node_A(0, j, first)
                    if edges:
                        for part in range(2):
                            part_of(j, 0, 0, part)
                    node_B(0, j)
                    if edges:
                        for a, h in ((0, 1), (1, 0), (1, 1)):
                            for part in range(2):
                                part_of(j, a, h, part)

                node(0, first=True)
                with pe.Fori(1, BLOCKS - 1) as j:
                    node(j)
                node(BLOCKS - 1, edges=False)
            else:
                node_A(1, 0, first=True)
                for part in range(2):
                    part_of(0, 0, 0, part)
                node_B(1, 0)
                for a, h in ((0, 1), (1, 0), (1, 1)):
                    for part in range(2):
                        part_of(0, a, h, part)
                pe.wait_ge(s_w_lo, PIECES)
                pe.wait_ge(s_wr_lo, 1)
                node_D(0)
                node_E(0, 0)

                def experts(k, par, node):
                    experts_start(k, par)
                    if node:
                        part_of(k + 1, 0, 0, 0)
                    node_F(k, par)
                    for e in range(NE):
                        def between():
                            if node and e > 0:
                                part_of(k + 1, e // 4, (e // 2) % 2, e % 2)
                            if e == 0:
                                node_G(k)
                            if node and e == STEP_B:
                                node_B(1, k + 1)
                            if node and e == NE - 1:
                                node_D(k + 1)

                        expert(k, e, between)
                        if node and e == 0:
                            node_A(1, k + 1)
                        if node and e == NE - 1:
                            node_E(k + 1, 1 - par)

                with pe.Fori(0, (BLOCKS - 1) // 2) as kk:
                    for par in range(2):
                        experts(2 * kk + par, par, True)
                experts(BLOCKS - 1, 0, False)

    @block.vector
    def _(dve):
        v = nc.vector
        dve.sem_inc(s_deg_free, 2)
        dve.sem_inc(s_agg_free, 1)
        dve.sem_inc(s_hid_lo, 2)
        dve.sem_inc(s_y_free, 2)
        count = [0]

        def pre(ins):
            count[0] += 1
            ins.then_inc(s_pre, 1)
            dve.wait_ge(s_pre, count[0])

        def rsqrt(step, y, var, eps, t):
            step(v.reciprocal(y, y))
            step(v.scalar_tensor_tensor(t, var, eps, y, ALU.add, ALU.mult))
            step(v.scalar_tensor_tensor(t, t, -0.5, y, ALU.mult, ALU.mult))
            step(v.tensor_scalar(t, t, -0.75, 1.5, ALU.max, ALU.add))
            step(v.tensor_tensor(y, y, t, ALU.mult))

        dve.wait_ge(s_dst_in, 48)
        dstf = ldst[:, LROW:2 * LROW]
        pre(v.tensor_copy(dstf, ldst[:, 0:LROW].bitcast(I32)))
        dve.sem_inc(s_prep, 1)
        groups = dstf.rearrange("p (h n) -> p h n", h=GROUP)
        pre(v.tensor_reduce(gext[:, 0, :], groups, AX.X, ALU.min))
        inside = ldst[:, 0:LROW]
        pre(v.scalar_tensor_tensor(inside, dstf, NOWHERE - 1, dstf, ALU.is_lt, ALU.mult))
        pre(v.tensor_reduce(gext[:, 1, :], inside.rearrange("p (h n) -> p h n", h=GROUP), AX.X, ALU.max))
        dve.wait_ge(s_pool, 10)
        for q in range(2):
            for h in range(2):
                pre(v.tensor_scalar(diag[:, (2 * q + h) * LROWS:(2 * q + h + 1) * LROWS], ident[0:LROWS, 0:LROWS],
                                    gext[:, q, h:h + 1], None, ALU.mult))
        dve.sem_inc(s_prep, 1)
        dve.wait_ge(s_ew_in, 48)
        ewf = lew[:, LROW:2 * LROW]
        pre(v.scalar_tensor_tensor(ewf, lew[:, 0:LROW], -1.0, lew[:, 0:LROW], ALU.mult, ALU.max))
        pre(v.scalar_tensor_tensor(ewf, ewf, FINITE_MAX, ewf, ALU.is_le, ALU.mult))
        pre(v.tensor_scalar(ewf, ewf, EDGE_MIN, None, ALU.max))
        pre(v.scalar_tensor_tensor(ewf, dstf, NOWHERE - 1, ewf, ALU.is_lt, ALU.mult))
        dve.sem_inc(s_prep, 1)
        dve.wait_ge(s_src_in, 48)
        pre(v.tensor_copy(lsrc[:, LROW:2 * LROW], lsrc[:, 0:LROW].bitcast(I32)))
        dve.sem_inc(s_prep, 1)
        def num(n):
            return room[:, n * NG:(n + 1) * NG]

        gmin, gmax, off, blk, pairf = (num(n) for n in range(5))
        dve.wait_ge(s_prep_pe, LCH + 1)
        for q, t in ((0, gmin), (1, gmax)):
            pre(v.tensor_copy(t.rearrange("p (n h) -> p h n", h=2),
                              psN[:, 0, q * 2 * LROWS:(q + 1) * 2 * LROWS].rearrange("p (h n) -> p h n", h=2)))
        mmin = small[:, 0:2 * PAIRS]
        pre(v.tensor_reduce(mmin, gmin.rearrange("p (m g) -> p m g", g=GROUPS), AX.X, ALU.min))
        pre(v.tensor_tensor(off.rearrange("p (m g) -> p m g", g=GROUPS), gmin.rearrange("p (m g) -> p m g", g=GROUPS),
                            mmin.unsqueeze(2).broadcast_to([128, 2 * PAIRS, GROUPS]), ALU.subtract))
        pre(v.tensor_reduce(scal[:, 0:1], off, AX.X, ALU.max))
        pre(v.tensor_tensor(blk, gmax, gmin, ALU.subtract))
        pre(v.tensor_reduce(scal[:, 1:2], blk, AX.X, ALU.max))
        pre(v.tensor_scalar(scal[:, 2:3], scal[:, 0:1], float(STRETCH - WIN), None, ALU.is_le))
        pre(v.scalar_tensor_tensor(scal[:, 2:3], scal[:, 1:2], float(WIN - 1), scal[:, 2:3], ALU.is_le, ALU.mult))
        pre(v.tensor_scalar(scal[:, 3:4], scal[:, 2:3], -float(PASSES - 1), float(PASSES - 1), ALU.mult, ALU.add))
        pre(v.tensor_scalar(blk, gmax, float(BLOCK), None, ALU.is_ge))
        for b in range(2, BLOCKS):
            pre(v.scalar_tensor_tensor(blk, gmax, float(b * BLOCK), blk, ALU.is_ge, ALU.add))
        pre(v.tensor_scalar(blk, blk, 2.0, float(LEAD_MIN), ALU.mult, ALU.add))
        pre(v.tensor_copy(pairf, pair_i))
        pre(v.scalar_tensor_tensor(blk, blk, float(PAIRS), pairf, ALU.min, ALU.subtract))
        pre(v.tensor_reduce(scal[:, 4:5], blk, AX.X, ALU.max))
        pre(v.tensor_copy(ctrl[0:1, 0:2], scal[0:1, 3:5]))
        pre(v.tensor_scalar(gmin, gmin, scal[:, 2:3], None, ALU.mult))
        pre(v.tensor_scalar(off, off, scal[:, 2:3], None, ALU.mult))
        pre(v.tensor_scalar(place[:, :], mmin, scal[:, 2:3], None, ALU.mult))
        metav = meta[:, :].rearrange("p (m w) -> p m w", w=META)
        pre(v.tensor_copy(metav[0:1, :, 0:GROUPS], off[32:33, :].rearrange("p (m g) -> p m g", g=GROUPS)))
        pre(v.tensor_copy(metav[0:1, :, GROUPS], place[32:33, :]))
        pre(v.tensor_tensor(rel[:, :].rearrange("p (n a b) -> p n a b", a=2, b=2),
                            psH[:, 0, 0:CHUNKS].rearrange("p (a b n) -> p n a b", a=2, b=2),
                            gmin.rearrange("p (n a) -> p n a", a=2).unsqueeze(3).broadcast_to([128, LROWS, 2, 2]),
                            ALU.subtract))
        dve.wait_ge(s_prep_pe, 2 * LCH + 1)
        pre(v.tensor_copy(ew[:, :].rearrange("p (n c) -> p n c", c=LCH),
                          psY[:, 0, 0:CHUNKS].rearrange("p (c n) -> p n c", c=LCH)))
        rest = room[:, 0:CHUNKS]
        pre(v.tensor_copy(ew3[:, :, 0], ew[:, :]))
        pre(v.tensor_tensor(rest, ew[:, :], ew3[:, :, 0], ALU.subtract))
        pre(v.tensor_copy(ew3[:, :, 1], rest))
        pre(v.tensor_tensor(ew3[:, :, 2], rest, ew3[:, :, 1], ALU.subtract))
        pre(v.tensor_copy(iota[:, :], iota_i[:, :]))
        dve.sem_inc(s_meta, 1)
        pre(v.memset(degrow, 0.0))
        dve.wait_ge(s_prep_pe, 3 * LCH + 1)
        v.tensor_copy(srcs[:, :].rearrange("p (n c) -> p n c", c=LCH),
                      psH[:, 1, 0:CHUNKS].rearrange("p (c n) -> p n c", c=LCH)).then_inc(s_srcs, 1)
        extra, lead = control(dve)

        def columns(pb, h):
            return ds(pb * (2 * MC) + h * MC, MC)

        def over_window(t):
            return t.unsqueeze(2).broadcast_to([128, MC, WIN])

        iota_bc = iota[:, :].unsqueeze(1).broadcast_to([128, MC, WIN])

        def stretch_place(pb, h):
            return dve.value_load(meta[0:1, ds(pb * (2 * META) + h * META + GROUPS, 1)], min_val=0, max_val=NP)

        def degree_onehots(pb, h):
            v.tensor_tensor(onehot_b[:, h, :, :], iota_bc, over_window(rel[:, columns(pb, h)]),
                            ALU.is_equal).then_inc(s_deg_oh, 1)
            v.tensor_copy(ew_st[:, h, :, :], ew3[:, columns(pb, h), :]).then_inc(s_deg_oh, 1)

        def degree_take(g, pb, h):
            m = 2 * g + h
            part = degrow[:, ds(stretch_place(pb, h), STRETCH)]
            dve.wait_ge(s_deg_mm, m + 1)
            v.tensor_tensor(part, part, psA[0:3, h, 0:STRETCH], ALU.add).then_inc(s_deg_free, 1)
            dve.wait_ge(s_deg_free, m + 3)
            carry(dve)

        def degree_pair(g, pb):
            degree_onehots(pb, 0)
            degree_onehots(pb, 1)
            degree_take(g, pb, 0)
            degree_take(g, pb, 1)

        def advance(nth):
            def after(p):
                v.tensor_scalar(rel[:, :], rel[:, :], -float(WIN), None, ALU.add).then_inc(s_adv, 1)
                v.tensor_scalar(place[:, :], place[:, :], float(WIN), None, ALU.add).then_inc(s_adv, 1)
                dve.wait_ge(s_adv, p * 3 + nth * ADVANCES + 2)
                v.tensor_copy(metav[0:1, :, GROUPS], place[32:33, :]).then_inc(s_adv, 1)
                dve.wait_ge(s_adv, p * 3 + nth * ADVANCES + 3)
                carry(dve)
            return after

        def rewind(nth):
            at = nth * ADVANCES + 3 * (PASSES - 1)
            with dve.If(extra > 0):
                v.tensor_scalar(rel[:, :], rel[:, :], float(WIN * (PASSES - 1)), None, ALU.add).then_inc(s_adv, 1)
                v.tensor_scalar(place[:, :], place[:, :], -float(WIN * (PASSES - 1)), None, ALU.add).then_inc(s_adv, 1)
                dve.wait_ge(s_adv, at + 2)
                v.tensor_copy(metav[0:1, :, GROUPS], place[32:33, :]).then_inc(s_adv, 1)
                dve.wait_ge(s_adv, at + 3)
            dve.nop()

        extra_passes(dve, extra, 0, degree_pair, advance(0))
        degree_onehots(PAIRS - 1, 0)
        with dve.Fori(0, PAIRS - 1) as i:
            g = extra * PAIRS + i
            degree_onehots(PAIRS - 1 - i, 1)
            degree_take(g, PAIRS - 1 - i, 0)
            degree_onehots(PAIRS - 2 - i, 0)
            degree_take(g, PAIRS - 1 - i, 1)
        degree_onehots(0, 1)
        degree_take(extra * PAIRS + PAIRS - 1, 0, 0)
        degree_take(extra * PAIRS + PAIRS - 1, 0, 1)
        dve.sem_inc(s_degrow, 1)
        rewind(0)
        for b in range(BLOCKS):
            dve.wait_ge(s_x_in[b], 16 if b < BLOCKS - 1 else 32)
            for t in range(BT):
                last = v.bn_stats(stats[:, t, :], x_all[:, b * BT + t, :])
            pre(last)
            for t in range(BT):
                last = v.bn_aggr(mv[:, b * BT + t, :], stats[:, t, :])
            pre(last)
            pre(v.tensor_scalar(x_all[:, b * BT:(b + 1) * BT, :], x_all[:, b * BT:(b + 1) * BT, :],
                                -FINITE_MAX, FINITE_MAX, ALU.max, ALU.min))
        dve.sem_inc(s_var_x, 1)
        dve.wait_ge(s_degT, 1)
        dve.wait_ge(s_sqrt_deg, 1)
        rsqrt(pre, dis[:, :], psN[0:TILE, 1, 0:TILES], 1.0, newton[:, :])
        dve.wait_ge(s_sqrt_x, 1)
        rsqrt(pre, rstd[:, :], mv[:, :, 1], LN_EPS, newton[:, :])
        pre(v.scalar_tensor_tensor(nmr[:, :], mv[:, :, 0], -1.0, rstd[:, :], ALU.mult, ALU.mult))
        pre(v.tensor_scalar(odd[:, :], nmr[:, :], 0.0, 0.0, ALU.mult, ALU.not_equal))
        nil = zero1[0:TILE, :].broadcast_to([TILE, TILES])
        pre(v.copy_predicated(rstd[:, :], odd[:, :], nil))
        pre(v.copy_predicated(nmr[:, :], odd[:, :], nil))
        pre(v.tensor_tensor(drow[:, 0, :], rstd[:, :], dis[:, :], ALU.mult))
        pre(v.tensor_tensor(drow[:, 1, :], nmr[:, :], dis[:, :], ALU.mult))
        dve.sem_inc(s_dis, 1)
        for t in range(1, TILES, 2):
            v.tensor_scalar(x_all[:, t, :], x_all[:, t, :], drow[:, 0, t:t + 1], drow[:, 1, t:t + 1],
                            ALU.mult, ALU.add).then_inc(s_g1_odd, 1)
        dve.wait_ge(s_prep_pe, 3 * LCH + 3)
        pre(v.tensor_copy(par_T, psY[:, 1, 0:10 * NE * HALF].rearrange("p (l i c) -> p l i c", l=2, i=5)))
        b_, g_, be_, m_, v_ = (par_T[:, :, i, :] for i in range(5))
        dve.sem_inc(s_var_par, 1)
        dve.wait_ge(s_sqrt_par, 1)
        rsqrt(pre, hid_s[:, :, :], v_, BN_EPS, hid_b[:, :, :])
        pre(v.tensor_tensor(hid_s[:, :, :], hid_s[:, :, :], g_, ALU.mult))
        pre(v.tensor_tensor(hid_b[:, :, :], b_, m_, ALU.subtract))
        pre(v.tensor_tensor(hid_b[:, :, :], hid_b[:, :, :], hid_s[:, :, :], ALU.mult))
        v.tensor_tensor(hid_b[:, :, :], hid_b[:, :, :], be_, ALU.add).then_inc(s_par, 1)
        dve.wait_ge(s_g1_out, 16 * BLOCKS)
        pre(v.memset(aggT[:, :, :], 0.0))

        def onehots(g, pb, h):
            m = 2 * g + h
            v.tensor_tensor(onehot[:, h, :, :], iota_bc, over_window(rel[:, columns(pb, h)]),
                            ALU.is_equal).then_inc(s_ohc, 1)
            dve.wait_ge(s_ohc, m + 1)
            v.tensor_tensor(onehot[:, h, :, :], onehot[:, h, :, :], over_window(ew[:, columns(pb, h)]),
                            ALU.mult).then_inc(s_oh, 1)

        def take(g, pb, h):
            m = 2 * g + h
            part = aggT[:, :, ds(stretch_place(pb, h), STRETCH)]
            dve.wait_ge(s_used, (m + 1) * GROUPS + GROUPS)
            v.tensor_tensor(part, part, psA[:, :, 0:STRETCH], ALU.add).then_inc(s_agg_free, 1)
            dve.wait_ge(s_agg_free, m + 2)
            carry(dve)

        def pair(g, pb):
            onehots(g, pb, 0)
            onehots(g, pb, 1)
            take(g, pb, 0)
            take(g, pb, 1)

        steps = {0: (s_ch1, CHAIN1), 1: (s_ch2, CHAIN2)}
        place_in = [0]

        def chain(layer, j, ins):
            s, per = steps[layer]
            place_in[0] += 1
            ins.then_inc(s, 1)
            dve.wait_ge(s, j * per + place_in[0])

        def block_stats(layer, j, src_t):
            for t in range(BT):
                last = v.bn_stats(stats[:, t, :], src_t[0:TILE, t, :])
            chain(layer, j, last)
            carry(dve)
            for t in range(BT):
                last = v.bn_aggr(bmv[:, t, :], stats[:, t, :])
            last.then_inc(s_var, 1)

        def block_rstd(layer, j, done, nth):
            dve.wait_ge(s_sqrt, nth)
            rsqrt(lambda ins: chain(layer, j, ins), brstd[:, :], bmv[:, :, 1], LN_EPS, newton[:, 0:BT])
            v.scalar_tensor_tensor(bnmr[:, :], bmv[:, :, 0], -1.0, brstd[:, :], ALU.mult, ALU.mult).then_inc(done, 1)

        def node_A(layer, j):
            n = layer * BLOCKS + j
            place_in[0] = 0
            own = aggT[:, :, ds((BLOCKS - 1 - j) * BLOCK, BLOCK)]
            dve.wait_ge(s_gT, n + 1)
            carry(dve)
            v.tensor_tensor(aggst[:, :, :], own, psN[:, :, 0:BLOCK], ALU.add).then_inc(s_aggst, 1)
            if layer == 0:
                dve.wait_ge(s_aggst, n + 1)
                carry(dve)
                chain(layer, j, v.tensor_tensor(own.bitcast(I32), own.bitcast(I32), own.bitcast(I32), ALU.bitwise_xor))

        def node_B(layer, j, first=False):
            n = layer * BLOCKS + j
            dve.wait_ge(s_conv, n + 1)
            if layer == 0 and not first:
                dve.wait_ge(s_h_out, 16 * j)
            if layer == 1 and first:
                dve.wait_ge(s_h_out, 16 * BLOCKS)
            for t in range(BT):
                last = v.scalar_tensor_tensor(hc[0:TILE, t, :], psN[0:TILE, t // 2, (t % 2) * D:(t % 2 + 1) * D],
                                              dis[:, ds((BLOCKS - 1 - j) * BT + t, 1)], gvec[:, 0, :],
                                              ALU.mult, ALU.add)
            last.then_inc(s_conv_ev, 1)
            dve.wait_ge(s_conv_ev, n + 1)
            hcf = hc[0:TILE, :, :].rearrange("p t d -> p (t d)")
            chain(layer, j, v.tensor_scalar(bad[:, :], hcf, 0.0, 0.0, ALU.mult, ALU.not_equal))
            carry(dve)
            chain(layer, j, v.copy_predicated(hcf, bad[:, :], zero1[0:TILE, :].broadcast_to([TILE, BT * D])))

        def node_S(layer, j):
            block_stats(layer, j, hc)

        def node_R(layer, j):
            block_rstd(layer, j, s_stat, j + 1 if layer == 0 else BLOCKS + 2 * j + 1)

        def node_H(j):
            dve.wait_ge(s_hres_in, (j + 1) * 16)
            if isinstance(j, int):
                dve.wait_ge(s_x_last, 32)
            v.tensor_scalar(h_res[0:TILE, :, :], h_res[0:TILE, :, :], -FINITE_MAX, FINITE_MAX,
                            ALU.max, ALU.min).then_inc(s_clean, 1)

        def node_C(layer, j):
            n = layer * BLOCKS + j
            h = hc[0:TILE, :, :]

            def bc(i):
                return gvec[:, i, :].unsqueeze(1).broadcast_to([TILE, BT, D])

            dve.wait_ge(s_norm, (n + 1) * BT)
            chain(layer, j, v.tensor_tensor(h, h, bc(1), ALU.mult))
            chain(layer, j, v.tensor_tensor(h, h, bc(2), ALU.add))
            chain(layer, j, v.scalar_tensor_tensor(h, h, FINITE_MAX, h, ALU.is_le, ALU.mult))
            if layer == 0:
                dve.wait_ge(s_h0, (j + 1) * BT)
            else:
                dve.wait_ge(s_hres_in, (n + 1) * 16)
            v.scalar_tensor_tensor(h, h, 0.0, h_res[0:TILE, :, :], ALU.max, ALU.add).then_inc(s_h, 1)

        def node_X(j, par, arrived, last=False):
            h = hc[0:TILE, :, :]
            dve.wait_ge(s_h, BLOCKS + j + 1)
            keep = h_res[0:TILE, :, :].bitcast(I32)
            hi32 = h.bitcast(I32)
            chain(1, j, v.tensor_scalar(keep, h, FINITE_MAX, -1.0, ALU.is_le, ALU.mult))
            chain(1, j, v.tensor_tensor(hi32, hi32, keep, ALU.bitwise_and))
            dve.wait_ge(s_x_blk[par], arrived)
            if last:
                dve.wait_ge(s_x_last, 64)
            a = acc[par][0:TILE, :, :]
            chain(1, j, v.tensor_tensor(a, a, h, ALU.add))

        def node_S2(j, par):
            block_stats(1, j, acc[par])

        def node_R2(j):
            block_rstd(1, j, s_stat2, BLOCKS + 2 * j + 2)

        def node_D(j, par):
            dve.wait_ge(s_hnT_hi, j + 1)
            v.tensor_tensor(hnT_lo[par][:, :, :], psN[:, :, 0:BLOCK], hnT_hi[par][:, :, :].bitcast(F32),
                            ALU.subtract).then_inc(s_hnT_lo, 1)

        def node_E(j):
            dve.wait_ge(s_logit, j + 1)
            chain(1, j, v.tensor_tensor(logit[:, :, :], psN[0:TILE, 0, 0:BT * NE].rearrange("p (t e) -> p t e", e=NE),
                                        br_bc[:, :].unsqueeze(1).broadcast_to([TILE, BT, NE]), ALU.add))
            chain(1, j, v.tensor_reduce(lmax[:, :], logit[:, :, :], AX.X, ALU.max))
            v.tensor_tensor(logit[:, :, :], logit[:, :, :], lmax[:, :].unsqueeze(2).broadcast_to([TILE, BT, NE]),
                            ALU.subtract).then_inc(s_lsub, 1)

        def node_F(j, par):
            dve.wait_ge(s_exp, j + 1)
            chain(1, j, v.tensor_reduce(lsum[:, :], logit[:, :, :], AX.X, ALU.add))
            chain(1, j, v.reciprocal(lsum[:, :], lsum[:, :]))
            v.tensor_tensor(gate[par][:, :, :], logit[:, :, :], lsum[:, :].unsqueeze(2).broadcast_to([TILE, BT, NE]),
                            ALU.mult).then_inc(s_gate, 1)

        def node_G(j, par):
            dve.wait_ge(s_gbo, j + 1)
            a = acc[par][0:TILE, :, :].rearrange("p (u t) d -> p u (t d)", u=2)
            v.tensor_tensor(a, a, psN[0:TILE, :, :], ALU.add).then_inc(s_acc0, 1)

        def low_half(k, idx, l, m):
            n = k * HALVES + idx
            dve.wait_ge(s_hid_hi, n + 1)
            v.tensor_tensor(hid_lo[l][:, m, :], hid[:, m, :], hid_hi[l][:, m, :].bitcast(F32),
                            ALU.subtract).then_inc(s_hid_lo, 1)

        def expert(k, e, par, between):
            for m in range(HALF):
                low_half(k, 4 * e + 2 + m, 1, m)
            if e + 1 < NE:
                for m in range(HALF):
                    low_half(k, 4 * (e + 1) + m, 0, m)
            between()
            for u in range(2):
                n = (k * NE + e) * 2 + u
                if e == 0:
                    dve.wait_ge(s_acc0, k + 1)
                else:
                    dve.wait_ge(s_y_free, n - 2 + 1 + 2)
                dve.wait_ge(s_y, n + 1)
                for t in (2 * u, 2 * u + 1):
                    last = v.scalar_tensor_tensor(acc[par][0:TILE, t, :], psY[0:TILE, u, (t % 2) * D:(t % 2 + 1) * D],
                                                  gate[par][:, t, e:e + 1], acc[par][0:TILE, t, :], ALU.mult, ALU.add)
                last.then_inc(s_y_free, 1)

        for layer in range(2):
            first = extra * (PAIRS * (layer + 1)) + PAIRS * layer
            extra_passes(dve, extra, extra * (PAIRS * layer) + PAIRS * layer, pair, advance(layer + 1))
            onehots(first, PAIRS - 1, 0)
            with dve.Fori(0, lead) as i:
                g = first + i
                onehots(g, PAIRS - 1 - i, 1)
                take(g, PAIRS - 1 - i, 0)
                with dve.If(i + 1 < PAIRS):
                    onehots(g + 1, within(PAIRS - 2 - i, 0, PAIRS - 2), 0)
                take(g, PAIRS - 1 - i, 1)

            def ahead(j, a, h):
                with dve.If(lead + 2 * j + a < PAIRS):
                    onehots(first + lead + 2 * j + a, within(PAIRS - 1 - lead - 2 * j - a, 0, PAIRS - 1 - LEAD_MIN), h)

            def took(j, a, h):
                with dve.If(lead + 2 * j + a < PAIRS):
                    take(first + lead + 2 * j + a, within(PAIRS - 1 - lead - 2 * j - a, 0, PAIRS - 1 - LEAD_MIN), h)

            def node_beside_edges(j, first=False, edges=True):
                ifs = (lambda f, *a: f(j, *a)) if edges else (lambda f, *a: None)
                node_A(layer, j)
                ifs(ahead, 0, 1)
                ifs(took, 0, 0)
                if first:
                    dve.wait_ge(s_gvec_in, 64 * (layer + 1))
                node_B(layer, j, first=first)
                ifs(ahead, 1, 0)
                node_S(layer, j)
                ifs(took, 0, 1)
                if layer == 0:
                    node_H(j)
                node_R(layer, j)
                ifs(ahead, 1, 1)
                ifs(took, 1, 0)
                node_C(layer, j)
                ifs(ahead, 2, 0)

            if layer == 0:
                node_beside_edges(0, first=True)
                took(0, 1, 1)
                with dve.Fori(1, BLOCKS - 1) as j:
                    node_beside_edges(j)
                    took(j, 1, 1)
                    dve.nop()
                node_beside_edges(BLOCKS - 1, edges=False)
                rewind(1)
            else:
                node_beside_edges(0, first=True)
                node_X(0, 0, 16, last=True)
                node_S2(0, 0)
                took(0, 1, 1)
                node_R2(0)
                node_D(0, 0)
                node_E(0)

                def experts(k, par, node, arrived=0):
                    node_F(k, par)
                    for m in range(HALF):
                        low_half(k, m, 0, m)
                    for e in range(NE):
                        def between():
                            if e == 0:
                                node_G(k, par)
                            if node and e == NE - 1:
                                node_D(k + 1, 1 - par)

                        expert(k, e, par, between)
                        if not node:
                            continue
                        if e == 0:
                            ahead(k + 1, 0, 1)
                            node_A(1, k + 1)
                        if e == 1:
                            took(k + 1, 0, 0)
                            node_B(1, k + 1)
                        if e == STEP_S:
                            node_S(1, k + 1)
                            ahead(k + 1, 1, 0)
                        if e == STEP_R:
                            took(k + 1, 0, 1)
                            node_R(1, k + 1)
                            ahead(k + 1, 1, 1)
                        if e == 4:
                            node_C(1, k + 1)
                        if e == 5:
                            took(k + 1, 1, 0)
                            node_X(k + 1, 1 - par, arrived)
                        if e == STEP_S2:
                            node_S2(k + 1, 1 - par)
                        if e == 6:
                            node_R2(k + 1)
                            ahead(k + 1, 2, 0)
                        if e == 7:
                            node_E(k + 1)
                            took(k + 1, 1, 1)

                with dve.Fori(0, (BLOCKS - 1) // 2) as kk:
                    for par in range(2):
                        experts(2 * kk + par, par, True, (kk + 1 + par) * 16)
                experts(BLOCKS - 1, 0, False)
                assert place_in[0] == CHAIN2


_NAMES = ["x", "src", "dst", "edge_weight"] \
    + ["L0_gnn_" + n for n in ("W1", "b1", "ln_g1", "ln_b1", "W2", "b2", "ln_g2", "ln_b2")] \
    + ["L0_ffn_" + n for n in ("Wr", "br", "W1", "b1", "g1", "be1", "m1", "v1", "W2", "b2", "g2", "be2", "m2", "v2",
                               "Wo", "bo")]


def kernel(**inputs):
    import numpy as _np
    import concourse.bacc as _bacc
    from concourse import mybir as _mybir
    from concourse.bass_utils import run_bass_kernel_spmd as _run

    nc = _bacc.Bacc("TRN2", target_bir_lowering=False, num_devices=1, dynamic_dma_scratch_size=8192)
    arrays, a = {}, {}
    for name in _NAMES:
        host = _np.ascontiguousarray(inputs[name])
        arrays["in_" + name] = host
        a[name] = nc.dram_tensor("in_" + name, host.shape, _mybir.dt.from_np(host.dtype), kind="ExternalInput").ap()
    out = nc.dram_tensor("out_0", (N, D), F32, kind="ExternalOutput").ap()

    def g(n):
        return a["L0_gnn_" + n]

    def f(n):
        return a["L0_ffn_" + n]

    build_program(nc, a["x"], a["src"], a["dst"], a["edge_weight"], (g("W1"), g("W2")), (g("b1"), g("b2")),
                  (g("ln_g1"), g("ln_g2")), (g("ln_b1"), g("ln_b2")), f("Wr"), f("br"),
                  [f(n) for n in ("b1", "g1", "be1", "m1", "v1")], [f(n) for n in ("b2", "g2", "be2", "m2", "v2")],
                  f("W1"), f("W2"), f("Wo"), f("bo"), out)
    r = _run(nc, [arrays], core_ids=[0])
    return r.results[0]["out_0"]
```

```python
from contextlib import ExitStack

import concourse.bass as bass
from concourse import mybir

F32 = mybir.dt.float32
F32R = mybir.dt.float32r
BF16 = mybir.dt.bfloat16
I32 = mybir.dt.int32
U8 = mybir.dt.uint8
ALU = mybir.AluOpType
ACT = mybir.ActivationFunctionType
AX = mybir.AxisListType

FINITE_MAX = 3.4028234663852886e38
LN_EPS = 1e-5
BN_EPS = 1e-3
EDGE_MIN = 1e-6

N, D = 3125, 256
E = 50000
NE = 8
HALF = D // 128
CHUNK = 128
GROUP = 2
GROUPS = 7
MC = GROUP * GROUPS
PAIRS = 14
CHUNKS = PAIRS * 2 * MC
NG = CHUNKS // GROUP
WIN = 64
STRETCH = 448
TILE = 112
BT = 4
BLOCK = TILE * BT
BLOCKS = 7
NP = BLOCK * BLOCKS
TILES = NP // TILE
PASSES = NP // WIN
AGG = NP + STRETCH
NOWHERE = 8192.0
LROWS, LCH = CHUNKS // 4, 4
META = 8
LAST_ROWS = N - (TILES - 1) * TILE
LROW = LCH * CHUNK
REST = E - (LROWS - 1) * LROW
HALVES = 4 * NE
PIECES = 3 * NE // 2
AT_CONV, AT_VARIANCE, AT_RSTD, AT_GAIN, AT_X1, AT_X1_RSTD, AT_HNT = range(1, NE)
LEAD_MIN = 2
DVE_TILES = [t for t in range(TILES) if t % 5 in (0, 2, 4)]
ACT_TILES = [t for t in range(TILES) if t % 5 in (1, 3)]
POOL_BLOCKS = 4
SPLIT = 4
ADVANCES = 3 * PASSES
CHAIN1, CHAIN2 = 12, 24


def build_program(nc, x, src, dst, edge_weight, gW, gb, gg, gbe, Wr, br, par1, par2, W1, W2, Wo, bo, out):
    ctx = ExitStack()
    with ctx:
        build_inside(ctx, nc, x, src, dst, edge_weight, gW, gb, gg, gbe, Wr, br, par1, par2,
                     W1, W2, Wo, bo, out)


def build_inside(ctx, nc, x, src, dst, edge_weight, gW, gb, gg, gbe, Wr, br, par1, par2,
                 W1, W2, Wo, bo, out):
    def sb(name, shape, dt=F32):
        return ctx.enter_context(nc.sbuf_tensor(name, shape, dt))

    def pb(name, shape, dt=F32):
        return ctx.enter_context(nc.psum_tensor(name, shape, dt))

    def sem(name):
        return ctx.enter_context(nc.semaphore(name))

    ds = bass.ds

    table = [nc.dram_tensor(f"table{n}", [NP, D], F32, kind="Internal").ap() for n in range(2)]
    resid = nc.dram_tensor("resid", [NP, D], F32, kind="Internal").ap()

    w_hi = [sb(f"w_hi{n}", [128, NE, HALF, D], F32R) for n in range(3)]
    w_lo = [sb(f"w_lo{n}", [128, NE, HALF, D], F32R) for n in range(3)]
    ring = sb("ring", [128, MC, D])
    onehot = sb("onehot", [128, 2, MC, WIN])
    onehot_b = onehot[:, :, :, :].bitcast(BF16)[:, :, :, 0:WIN]
    aggT = sb("aggT", [128, HALF, AGG])
    srcs = sb("srcs", [128, CHUNKS], I32)
    rel = sb("rel", [128, CHUNKS])
    ew = sb("ew", [128, CHUNKS])
    hnT_hi = [sb(f"hnT_hi{n}", [128, HALF, BLOCK], F32R) for n in range(2)]
    hnT_lo = [sb(f"hnT_lo{n}", [128, HALF, BLOCK], F32R) for n in range(2)]
    hid_hi = [sb(f"hid_hi{n}", [128, HALF, BLOCK], F32R) for n in range(2)]
    hid_lo = [sb(f"hid_lo{n}", [128, HALF, BLOCK], F32R) for n in range(2)]
    hid = sb("hid", [128, HALF, BLOCK])
    acc = [sb(f"acc{n}", [128, BT, D]) for n in range(2)]
    g_blk = sb("g_blk", [128, BT, D])
    h_res = sb("h_res", [128, BT, D])
    hc = sb("hc", [128, BT, D])
    aggst = sb("aggst", [128, HALF, BLOCK])
    bad = sb("bad", [TILE, BT * D], U8)
    gW_sb = sb("gW_sb", [128, HALF, D])
    gvec = sb("gvec", [TILE, 3, D])
    bo_meta = sb("bo_meta", [33, D])
    bo_sb = bo_meta[0:NE, :]
    meta = bo_meta[32:33, 0:2 * PAIRS * META].bitcast(I32)
    places = bo_meta[32:33, 2 * PAIRS * META:2 * PAIRS * (META + 1)].bitcast(I32)
    ident = sb("ident", [128, 128])
    iota = sb("iota", [128, WIN])
    zeros_b = sb("zeros_b", [128, STRETCH], BF16)
    zero1 = sb("zero1", [128, 1])
    ones1 = sb("ones1", [128, 1])
    br_bc = sb("br_bc", [TILE, NE])
    hid_s = sb("hid_s", [128, 2, NE * HALF])
    hid_b = sb("hid_b", [128, 2, NE * HALF])
    dis = sb("dis", [TILE, TILES])
    stats = sb("stats", [TILE, BT, 6])
    mv = sb("mv", [TILE, TILES, 2])
    rstd = sb("rstd", [TILE, TILES])
    nmr = sb("nmr", [TILE, TILES])
    logit = sb("logit", [TILE, BT, NE])
    lmax = sb("lmax", [TILE, BT])
    lsum = sb("lsum", [TILE, BT])
    gate = [sb(f"gate{n}", [TILE, BT, NE]) for n in range(2)]
    wr_f = sb("wr_f", [128, HALF, NE])
    wr_hi = sb("wr_hi", [128, HALF, NE], F32R)
    wr_lo = sb("wr_lo", [128, HALF, NE], F32R)
    small = sb("small", [128, 2 * PAIRS])
    place = sb("place", [128, 2 * PAIRS])
    bmv = sb("bmv", [TILE, BT, 2])
    newton = sb("newton", [TILE, TILES])
    eps = sb("eps", [128, 2])
    brstd = sb("brstd", [TILE, BT])
    bnmr = sb("bnmr", [TILE, BT])
    drow = sb("drow", [TILE, 2, TILES])
    odd = sb("odd", [TILE, TILES], U8)
    ctrl = sb("ctrl", [1, 4], I32)
    idx_st = sb("idx_st", [128, 2, MC], I32)

    scal = sb("scal", [128, 8])
    gext = sb("gext", [LROWS, 2, GROUP])

    gateT = aggst[0:NE, 0, :]

    def flat(t):
        return t[:, :, :].rearrange("p a b -> p (a b)")

    x_all = flat(aggT)[0:TILE, :].rearrange("p (t d) -> p t d", d=D)
    degrow = flat(ring)[0:3, :]
    ew3 = flat(hid).bitcast(BF16)[:, 0:3 * CHUNKS].rearrange("p (c k) -> p c k", k=3)
    iota_i = flat(hid)[:, 3 * CHUNKS // 2:3 * CHUNKS // 2 + WIN].bitcast(I32)
    ew_st = flat(hid)[:, 656:656 + 3 * MC].bitcast(BF16).rearrange("p (h s k) -> p h s k", h=2, k=3)
    par_T = flat(hid)[:, 704:704 + 10 * NE * HALF].rearrange("p (l i c) -> p l i c", l=2, i=5)
    ldst, lsrc, lew = (flat(t)[0:LROWS, :] for t in (hc, g_blk, h_res))
    diag = flat(acc[0])[0:LROWS, 0:4 * LROWS]
    ones_m = flat(acc[0])[0:LROWS, 512:640]
    room = flat(acc[1])
    pair_i = flat(aggst)[:, 0:NG].bitcast(I32)
    par_st = flat(aggst)[0:5 * NE * HALF, 512:768].rearrange("p (l n) -> p l n", l=2)
    stage = [acc[n][:, :, :].rearrange("p (e k) n -> p e k n", k=HALF) for n in range(2)]

    psA = pb("psA", [128, 2, 512])
    psN = pb("psN", [128, 2, 512])
    psH = pb("psH", [128, 2, 512])
    psY = pb("psY", [128, 2, 512])

    s_pad = sem("s_pad")
    s_pool = sem("s_pool")
    s_wr_hi = sem("s_wr_hi")
    s_wr_lo = sem("s_wr_lo")
    s_x_last = sem("s_x_last")
    s_degrow = sem("s_degrow")
    s_carried = sem("s_carried")
    s_dst_in = sem("s_dst_in")
    s_src_in = sem("s_src_in")
    s_ew_in = sem("s_ew_in")
    s_x_in = [sem(f"s_x_in{b}") for b in range(BLOCKS)]
    s_const_in = sem("s_const_in")
    s_par_in = sem("s_par_in")
    s_pre = sem("s_pre")
    s_prep = sem("s_prep")
    s_prep_pe = sem("s_prep_pe")
    s_meta = sem("s_meta")
    s_srcs = sem("s_srcs")
    s_var_x = sem("s_var_x")
    s_sqrt_x = sem("s_sqrt_x")
    s_var_par = sem("s_var_par")
    s_sqrt_par = sem("s_sqrt_par")
    s_sqrt_deg = sem("s_sqrt_deg")
    s_var = sem("s_var")
    s_sqrt = sem("s_sqrt")
    s_h0 = sem("s_h0")
    s_clean = sem("s_clean")
    s_g1_dve = sem("s_g1_dve")
    s_x_stat = sem("s_x_stat")
    s_x_clean = sem("s_x_clean")
    s_degrow_clear = sem("s_degrow_clear")
    s_dis = sem("s_dis")
    s_g1 = sem("s_g1")
    s_g1_out = sem("s_g1_out")
    s_deg_oh = sem("s_deg_oh")
    s_deg_mm = sem("s_deg_mm")
    s_deg_free = sem("s_deg_free")
    s_degT = sem("s_degT")
    s_wst_in = [sem(f"s_wst_in{n}") for n in range(2)]
    s_w_hi = sem("s_w_hi")
    s_w_lo = sem("s_w_lo")
    s_par = sem("s_par")
    s_gath = [sem(f"s_gath{s}") for s in range(MC)]
    s_used = sem("s_used")
    s_oh = sem("s_oh")
    s_agg_free = sem("s_agg_free")
    s_idx = sem("s_idx")
    s_ohc = sem("s_ohc")
    s_adv = sem("s_adv")
    s_g_in = sem("s_g_in")
    s_hres_in = sem("s_hres_in")
    s_x_blk = [sem(f"s_x_blk{n}") for n in range(2)]
    s_gvec_in = sem("s_gvec_in")
    s_gT = sem("s_gT")
    s_aggst = sem("s_aggst")
    s_conv = sem("s_conv")
    s_conv_ev = sem("s_conv_ev")
    s_stat = sem("s_stat")
    s_norm = sem("s_norm")
    s_h = sem("s_h")
    s_g2 = sem("s_g2")
    s_h_out = sem("s_h_out")
    s_g2_out = sem("s_g2_out")
    s_ch1 = sem("s_ch1")
    s_ch2 = sem("s_ch2")
    s_stat2 = sem("s_stat2")
    s_hn = sem("s_hn")
    s_hnT = sem("s_hnT")
    s_hnT_hi = sem("s_hnT_hi")
    s_hnT_lo = sem("s_hnT_lo")
    s_logit = sem("s_logit")
    s_lsub = sem("s_lsub")
    s_exp = sem("s_exp")
    s_gate = sem("s_gate")
    s_gateT = sem("s_gateT")
    s_gateT_sb = sem("s_gateT_sb")
    s_gbo = sem("s_gbo")
    s_acc0 = sem("s_acc0")
    s_hid = sem("s_hid")
    s_hid_free = sem("s_hid_free")
    s_hid_hi = sem("s_hid_hi")
    s_hid_lo = sem("s_hid_lo")
    s_y = sem("s_y")
    s_y_free = sem("s_y_free")
    s_out = [sem(f"s_out{n}") for n in range(2)]

    def within(value, low, high):
        return value if isinstance(value, int) else value.with_bounds(min_val=low, max_val=high)

    def carry(eng):
        eng.sem_inc(s_carried, 1)

    def control(eng):
        eng.wait_ge(s_meta, 1)
        extra = eng.value_load(ctrl[0:1, 0:1], min_val=0, max_val=PASSES - 1)
        lead = eng.value_load(ctrl[0:1, 1:2], min_val=LEAD_MIN, max_val=PAIRS)
        return extra, lead

    def extra_passes(eng, extra, base, pair, after=None):
        with eng.If(extra > 0):
            with eng.Fori(0, PASSES - 1) as p:
                with eng.Fori(0, PAIRS) as i:
                    pair(base + p * PAIRS + i, PAIRS - 1 - i)
                if after is not None:
                    after(p)

    block = ctx.enter_context(nc.Block())

    @block.sync
    def _(sp):
        sp.wait_ge(s_pad, 3)
        for tile, array, s_in in ((ldst, dst, s_dst_in), (lew, edge_weight, s_ew_in), (lsrc, src, s_src_in)):
            t = tile[:, 0:LROW] if array is edge_weight else tile[:, 0:LROW].bitcast(I32)
            sp.dma_start(t[0:96, :], array[0:96 * LROW].rearrange("(p n) -> p n", n=LROW)).then_inc(s_in, 16)
            sp.dma_start(t[96:97, :], array[96 * LROW:97 * LROW].rearrange("(p n) -> p n", n=LROW)).then_inc(s_in, 16)
            sp.dma_start(t[97:98, 0:REST], array[97 * LROW:E].rearrange("(p n) -> p n", p=1)).then_inc(s_in, 16)
        for b in range(BLOCKS):
            full = BT if b < BLOCKS - 1 else BT - 1
            sp.dma_start(x_all[:, b * BT:b * BT + full, :],
                         x[b * BLOCK:b * BLOCK + full * TILE, :].rearrange("(t p) d -> p t d", p=TILE)
                         ).then_inc(s_x_in[b], 16)
        sp.wait_ge(s_pad, 4)
        sp.dma_start(x_all[0:LAST_ROWS, TILES - 1, :], x[N - LAST_ROWS:N, :]).then_inc(s_x_in[BLOCKS - 1], 16)
        for l, arrays in enumerate((par1, par2)):
            for i, a in enumerate(arrays):
                rows16 = NE * HALF
                sp.dma_start(par_st[i * rows16:(i + 1) * rows16, l, :], a.rearrange("e (m p) -> (e m) p", p=128)).then_inc(s_par_in, 16)
        sp.dma_start(bo_sb[:, :], bo).then_inc(s_const_in, 16)
        sp.dma_start(br_bc[:, :], br.unsqueeze(0).broadcast_to([TILE, NE])).then_inc(s_const_in, 16)
        sp.dma_start(wr_f[:, :, :], Wr.rearrange("(k p) e -> p k e", p=128)).then_inc(s_const_in, 16)

        def rows(t, b):
            return t[ds(within(b * BLOCK, 0, t.shape[0] - BLOCK), BLOCK), :].rearrange("(t p) d -> p t d", p=TILE)

        def static_rows(t, b):
            return t[b * BLOCK:(b + 1) * BLOCK, :].rearrange("(t p) d -> p t d", p=TILE)

        def layer_consts(layer):
            sp.dma_start(gW_sb[:, :, :], gW[layer].rearrange("(k p) n -> p k n", p=128)).then_inc(s_gvec_in, 16)
            for i, v in enumerate((gb[layer], gg[layer], gbe[layer])):
                sp.dma_start(gvec[:, i, :], v.unsqueeze(0).broadcast_to([TILE, D])).then_inc(s_gvec_in, 16)

        layer_consts(0)
        sp.wait_ge(s_meta, 1)
        for piece in range(PIECES):
            w, e, u = (W1, W2, Wo)[piece // 4], 2 * (piece % 4), piece % 2
            if piece >= 2:
                sp.wait_ge(s_w_lo, piece - 1)
            for i in range(2):
                sp.dma_start(stage[u][:, i, :, :], w[e + i].rearrange("(k p) n -> p k n", p=128)).then_inc(s_wst_in[u], 16)
        for b in range(BLOCKS):
            sp.wait_ge(s_g1, sum(t < (b + 1) * BT for t in ACT_TILES))
            sp.wait_ge(s_g1_dve, sum(t < (b + 1) * BT for t in DVE_TILES))
            sp.dma_start(static_rows(table[0], b), x_all[:, b * BT:(b + 1) * BT, :]).then_inc(s_g1_out, 16)

        def load_table_block(layer, j):
            sp.dma_start(g_blk[0:TILE, :, :], rows(table[layer], BLOCKS - 1 - j)).then_inc(s_g_in, 16)

        def load_x_block(tile, s_in, k):
            sp.dma_start(tile[0:TILE, :, :], rows(x, BLOCKS - 1 - k)).then_inc(s_in, 16)

        def load_last_x_block(tile, s_in):
            tail = (BLOCKS - 1) * BLOCK
            sp.dma_start(tile[0:TILE, 0:BT - 1, :],
                         x[tail:tail + (BT - 1) * TILE, :].rearrange("(t p) d -> p t d", p=TILE)).then_inc(s_in, 16)
            sp.dma_start(tile[0:LAST_ROWS, BT - 1, :], x[N - LAST_ROWS:N, :]).then_inc(s_x_last, 16)
            sp.dma_start(tile[LAST_ROWS:TILE, BT - 1, :], x[0:TILE - LAST_ROWS, :]).then_inc(s_x_last, 16)

        def load_resid_block(j):
            sp.dma_start(h_res[0:TILE, :, :], rows(resid, BLOCKS - 1 - j)).then_inc(s_hres_in, 16)

        def store_layer1(j):
            b = BLOCKS - 1 - j
            sp.wait_ge(s_h, j + 1)
            carry(sp)
            sp.dma_start(rows(resid, b), hc[0:TILE, :, :]).then_inc(s_h_out, 16)
            sp.wait_ge(s_g2, BT * (j + 1))
            carry(sp)
            sp.dma_start(rows(table[1], b), h_res[0:TILE, :, :]).then_inc(s_g2_out, 16)

        def store_out(k, par, last_piece=True):
            first = (BLOCKS - 1 - k) * BLOCK
            sp.dma_start(out[ds(first, (BT - 1) * TILE), :].rearrange("(t p) d -> p t d", p=TILE),
                         acc[par][0:TILE, 0:BT - 1, :]).then_inc(s_out[par], 16)
            sp.dma_start(out[ds(first + (BT - 1) * TILE, LAST_ROWS), :],
                         acc[par][0:LAST_ROWS, BT - 1, :]).then_inc(s_out[par], 16)
            if last_piece:
                sp.dma_start(out[ds(first + (BT - 1) * TILE + LAST_ROWS, TILE - LAST_ROWS), :],
                             acc[par][LAST_ROWS:TILE, BT - 1, :]).then_inc(s_out[par], 16)

        sp.wait_ge(s_g1_out, 16 * BLOCKS)
        sp.wait_ge(s_srcs, 1)
        load_table_block(0, 0)
        load_last_x_block(h_res, s_hres_in)
        store_layer1(0)
        with sp.Fori(1, BLOCKS) as j:
            sp.wait_ge(s_gT, j)
            carry(sp)
            load_table_block(0, j)
            sp.wait_ge(s_g2_out, 16 * j)
            carry(sp)
            load_x_block(h_res, s_hres_in, j)
            store_layer1(j)
        sp.wait_ge(s_g2_out, 16 * BLOCKS)
        sp.wait_ge(s_h_out, 16 * BLOCKS)
        layer_consts(1)
        load_table_block(1, 0)
        load_resid_block(0)
        load_last_x_block(acc[0], s_x_blk[0])
        sp.wait_ge(s_gT, BLOCKS + 1)
        load_table_block(1, 1)
        sp.wait_ge(s_acc0, 1)
        load_resid_block(1)
        load_x_block(acc[1], s_x_blk[1], 1)
        with sp.Fori(0, (BLOCKS - 1) // 2) as kk:
            for par in range(2):
                k = 2 * kk + par
                with sp.If(k + 2 < BLOCKS):
                    sp.wait_ge(s_gT, BLOCKS + k + 2)
                    carry(sp)
                    load_table_block(1, k + 2)
                    sp.wait_ge(s_acc0, k + 2)
                    carry(sp)
                    load_resid_block(k + 2)
                sp.wait_ge(s_y_free, 2 * NE * (k + 1) + 2)
                carry(sp)
                if par == 0:
                    store_out(k, 0, last_piece=False)
                    with sp.If(kk > 0):
                        first = within((BLOCKS - 1 - k) * BLOCK, 0, (BLOCKS - 3) * BLOCK)
                        sp.dma_start(out[ds(first + (BT - 1) * TILE + LAST_ROWS, TILE - LAST_ROWS), :],
                                     acc[0][LAST_ROWS:TILE, BT - 1, :]).then_inc(s_out[0], 16)
                    with sp.Else():
                        sp.dma_start(table[0][0:TILE - LAST_ROWS, :],
                                     acc[0][LAST_ROWS:TILE, BT - 1, :]).then_inc(s_out[0], 16)
                else:
                    store_out(k, 1)
                sp.wait_ge(s_out[par], 48 * (kk + 1))
                carry(sp)
                with sp.If(k + 2 < BLOCKS):
                    load_x_block(acc[par], s_x_blk[par], k + 2)
                sp.nop()
        sp.wait_ge(s_y_free, 2 * NE * BLOCKS + 2)
        store_out(BLOCKS - 1, 0)
        sp.wait_ge(s_out[0], 48 * 4)
        sp.wait_ge(s_out[1], 48 * 3)

    @block.gpsimd
    def _(pool):
        nc.gpsimd.memset(ldst[:, 0:LROW].bitcast(I32), int(NOWHERE)).then_inc(s_pad, 1)
        nc.gpsimd.memset(lew[:, 0:LROW], 0.0).then_inc(s_pad, 1)
        nc.gpsimd.memset(lsrc[:, 0:LROW].bitcast(I32), 0).then_inc(s_pad, 1)
        nc.gpsimd.memset(x_all[:, TILES - 1, :], 0.0).then_inc(s_pad, 1)
        nc.gpsimd.memset(ident[:, :], 0.0).then_inc(s_pool, 1)
        nc.gpsimd.memset(zeros_b[:, :], 0.0).then_inc(s_pool, 1)
        nc.gpsimd.memset(ones_m[:, :], 1.0).then_inc(s_pool, 1)
        nc.gpsimd.memset(ones1[:, :], 1.0).then_inc(s_pool, 1)
        nc.gpsimd.memset(zero1[:, :], 0.0).then_inc(s_pool, 1)
        nc.gpsimd.iota(iota_i[:, :], [[1, WIN]], base=0, channel_multiplier=0).then_inc(s_pool, 1)
        nc.gpsimd.iota(pair_i, [[1, PAIRS], [0, NG // PAIRS]], base=0, channel_multiplier=0).then_inc(s_pool, 1)
        nc.gpsimd.memset(eps[:, 0:1], LN_EPS).then_inc(s_pool, 1)
        nc.gpsimd.memset(eps[:, 1:2], BN_EPS).then_inc(s_pool, 1)
        pool.wait_ge(s_pool, 9)
        nc.gpsimd.affine_select(out=ident[:, :], in_=ident[:, :], compare_op=ALU.not_equal, fill=1.0, base=0,
                                pattern=[[-1, 128]], channel_multiplier=1).then_inc(s_pool, 1)
        nc.gpsimd.memset(degrow, 0.0).then_inc(s_degrow_clear, 1)
        pool.wait_ge(s_wr_hi, 1)
        nc.gpsimd.tensor_tensor(wr_lo[:, :, :], wr_f[:, :, :], wr_hi[:, :, :].bitcast(F32), ALU.subtract).then_inc(s_wr_lo, 1)
        for piece in range(PIECES):
            t, e, u = piece // 4, 2 * (piece % 4), piece % 2
            pool.wait_ge(s_w_hi, piece + 1)
            nc.gpsimd.tensor_tensor(w_lo[t][:, e:e + 2, :, :], stage[u], w_hi[t][:, e:e + 2, :, :].bitcast(F32),
                                    ALU.subtract).then_inc(s_w_lo, 1)
        for b in range(POOL_BLOCKS):
            pool.wait_ge(s_x_stat, b + 1)
            xb = x_all[:, b * BT:(b + 1) * BT, :]
            nc.gpsimd.tensor_scalar(xb, xb, -FINITE_MAX, FINITE_MAX, ALU.max, ALU.min).then_inc(s_x_clean, 1)
        extra, _ = control(pool)
        pool.wait_ge(s_srcs, 1)

        def gathers(layer, g, pb):
            for h in range(2):
                m = 2 * g + h
                nc.gpsimd.tensor_copy(idx_st[:, h, :], srcs[:, ds(pb * (2 * MC) + h * MC, MC)]).then_inc(s_idx, 1)
                pool.wait_ge(s_idx, m + 1)
                for s in range(MC):
                    if s % GROUP == 0:
                        pool.wait_ge(s_used, m * GROUPS + s // GROUP + 1)
                        carry(pool)
                    nc.gpsimd.indirect_dma_start(
                        ring[:, s, :], None, table[layer],
                        bass.IndirectOffsetOnAxis(ap=idx_st[:, h, s:s + 1], axis=0)).then_inc(s_gath[s], 16)

        pool.wait_ge(s_g1_out, 16 * BLOCKS)
        pool.wait_ge(s_degT, 1)
        extra_passes(pool, extra, 0, lambda g, pb: gathers(0, g, pb))
        with pool.Fori(0, PAIRS) as i:
            gathers(0, extra * PAIRS + i, PAIRS - 1 - i)
        pool.wait_ge(s_g2_out, 16 * BLOCKS)
        extra_passes(pool, extra, extra * PAIRS + PAIRS, lambda g, pb: gathers(1, g, pb))
        with pool.Fori(0, PAIRS) as i:
            gathers(1, extra * (2 * PAIRS) + PAIRS + i, PAIRS - 1 - i)

    @block.scalar
    def _(act):
        act.sem_inc(s_hid_free, 2)

        def split_piece(piece):
            t, e, u = piece // 4, 2 * (piece % 4), piece % 2
            act.wait_ge(s_wst_in[u], 32 * (piece // 2 + 1))
            nc.scalar.activation(w_hi[t][:, e:e + 2, :, :], stage[u], ACT.Copy).then_inc(s_w_hi, 1)

        act.wait_ge(s_const_in, 48)
        nc.scalar.activation(wr_hi[:, :, :], wr_f[:, :, :], ACT.Copy).then_inc(s_wr_hi, 1)
        for piece in range(PIECES):
            split_piece(piece)
        act.wait_ge(s_pool, 10)
        act.wait_ge(s_degT, 1)
        nc.scalar.activation(dis[:, :], psN[0:TILE, 1, 0:TILES], ACT.Sqrt, bias=ones1[0:TILE, :]).then_inc(s_sqrt_deg, 1)
        act.wait_ge(s_var_x, 1)
        nc.scalar.activation(rstd[:, :], mv[:, :, 1], ACT.Sqrt, bias=eps[0:TILE, 0:1]).then_inc(s_sqrt_x, 1)
        act.wait_ge(s_dis, 1)
        for t in ACT_TILES:
            act.wait_ge(s_x_clean, min(t // BT + 1, POOL_BLOCKS))
            nc.scalar.activation(x_all[:, t, :], x_all[:, t, :], ACT.Identity,
                                 bias=drow[:, 1, t:t + 1], scale=drow[:, 0, t:t + 1]).then_inc(s_g1, 1)
        act.wait_ge(s_var_par, 1)
        nc.scalar.activation(hid_s[:, :, :], par_T[:, :, 4, :], ACT.Sqrt, bias=eps[:, 1:2]).then_inc(s_sqrt_par, 1)
        def root(nth):
            act.wait_ge(s_var, nth)
            nc.scalar.activation(brstd[:, :], bmv[:, :, 1], ACT.Sqrt, bias=eps[0:TILE, 0:1]).then_inc(s_sqrt, 1)

        def norm(layer, j):
            act.wait_ge(s_stat, layer * BLOCKS + j + 1)
            for t in range(BT):
                nc.scalar.activation(hc[0:TILE, t, :], hc[0:TILE, t, :], ACT.Identity,
                                     bias=bnmr[:, t:t + 1], scale=brstd[:, t:t + 1]).then_inc(s_norm, 1)

        def first_residual(j):
            act.wait_ge(s_clean, j + 1)
            for t in range(BT):
                col = ds((BLOCKS - 1 - j) * BT + t, 1)
                nc.scalar.activation(h_res[0:TILE, t, :], h_res[0:TILE, t, :], ACT.Identity,
                                     bias=nmr[:, col], scale=rstd[:, col]).then_inc(s_h0, 1)

        def second_table(j):
            act.wait_ge(s_h, j + 1)
            for t in range(BT):
                nc.scalar.activation(h_res[0:TILE, t, :], hc[0:TILE, t, :], ACT.Copy,
                                     scale=dis[:, ds((BLOCKS - 1 - j) * BT + t, 1)]).then_inc(s_g2, 1)

        def norm_x1(j, par):
            act.wait_ge(s_stat2, j + 1)
            for t in range(BT):
                nc.scalar.activation(hc[0:TILE, t, :], acc[par][0:TILE, t, :], ACT.Identity,
                                     bias=bnmr[:, t:t + 1], scale=brstd[:, t:t + 1]).then_inc(s_hn, 1)

        def hnT_high(j, par):
            act.wait_ge(s_hnT, j + 1)
            nc.scalar.activation(hnT_hi[par][:, :, :], psN[:, :, 0:BLOCK], ACT.Copy).then_inc(s_hnT_hi, 1)

        def exponentials(j):
            act.wait_ge(s_lsub, j + 1)
            nc.scalar.activation(logit[:, :, :], logit[:, :, :], ACT.Exp).then_inc(s_exp, 1)

        def gates_T(j):
            act.wait_ge(s_gateT, j + 1)
            nc.scalar.activation(gateT[:, :], psN[0:NE, 1, 0:BLOCK], ACT.Copy).then_inc(s_gateT_sb, 1)

        def hidden_half(k, idx, l, e, m):
            n = k * HALVES + idx
            act.wait_ge(s_hid, n + 1)
            act.wait_ge(s_hid_lo, n + 1)
            col = e * HALF + m
            nc.scalar.activation(hid[:, m, :], psH[:, m, 0:BLOCK], ACT.Relu, bias=hid_b[:, l, col:col + 1],
                                 scale=hid_s[:, l, col:col + 1]).then_inc(s_hid_free, 1)
            act.wait_ge(s_hid_free, n + 3)
            nc.scalar.activation(hid_hi[l][:, m, :], hid[:, m, :], ACT.Copy).then_inc(s_hid_hi, 1)

        def expert(k, e, between):
            for m in range(HALF):
                hidden_half(k, 4 * e + 2 + m, 1, e, m)
            between()
            if e + 1 < NE:
                for m in range(HALF):
                    hidden_half(k, 4 * (e + 1) + m, 0, e + 1, m)

        def node_layer1(j):
            first_residual(j)
            root(j + 1)
            norm(0, j)
            second_table(j)

        node_layer1(0)
        with act.Fori(1, BLOCKS) as j:
            node_layer1(j)
        root(BLOCKS + 1)
        norm(1, 0)
        root(BLOCKS + 2)
        norm_x1(0, 0)
        hnT_high(0, 0)

        def experts(k, par, node, edges=True):
            exponentials(k)
            for m in range(HALF):
                hidden_half(k, m, 0, 0, m)
            gates_T(k)
            for e in range(NE):
                def between():
                    if node and edges and e == AT_RSTD:
                        root(BLOCKS + 2 * (k + 1) + 1)
                    if node and not edges and e == AT_RSTD:
                        norm(1, k + 1)
                    if node and edges and e == AT_X1_RSTD:
                        root(BLOCKS + 2 * (k + 1) + 2)
                    if node and e == AT_HNT:
                        hnT_high(k + 1, 1 - par)

                expert(k, e, between)
                if node and not edges and e == AT_VARIANCE:
                    root(BLOCKS + 2 * (k + 1) + 1)
                if node and edges and e == AT_RSTD:
                    norm(1, k + 1)
                if node and not edges and e == AT_X1:
                    root(BLOCKS + 2 * (k + 1) + 2)
                if node and e == AT_X1_RSTD:
                    norm_x1(k + 1, 1 - par)

        act.wait_ge(s_par, 1)
        with act.Fori(0, BLOCKS // 2 - 1) as kk:
            for par in range(2):
                experts(2 * kk + par, par, True)
        experts(BLOCKS - 3, 0, True)
        experts(BLOCKS - 2, 1, True, edges=False)
        experts(BLOCKS - 1, 0, False)

    @block.tensor
    def _(pe):
        pe.sem_inc(s_used, GROUPS)
        pe.wait_ge(s_pool, 10)
        pe.wait_ge(s_prep, 1)
        for c in range(LCH):
            nc.tensor.transpose(psH[:, 0, c * LROWS:(c + 1) * LROWS], ldst[:, LROW + c * CHUNK:LROW + (c + 1) * CHUNK],
                                ident[0:LROWS, 0:LROWS]).then_inc(s_prep_pe, 1)
        pe.wait_ge(s_prep, 2)
        nc.tensor.matmul(psN[:, 0, 0:4 * LROWS], ones_m, diag, start=True, stop=True).then_inc(s_prep_pe, 1)
        pe.wait_ge(s_prep, 3)
        for c in range(LCH):
            nc.tensor.transpose(psY[:, 0, c * LROWS:(c + 1) * LROWS], lew[:, LROW + c * CHUNK:LROW + (c + 1) * CHUNK],
                                ident[0:LROWS, 0:LROWS]).then_inc(s_prep_pe, 1)
        pe.wait_ge(s_prep, 4)
        for c in range(LCH):
            nc.tensor.transpose(psH[:, 1, c * LROWS:(c + 1) * LROWS], lsrc[:, LROW + c * CHUNK:LROW + (c + 1) * CHUNK],
                                ident[0:LROWS, 0:LROWS]).then_inc(s_prep_pe, 1)
        pe.wait_ge(s_par_in, 16 * 10)
        rows80 = 5 * NE * HALF
        for l in range(2):
            nc.tensor.transpose(psY[:, 1, l * rows80:(l + 1) * rows80], par_st[:, l, :],
                                ident[0:rows80, 0:rows80]).then_inc(s_prep_pe, 1)

        extra, lead = control(pe)

        places = []

        def window_regs(pb, h, first, last):
            places.append(None)
            regs = [pe.alloc_register(f"win{len(places)}_{n}") for n in range(first, last)]
            pe.load(regs, meta[0:1, ds(pb * (2 * META) + h * META + first, last - first)])
            return regs, [pe.snap(r, min_val=0, max_val=STRETCH - WIN) for r in regs]

        def degree_pair(g, pb):
            for h in range(2):
                m = 2 * g + h
                regs, offs = window_regs(pb, h, 0, GROUPS)
                pe.wait_ge(s_deg_free, m + 1)
                nc.tensor.matmul(psA[0:3, h, 0:STRETCH], zeros_b[:, 0:3], zeros_b[:, :], start=True, stop=True)
                pe.wait_ge(s_deg_oh, 2 * m + 2)
                for s in range(MC):
                    last = nc.tensor.matmul(psA[0:3, h, ds(offs[s // GROUP], WIN)], ew_st[:, h, s, :],
                                            onehot_b[:, h, s, :], start=False, stop=True, skip_group_check=True)
                last.then_inc(s_deg_mm, 1)
                for r in regs:
                    pe.free_register(r)

        extra_passes(pe, extra, 0, degree_pair)
        with pe.Fori(0, PAIRS) as i:
            degree_pair(extra * PAIRS + i, PAIRS - 1 - i)
        pe.wait_ge(s_degrow, 1)
        for t in range(TILES):
            last = nc.tensor.matmul(psN[0:TILE, 1, t:t + 1], degrow[:, t * TILE:(t + 1) * TILE], ones1[0:3, :],
                                    start=True, stop=True)
        last.then_inc(s_degT, 1)

        def macro(g, pb, h, part):
            m = 2 * g + h
            first, last = ((0, SPLIT), (SPLIT, GROUPS))[part]
            regs, offs = window_regs(pb, h, first, last)
            if part == 0:
                pe.wait_ge(s_agg_free, m + 1)
                for f in range(HALF):
                    nc.tensor.matmul(psA[:, f, 0:STRETCH], zeros_b[:, 0:128], zeros_b[:, :], start=True, stop=True)
            if part == 0:
                pe.wait_ge(s_oh, m + 1)
            for s in range(first * GROUP, last * GROUP):
                pe.wait_ge(s_gath[s], (m + 1) * 16)
                for f in range(HALF):
                    ins = nc.tensor.matmul(psA[:, f, ds(offs[s // GROUP - first], WIN)], ring[:, s, f * 128:(f + 1) * 128],
                                           onehot[:, h, s, :], start=False, stop=True, skip_group_check=True)
                if s % GROUP == GROUP - 1:
                    ins.then_inc(s_used, 1)
            for r in regs:
                pe.free_register(r)

        def pair(g, pb):
            for h in range(2):
                for part in range(2):
                    macro(g, pb, h, part)

        def transpose_table(layer, j, first=False):
            n = layer * BLOCKS + j
            pe.wait_ge(s_g_in, (n + 1) * 16)
            if layer == 0:
                if not first:
                    pe.wait_ge(s_conv_ev, n)
            elif first:
                pe.wait_ge(s_conv_ev, n)
            else:
                pe.wait_ge(s_acc0, j)
            for f in range(HALF):
                for t in range(BT):
                    last = nc.tensor.transpose(psN[:, f, t * TILE:(t + 1) * TILE],
                                               g_blk[0:TILE, t, f * 128:(f + 1) * 128], ident[0:TILE, 0:TILE])
            last.then_inc(s_gT, 1)

        def conv(layer, j):
            pe.wait_ge(s_gvec_in, 64 * (layer + 1))
            pe.wait_ge(s_aggst, layer * BLOCKS + j + 1)
            for t in range(BT):
                for f in range(HALF):
                    last = nc.tensor.matmul(psN[0:TILE, t // 2, (t % 2) * D:(t % 2 + 1) * D],
                                            aggst[:, f, t * TILE:(t + 1) * TILE], gW_sb[:, f, :],
                                            start=(f == 0), stop=(f == HALF - 1))
            last.then_inc(s_conv, 1)

        def transpose_hn(j):
            pe.wait_ge(s_hn, (j + 1) * BT)
            for f in range(HALF):
                for t in range(BT):
                    last = nc.tensor.transpose(psN[:, f, t * TILE:(t + 1) * TILE],
                                               hc[0:TILE, t, f * 128:(f + 1) * 128], ident[0:TILE, 0:TILE])
            last.then_inc(s_hnT, 1)

        def three(ps, hi, lo, whi, wlo, weights_stationary, start, stop):
            for i, (a, w) in enumerate(((hi, whi), (hi, wlo), (lo, whi))):
                lhsT, rhs = (w, a) if weights_stationary else (a, w)
                last = nc.tensor.matmul(ps, lhsT, rhs, start=start and i == 0, stop=stop and i == 2)
            return last

        def logits(j, par):
            pe.wait_ge(s_hnT_lo, j + 1)
            for t in range(BT):
                ts = slice(t * TILE, (t + 1) * TILE)
                for f in range(HALF):
                    last = three(psN[0:TILE, 0, t * NE:(t + 1) * NE], hnT_hi[par][:, f, ts], hnT_lo[par][:, f, ts],
                                 wr_hi[:, f, :], wr_lo[:, f, :], False, f == 0, f == HALF - 1)
            last.then_inc(s_logit, 1)

        def transpose_gates(j, par):
            pe.wait_ge(s_gate, j + 1)
            for t in range(BT):
                last = nc.tensor.transpose(psN[0:NE, 1, t * TILE:(t + 1) * TILE], gate[par][:, t, :], ident[0:TILE, 0:TILE])
            last.then_inc(s_gateT, 1)

        def gates_times_bo(j):
            pe.wait_ge(s_gateT_sb, j + 1)
            for t in range(BT):
                last = nc.tensor.matmul(psN[0:TILE, t // 2, (t % 2) * D:(t % 2 + 1) * D],
                                        gateT[:, t * TILE:(t + 1) * TILE], bo_sb[:, :], start=True, stop=True)
            last.then_inc(s_gbo, 1)

        def hidden(k, idx, l, e, m):
            n = k * HALVES + idx
            pe.wait_ge(s_hid_free, n + 1)
            src_hi, src_lo = (hnT_hi[k_par[0]], hnT_lo[k_par[0]]) if l == 0 else (hid_hi[0], hid_lo[0])
            ms = slice(m * 128, (m + 1) * 128)
            for f in range(HALF):
                last = three(psH[:, m, 0:BLOCK], src_hi[:, f, :], src_lo[:, f, :], w_hi[l][:, e, f, ms],
                             w_lo[l][:, e, f, ms], True, f == 0, f == HALF - 1)
            last.then_inc(s_hid, 1)

        k_par = [0]

        def experts_start(k, par):
            k_par[0] = par
            pe.wait_ge(s_hnT_lo, k + 1)
            for m in range(HALF):
                hidden(k, m, 0, 0, m)

        def expert(k, e, between):
            pe.wait_ge(s_hid_lo, k * HALVES + 4 * e + 2 + 2)
            for m in range(HALF):
                hidden(k, 4 * e + 2 + m, 1, e, m)
            if e + 1 < NE:
                for m in range(HALF):
                    hidden(k, 4 * (e + 1) + m, 0, e + 1, m)
            between()
            pe.wait_ge(s_hid_lo, k * HALVES + 4 * e + 4 + 2)
            for u in range(2):
                n = (k * NE + e) * 2 + u
                pe.wait_ge(s_y_free, n + 1)
                for t in (2 * u, 2 * u + 1):
                    ts = slice(t * TILE, (t + 1) * TILE)
                    for f in range(HALF):
                        last = three(psY[0:TILE, u, (t % 2) * D:(t % 2 + 1) * D], hid_hi[1][:, f, ts],
                                     hid_lo[1][:, f, ts], w_hi[2][:, e, f, :], w_lo[2][:, e, f, :], False,
                                     f == 0, f == HALF - 1)
                last.then_inc(s_y, 1)

        for layer in range(2):
            first = extra * (PAIRS * (layer + 1)) + PAIRS * layer
            extra_passes(pe, extra, extra * (PAIRS * layer) + PAIRS * layer, pair)
            with pe.Fori(0, lead) as i:
                pair(first + i, PAIRS - 1 - i)

            def part_of(j, a, h, part, first=first):
                with pe.If(lead + 2 * j + a < PAIRS):
                    macro(first + lead + 2 * j + a, within(PAIRS - 1 - lead - 2 * j - a, 0, PAIRS - 1 - LEAD_MIN), h, part)

            if layer == 0:
                def node(j, first=False, edges=True):
                    transpose_table(0, j, first)
                    if edges:
                        for part in range(2):
                            part_of(j, 0, 0, part)
                    conv(0, j)
                    if edges:
                        for a, h in ((0, 1), (1, 0), (1, 1)):
                            for part in range(2):
                                part_of(j, a, h, part)

                node(0, first=True)
                with pe.Fori(1, BLOCKS - 1) as j:
                    node(j)
                node(BLOCKS - 1, edges=False)
            else:
                transpose_table(1, 0, first=True)
                for part in range(2):
                    part_of(0, 0, 0, part)
                conv(1, 0)
                for a, h in ((0, 1), (1, 0)):
                    for part in range(2):
                        part_of(0, a, h, part)
                part_of(0, 1, 1, 0)
                pe.wait_ge(s_w_lo, PIECES)
                pe.wait_ge(s_wr_lo, 1)
                transpose_hn(0)
                logits(0, 0)
                part_of(0, 1, 1, 1)

                def experts(k, par, node, edges=True):
                    edges = edges and node
                    experts_start(k, par)
                    if edges:
                        part_of(k + 1, 0, 0, 0)
                    transpose_gates(k, par)
                    for e in range(NE):
                        def between():
                            if edges and e > 0:
                                part_of(k + 1, e // 4, (e // 2) % 2, e % 2)
                            if e == 0:
                                gates_times_bo(k)
                            if node and e == AT_CONV:
                                conv(1, k + 1)
                            if node and e == AT_HNT:
                                transpose_hn(k + 1)

                        expert(k, e, between)
                        if node and e == 0:
                            transpose_table(1, k + 1)
                        if node and e == AT_HNT:
                            logits(k + 1, 1 - par)

                with pe.Fori(0, BLOCKS // 2 - 1) as kk:
                    for par in range(2):
                        experts(2 * kk + par, par, True)
                experts(BLOCKS - 3, 0, True)
                experts(BLOCKS - 2, 1, True, edges=False)
                experts(BLOCKS - 1, 0, False)

    @block.vector
    def _(dve):
        v = nc.vector
        dve.sem_inc(s_deg_free, 2)
        dve.sem_inc(s_agg_free, 1)
        dve.sem_inc(s_hid_lo, 2)
        dve.sem_inc(s_y_free, 2)
        count = [0]

        def pre(ins):
            count[0] += 1
            ins.then_inc(s_pre, 1)
            dve.wait_ge(s_pre, count[0])

        def rsqrt(step, y, var, eps, t):
            step(v.reciprocal(y, y))
            step(v.scalar_tensor_tensor(t, var, eps, y, ALU.add, ALU.mult))
            step(v.scalar_tensor_tensor(t, t, -0.5, y, ALU.mult, ALU.mult))
            step(v.tensor_scalar(t, t, -0.75, 1.5, ALU.max, ALU.add))
            step(v.tensor_tensor(y, y, t, ALU.mult))

        dve.wait_ge(s_dst_in, 48)
        dstf = ldst[:, LROW:2 * LROW]
        pre(v.tensor_copy(dstf, ldst[:, 0:LROW].bitcast(I32)))
        dve.sem_inc(s_prep, 1)
        groups = dstf.rearrange("p (h n) -> p h n", h=GROUP)
        pre(v.tensor_reduce(gext[:, 0, :], groups, AX.X, ALU.min))
        inside = ldst[:, 0:LROW]
        pre(v.scalar_tensor_tensor(inside, dstf, NOWHERE - 1, dstf, ALU.is_lt, ALU.mult))
        pre(v.tensor_reduce(gext[:, 1, :], inside.rearrange("p (h n) -> p h n", h=GROUP), AX.X, ALU.max))
        dve.wait_ge(s_pool, 10)
        for q in range(2):
            for h in range(2):
                pre(v.tensor_scalar(diag[:, (2 * q + h) * LROWS:(2 * q + h + 1) * LROWS], ident[0:LROWS, 0:LROWS],
                                    gext[:, q, h:h + 1], None, ALU.mult))
        dve.sem_inc(s_prep, 1)
        dve.wait_ge(s_ew_in, 48)
        ewf = lew[:, LROW:2 * LROW]
        pre(v.scalar_tensor_tensor(ewf, lew[:, 0:LROW], -1.0, lew[:, 0:LROW], ALU.mult, ALU.max))
        pre(v.scalar_tensor_tensor(ewf, ewf, FINITE_MAX, ewf, ALU.is_le, ALU.mult))
        pre(v.tensor_scalar(ewf, ewf, EDGE_MIN, None, ALU.max))
        pre(v.scalar_tensor_tensor(ewf, dstf, NOWHERE - 1, ewf, ALU.is_lt, ALU.mult))
        dve.sem_inc(s_prep, 1)
        dve.wait_ge(s_src_in, 48)
        pre(v.tensor_copy(lsrc[:, LROW:2 * LROW], lsrc[:, 0:LROW].bitcast(I32)))
        dve.sem_inc(s_prep, 1)
        def num(n):
            return room[:, n * NG:(n + 1) * NG]

        gmin, gmax, off, blk, pairf = (num(n) for n in range(5))
        dve.wait_ge(s_prep_pe, LCH + 1)
        for q, t in ((0, gmin), (1, gmax)):
            pre(v.tensor_copy(t.rearrange("p (n h) -> p h n", h=2),
                              psN[:, 0, q * 2 * LROWS:(q + 1) * 2 * LROWS].rearrange("p (h n) -> p h n", h=2)))
        mmin = small[:, 0:2 * PAIRS]
        pre(v.tensor_reduce(mmin, gmin.rearrange("p (m g) -> p m g", g=GROUPS), AX.X, ALU.min))
        pre(v.tensor_tensor(off.rearrange("p (m g) -> p m g", g=GROUPS), gmin.rearrange("p (m g) -> p m g", g=GROUPS),
                            mmin.unsqueeze(2).broadcast_to([128, 2 * PAIRS, GROUPS]), ALU.subtract))
        pre(v.tensor_reduce(scal[:, 0:1], off, AX.X, ALU.max))
        pre(v.tensor_tensor(blk, gmax, gmin, ALU.subtract))
        pre(v.tensor_reduce(scal[:, 1:2], blk, AX.X, ALU.max))
        pre(v.tensor_scalar(scal[:, 2:3], scal[:, 0:1], float(STRETCH - WIN), None, ALU.is_le))
        pre(v.scalar_tensor_tensor(scal[:, 2:3], scal[:, 1:2], float(WIN - 1), scal[:, 2:3], ALU.is_le, ALU.mult))
        pre(v.tensor_scalar(scal[:, 3:4], scal[:, 2:3], -float(PASSES - 1), float(PASSES - 1), ALU.mult, ALU.add))
        pre(v.tensor_scalar(blk, gmax, float(BLOCK), None, ALU.is_ge))
        for b in range(2, BLOCKS):
            pre(v.scalar_tensor_tensor(blk, gmax, float(b * BLOCK), blk, ALU.is_ge, ALU.add))
        pre(v.tensor_scalar(blk, blk, 2.0, float(LEAD_MIN), ALU.mult, ALU.add))
        pre(v.tensor_copy(pairf, pair_i))
        pre(v.scalar_tensor_tensor(blk, blk, float(PAIRS), pairf, ALU.min, ALU.subtract))
        pre(v.tensor_reduce(scal[:, 4:5], blk, AX.X, ALU.max))
        pre(v.tensor_copy(ctrl[0:1, 0:2], scal[0:1, 3:5]))
        pre(v.tensor_scalar(gmin, gmin, scal[:, 2:3], None, ALU.mult))
        pre(v.tensor_scalar(off, off, scal[:, 2:3], None, ALU.mult))
        pre(v.tensor_scalar(place[:, :], mmin, scal[:, 2:3], None, ALU.mult))
        metav = meta[:, :].rearrange("p (m w) -> p m w", w=META)
        pre(v.tensor_copy(metav[0:1, :, 0:GROUPS], off[32:33, :].rearrange("p (m g) -> p m g", g=GROUPS)))
        pre(v.tensor_copy(metav[0:1, :, GROUPS], place[32:33, :]))
        pre(v.tensor_copy(places, place[32:33, :]))
        pre(v.tensor_tensor(rel[:, :].rearrange("p (n a b) -> p n a b", a=2, b=2),
                            psH[:, 0, 0:CHUNKS].rearrange("p (a b n) -> p n a b", a=2, b=2),
                            gmin.rearrange("p (n a) -> p n a", a=2).unsqueeze(3).broadcast_to([128, LROWS, 2, 2]),
                            ALU.subtract))
        dve.wait_ge(s_prep_pe, 2 * LCH + 1)
        pre(v.tensor_copy(ew[:, :].rearrange("p (n c) -> p n c", c=LCH),
                          psY[:, 0, 0:CHUNKS].rearrange("p (c n) -> p n c", c=LCH)))
        rest = room[:, 0:CHUNKS]
        pre(v.tensor_copy(ew3[:, :, 0], ew[:, :]))
        pre(v.tensor_tensor(rest, ew[:, :], ew3[:, :, 0], ALU.subtract))
        pre(v.tensor_copy(ew3[:, :, 1], rest))
        pre(v.tensor_tensor(ew3[:, :, 2], rest, ew3[:, :, 1], ALU.subtract))
        pre(v.tensor_copy(iota[:, :], iota_i[:, :]))
        dve.sem_inc(s_meta, 1)
        dve.wait_ge(s_prep_pe, 3 * LCH + 1)
        v.tensor_copy(srcs[:, :].rearrange("p (n c) -> p n c", c=LCH),
                      psH[:, 1, 0:CHUNKS].rearrange("p (c n) -> p n c", c=LCH)).then_inc(s_srcs, 1)
        extra, lead = control(dve)

        def columns(pb, h):
            return ds(pb * (2 * MC) + h * MC, MC)

        def over_window(t):
            return t.unsqueeze(2).broadcast_to([128, MC, WIN])

        iota_bc = iota[:, :].unsqueeze(1).broadcast_to([128, MC, WIN])

        def stretch_place(pb, h):
            return dve.value_load(meta[0:1, ds(pb * (2 * META) + h * META + GROUPS, 1)], min_val=0, max_val=NP)

        def degree_onehots(pb, h):
            v.tensor_tensor(onehot_b[:, h, :, :], iota_bc, over_window(rel[:, columns(pb, h)]),
                            ALU.is_equal).then_inc(s_deg_oh, 1)
            v.tensor_copy(ew_st[:, h, :, :], ew3[:, columns(pb, h), :]).then_inc(s_deg_oh, 1)

        def degree_take(g, pb, h, at=None):
            m = 2 * g + h
            part = degrow[:, ds(stretch_place(pb, h) if at is None else at[h], STRETCH)]
            dve.wait_ge(s_deg_mm, m + 1)
            v.tensor_tensor(part, part, psA[0:3, h, 0:STRETCH], ALU.add).then_inc(s_deg_free, 1)
            dve.wait_ge(s_deg_free, m + 3)
            carry(dve)

        def degree_pair(g, pb):
            degree_onehots(pb, 0)
            degree_onehots(pb, 1)
            degree_take(g, pb, 0)
            degree_take(g, pb, 1)

        def advance(nth):
            def after(p):
                v.tensor_scalar(rel[:, :], rel[:, :], -float(WIN), None, ALU.add).then_inc(s_adv, 1)
                v.tensor_scalar(place[:, :], place[:, :], float(WIN), None, ALU.add).then_inc(s_adv, 1)
                dve.wait_ge(s_adv, p * 3 + nth * ADVANCES + 2)
                v.tensor_copy(metav[0:1, :, GROUPS], place[32:33, :])
                v.tensor_copy(places, place[32:33, :]).then_inc(s_adv, 1)
                dve.wait_ge(s_adv, p * 3 + nth * ADVANCES + 3)
                carry(dve)
            return after

        def rewind(nth):
            at = nth * ADVANCES + 3 * (PASSES - 1)
            with dve.If(extra > 0):
                v.tensor_scalar(rel[:, :], rel[:, :], float(WIN * (PASSES - 1)), None, ALU.add).then_inc(s_adv, 1)
                v.tensor_scalar(place[:, :], place[:, :], -float(WIN * (PASSES - 1)), None, ALU.add).then_inc(s_adv, 1)
                dve.wait_ge(s_adv, at + 2)
                v.tensor_copy(metav[0:1, :, GROUPS], place[32:33, :])
                v.tensor_copy(places, place[32:33, :]).then_inc(s_adv, 1)
                dve.wait_ge(s_adv, at + 3)
            dve.nop()

        dve.wait_ge(s_degrow_clear, 1)
        extra_passes(dve, extra, 0, degree_pair, advance(0))
        degree_onehots(PAIRS - 1, 0)
        with dve.Fori(0, PAIRS - 1) as i:
            g = extra * PAIRS + i
            degree_onehots(PAIRS - 1 - i, 1)
            regs = [dve.alloc_register(f"stretch{h}") for h in range(2)]
            dve.load(regs, places[0:1, ds((PAIRS - 1 - i) * 2, 2)])
            at = [dve.snap(r, min_val=0, max_val=NP) for r in regs]
            degree_take(g, PAIRS - 1 - i, 0, at)
            degree_onehots(PAIRS - 2 - i, 0)
            degree_take(g, PAIRS - 1 - i, 1, at)
            for r in regs:
                dve.free_register(r)
        degree_onehots(0, 1)
        degree_take(extra * PAIRS + PAIRS - 1, 0, 0)
        degree_take(extra * PAIRS + PAIRS - 1, 0, 1)
        dve.sem_inc(s_degrow, 1)
        rewind(0)
        for b in range(BLOCKS):
            dve.wait_ge(s_x_in[b], 16 if b < BLOCKS - 1 else 32)
            for t in range(BT):
                last = v.bn_stats(stats[:, t, :], x_all[:, b * BT + t, :])
            pre(last)
            for t in range(BT):
                last = v.bn_aggr(mv[:, b * BT + t, :], stats[:, t, :])
            pre(last)
            if b < POOL_BLOCKS:
                dve.sem_inc(s_x_stat, 1)
            else:
                pre(v.tensor_scalar(x_all[:, b * BT:(b + 1) * BT, :], x_all[:, b * BT:(b + 1) * BT, :],
                                    -FINITE_MAX, FINITE_MAX, ALU.max, ALU.min))
        dve.sem_inc(s_var_x, 1)
        dve.wait_ge(s_degT, 1)
        dve.wait_ge(s_sqrt_deg, 1)
        rsqrt(pre, dis[:, :], psN[0:TILE, 1, 0:TILES], 1.0, newton[:, :])
        dve.wait_ge(s_sqrt_x, 1)
        rsqrt(pre, rstd[:, :], mv[:, :, 1], LN_EPS, newton[:, :])
        pre(v.scalar_tensor_tensor(nmr[:, :], mv[:, :, 0], -1.0, rstd[:, :], ALU.mult, ALU.mult))
        pre(v.tensor_scalar(odd[:, :], nmr[:, :], 0.0, 0.0, ALU.mult, ALU.not_equal))
        nil = zero1[0:TILE, :].broadcast_to([TILE, TILES])
        pre(v.copy_predicated(rstd[:, :], odd[:, :], nil))
        pre(v.copy_predicated(nmr[:, :], odd[:, :], nil))
        pre(v.tensor_tensor(drow[:, 0, :], rstd[:, :], dis[:, :], ALU.mult))
        pre(v.tensor_tensor(drow[:, 1, :], nmr[:, :], dis[:, :], ALU.mult))
        dve.sem_inc(s_dis, 1)
        for t in DVE_TILES:
            dve.wait_ge(s_x_clean, min(t // BT + 1, POOL_BLOCKS))
            v.tensor_scalar(x_all[:, t, :], x_all[:, t, :], drow[:, 0, t:t + 1], drow[:, 1, t:t + 1],
                            ALU.mult, ALU.add).then_inc(s_g1_dve, 1)
        dve.wait_ge(s_prep_pe, 3 * LCH + 3)
        pre(v.tensor_copy(par_T, psY[:, 1, 0:10 * NE * HALF].rearrange("p (l i c) -> p l i c", l=2, i=5)))
        b_, g_, be_, m_, v_ = (par_T[:, :, i, :] for i in range(5))
        dve.sem_inc(s_var_par, 1)
        dve.wait_ge(s_sqrt_par, 1)
        rsqrt(pre, hid_s[:, :, :], v_, BN_EPS, hid_b[:, :, :])
        pre(v.tensor_tensor(hid_s[:, :, :], hid_s[:, :, :], g_, ALU.mult))
        pre(v.tensor_tensor(hid_b[:, :, :], b_, m_, ALU.subtract))
        pre(v.tensor_tensor(hid_b[:, :, :], hid_b[:, :, :], hid_s[:, :, :], ALU.mult))
        v.tensor_tensor(hid_b[:, :, :], hid_b[:, :, :], be_, ALU.add).then_inc(s_par, 1)
        dve.wait_ge(s_g1_out, 16 * BLOCKS)
        pre(v.memset(aggT[:, :, :], 0.0))

        def onehots(g, pb, h):
            m = 2 * g + h
            v.tensor_tensor(onehot[:, h, :, :], iota_bc, over_window(rel[:, columns(pb, h)]),
                            ALU.is_equal).then_inc(s_ohc, 1)
            dve.wait_ge(s_ohc, m + 1)
            v.tensor_tensor(onehot[:, h, :, :], onehot[:, h, :, :], over_window(ew[:, columns(pb, h)]),
                            ALU.mult).then_inc(s_oh, 1)

        def take(g, pb, h):
            m = 2 * g + h
            part = aggT[:, :, ds(stretch_place(pb, h), STRETCH)]
            dve.wait_ge(s_used, (m + 1) * GROUPS + GROUPS)
            v.tensor_tensor(part, part, psA[:, :, 0:STRETCH], ALU.add).then_inc(s_agg_free, 1)
            dve.wait_ge(s_agg_free, m + 2)
            carry(dve)

        def pair(g, pb):
            onehots(g, pb, 0)
            onehots(g, pb, 1)
            take(g, pb, 0)
            take(g, pb, 1)

        steps = {0: (s_ch1, CHAIN1), 1: (s_ch2, CHAIN2)}
        place_in = [0]

        def chain(layer, j, ins):
            s, per = steps[layer]
            place_in[0] += 1
            ins.then_inc(s, 1)
            dve.wait_ge(s, j * per + place_in[0])

        def block_stats(layer, j, src_t):
            for t in range(BT):
                last = v.bn_stats(stats[:, t, :], src_t[0:TILE, t, :])
            chain(layer, j, last)
            carry(dve)
            for t in range(BT):
                last = v.bn_aggr(bmv[:, t, :], stats[:, t, :])
            last.then_inc(s_var, 1)

        def block_rstd(layer, j, done, nth):
            dve.wait_ge(s_sqrt, nth)
            rsqrt(lambda ins: chain(layer, j, ins), brstd[:, :], bmv[:, :, 1], LN_EPS, newton[:, 0:BT])
            v.scalar_tensor_tensor(bnmr[:, :], bmv[:, :, 0], -1.0, brstd[:, :], ALU.mult, ALU.mult).then_inc(done, 1)

        def add_own(layer, j):
            n = layer * BLOCKS + j
            place_in[0] = 0
            own = aggT[:, :, ds((BLOCKS - 1 - j) * BLOCK, BLOCK)]
            dve.wait_ge(s_gT, n + 1)
            carry(dve)
            v.tensor_tensor(aggst[:, :, :], own, psN[:, :, 0:BLOCK], ALU.add).then_inc(s_aggst, 1)
            if layer == 0:
                dve.wait_ge(s_aggst, n + 1)
                carry(dve)
                chain(layer, j, v.tensor_tensor(own.bitcast(I32), own.bitcast(I32), own.bitcast(I32), ALU.bitwise_xor))

        def take_conv(layer, j, first=False):
            n = layer * BLOCKS + j
            dve.wait_ge(s_conv, n + 1)
            if layer == 0 and not first:
                dve.wait_ge(s_h_out, 16 * j)
            if layer == 1 and first:
                dve.wait_ge(s_h_out, 16 * BLOCKS)
            for t in range(BT):
                last = v.scalar_tensor_tensor(hc[0:TILE, t, :], psN[0:TILE, t // 2, (t % 2) * D:(t % 2 + 1) * D],
                                              dis[:, ds((BLOCKS - 1 - j) * BT + t, 1)], gvec[:, 0, :],
                                              ALU.mult, ALU.add)
            last.then_inc(s_conv_ev, 1)
            dve.wait_ge(s_conv_ev, n + 1)

        def clean_conv(layer, j):
            hcf = hc[0:TILE, :, :].rearrange("p t d -> p (t d)")
            chain(layer, j, v.tensor_scalar(bad[:, :], hcf, 0.0, 0.0, ALU.mult, ALU.not_equal))
            carry(dve)
            chain(layer, j, v.copy_predicated(hcf, bad[:, :], zero1[0:TILE, :].broadcast_to([TILE, BT * D])))

        def variance(layer, j):
            block_stats(layer, j, hc)

        def rstd_of(layer, j):
            block_rstd(layer, j, s_stat, j + 1 if layer == 0 else BLOCKS + 2 * j + 1)

        def clean_x(j):
            dve.wait_ge(s_hres_in, (j + 1) * 16)
            if isinstance(j, int):
                dve.wait_ge(s_x_last, 32)
            v.tensor_scalar(h_res[0:TILE, :, :], h_res[0:TILE, :, :], -FINITE_MAX, FINITE_MAX,
                            ALU.max, ALU.min).then_inc(s_clean, 1)

        def gain_and_shift(layer, j):
            n = layer * BLOCKS + j
            h = hc[0:TILE, :, :]

            def bc(i):
                return gvec[:, i, :].unsqueeze(1).broadcast_to([TILE, BT, D])

            dve.wait_ge(s_norm, (n + 1) * BT)
            chain(layer, j, v.tensor_tensor(h, h, bc(1), ALU.mult))
            chain(layer, j, v.tensor_tensor(h, h, bc(2), ALU.add))

        def relu_and_residual(layer, j):
            n = layer * BLOCKS + j
            h = hc[0:TILE, :, :]
            chain(layer, j, v.scalar_tensor_tensor(h, h, FINITE_MAX, h, ALU.is_le, ALU.mult))
            if layer == 0:
                dve.wait_ge(s_h0, (j + 1) * BT)
            else:
                dve.wait_ge(s_hres_in, (n + 1) * 16)
            v.scalar_tensor_tensor(h, h, 0.0, h_res[0:TILE, :, :], ALU.max, ALU.add).then_inc(s_h, 1)

        def start_x1(j, par, arrived, last=False):
            h = hc[0:TILE, :, :]
            dve.wait_ge(s_h, BLOCKS + j + 1)
            keep = h_res[0:TILE, :, :].bitcast(I32)
            hi32 = h.bitcast(I32)
            chain(1, j, v.tensor_scalar(keep, h, FINITE_MAX, -1.0, ALU.is_le, ALU.mult))
            chain(1, j, v.tensor_tensor(hi32, hi32, keep, ALU.bitwise_and))
            dve.wait_ge(s_x_blk[par], arrived)
            if last:
                dve.wait_ge(s_x_last, 64)
            a = acc[par][0:TILE, :, :]
            chain(1, j, v.tensor_tensor(a, a, h, ALU.add))

        def x1_variance(j, par):
            block_stats(1, j, acc[par])

        def x1_rstd(j):
            block_rstd(1, j, s_stat2, BLOCKS + 2 * j + 2)

        def hnT_low(j, par):
            dve.wait_ge(s_hnT_hi, j + 1)
            v.tensor_tensor(hnT_lo[par][:, :, :], psN[:, :, 0:BLOCK], hnT_hi[par][:, :, :].bitcast(F32),
                            ALU.subtract).then_inc(s_hnT_lo, 1)

        def logits_less_max(j):
            dve.wait_ge(s_logit, j + 1)
            chain(1, j, v.tensor_tensor(logit[:, :, :], psN[0:TILE, 0, 0:BT * NE].rearrange("p (t e) -> p t e", e=NE),
                                        br_bc[:, :].unsqueeze(1).broadcast_to([TILE, BT, NE]), ALU.add))
            chain(1, j, v.tensor_reduce(lmax[:, :], logit[:, :, :], AX.X, ALU.max))
            v.tensor_tensor(logit[:, :, :], logit[:, :, :], lmax[:, :].unsqueeze(2).broadcast_to([TILE, BT, NE]),
                            ALU.subtract).then_inc(s_lsub, 1)

        def finish_gates(j, par):
            dve.wait_ge(s_exp, j + 1)
            chain(1, j, v.tensor_reduce(lsum[:, :], logit[:, :, :], AX.X, ALU.add))
            chain(1, j, v.reciprocal(lsum[:, :], lsum[:, :]))
            v.tensor_tensor(gate[par][:, :, :], logit[:, :, :], lsum[:, :].unsqueeze(2).broadcast_to([TILE, BT, NE]),
                            ALU.mult).then_inc(s_gate, 1)

        def start_acc(j, par):
            dve.wait_ge(s_gbo, j + 1)
            a = acc[par][0:TILE, :, :].rearrange("p (u t) d -> p u (t d)", u=2)
            v.tensor_tensor(a, a, psN[0:TILE, :, :], ALU.add).then_inc(s_acc0, 1)

        def low_half(k, idx, l, m):
            n = k * HALVES + idx
            dve.wait_ge(s_hid_hi, n + 1)
            v.tensor_tensor(hid_lo[l][:, m, :], hid[:, m, :], hid_hi[l][:, m, :].bitcast(F32),
                            ALU.subtract).then_inc(s_hid_lo, 1)

        def expert(k, e, par, between):
            for m in range(HALF):
                low_half(k, 4 * e + 2 + m, 1, m)
            if e + 1 < NE:
                for m in range(HALF):
                    low_half(k, 4 * (e + 1) + m, 0, m)
            between()
            for u in range(2):
                n = (k * NE + e) * 2 + u
                if e == 0:
                    dve.wait_ge(s_acc0, k + 1)
                else:
                    dve.wait_ge(s_y_free, n - 2 + 1 + 2)
                dve.wait_ge(s_y, n + 1)
                for t in (2 * u, 2 * u + 1):
                    last = v.scalar_tensor_tensor(acc[par][0:TILE, t, :], psY[0:TILE, u, (t % 2) * D:(t % 2 + 1) * D],
                                                  gate[par][:, t, e:e + 1], acc[par][0:TILE, t, :], ALU.mult, ALU.add)
                last.then_inc(s_y_free, 1)

        for layer in range(2):
            first = extra * (PAIRS * (layer + 1)) + PAIRS * layer
            extra_passes(dve, extra, extra * (PAIRS * layer) + PAIRS * layer, pair, advance(layer + 1))
            onehots(first, PAIRS - 1, 0)
            with dve.Fori(0, lead) as i:
                g = first + i
                onehots(g, PAIRS - 1 - i, 1)
                take(g, PAIRS - 1 - i, 0)
                with dve.If(i + 1 < PAIRS):
                    onehots(g + 1, within(PAIRS - 2 - i, 0, PAIRS - 2), 0)
                take(g, PAIRS - 1 - i, 1)

            def ahead(j, a, h):
                with dve.If(lead + 2 * j + a < PAIRS):
                    onehots(first + lead + 2 * j + a, within(PAIRS - 1 - lead - 2 * j - a, 0, PAIRS - 1 - LEAD_MIN), h)

            def took(j, a, h):
                with dve.If(lead + 2 * j + a < PAIRS):
                    take(first + lead + 2 * j + a, within(PAIRS - 1 - lead - 2 * j - a, 0, PAIRS - 1 - LEAD_MIN), h)

            def node_beside_edges(j, first=False, edges=True):
                ifs = (lambda f, *a: f(j, *a)) if edges else (lambda f, *a: None)
                add_own(layer, j)
                ifs(ahead, 0, 1)
                ifs(took, 0, 0)
                if first:
                    dve.wait_ge(s_gvec_in, 64 * (layer + 1))
                take_conv(layer, j, first=first)
                clean_conv(layer, j)
                ifs(ahead, 1, 0)
                variance(layer, j)
                ifs(took, 0, 1)
                if layer == 0:
                    clean_x(j)
                rstd_of(layer, j)
                ifs(ahead, 1, 1)
                if layer == 1:
                    gain_and_shift(1, 0)
                    relu_and_residual(1, 0)
                    start_x1(0, 0, 16, last=True)
                    x1_variance(0, 0)
                    took(0, 1, 0)
                    x1_rstd(0)
                    hnT_low(0, 0)
                    logits_less_max(0)
                    took(0, 1, 1)
                    ahead(0, 2, 0)
                    return
                ifs(took, 1, 0)
                gain_and_shift(layer, j)
                relu_and_residual(layer, j)
                ifs(ahead, 2, 0)

            if layer == 0:
                node_beside_edges(0, first=True)
                took(0, 1, 1)
                with dve.Fori(1, BLOCKS - 1) as j:
                    node_beside_edges(j)
                    took(j, 1, 1)
                    dve.nop()
                node_beside_edges(BLOCKS - 1, edges=False)
                rewind(1)
            else:
                node_beside_edges(0, first=True)

                def experts(k, par, node, arrived=0, edges=True):
                    def took_if(*at):
                        if edges:
                            took(k + 1, *at)

                    def ahead_if(*at):
                        if edges:
                            ahead(k + 1, *at)

                    finish_gates(k, par)
                    for m in range(HALF):
                        low_half(k, m, 0, m)
                    for e in range(NE):
                        def between():
                            if e == 0:
                                start_acc(k, par)
                            if not node:
                                return
                            if e == AT_CONV:
                                take_conv(1, k + 1)
                            if e == AT_VARIANCE:
                                variance(1, k + 1)
                            if e == AT_RSTD and edges:
                                rstd_of(1, k + 1)
                            if e == (AT_GAIN if edges else AT_GAIN - 1):
                                gain_and_shift(1, k + 1)
                            if e == (AT_X1 if edges else AT_X1 - 1):
                                start_x1(k + 1, 1 - par, arrived)
                            if e == AT_X1 and not edges:
                                x1_variance(k + 1, 1 - par)
                            if e == AT_X1_RSTD:
                                x1_rstd(k + 1)
                            if e == AT_HNT:
                                hnT_low(k + 1, 1 - par)

                        expert(k, e, par, between)
                        if not node:
                            continue
                        if e == 0:
                            ahead_if(0, 1)
                            add_own(1, k + 1)
                        if e == AT_CONV:
                            took_if(0, 0)
                            clean_conv(1, k + 1)
                        if e == AT_VARIANCE:
                            ahead_if(1, 0)
                            if not edges:
                                rstd_of(1, k + 1)
                        if e == AT_RSTD:
                            took_if(0, 1)
                            ahead_if(1, 1)
                        if e == (AT_GAIN if edges else AT_GAIN - 1):
                            relu_and_residual(1, k + 1)
                        if e == AT_X1 and edges:
                            took_if(1, 0)
                            x1_variance(k + 1, 1 - par)
                        if e == AT_X1_RSTD:
                            ahead_if(2, 0)
                        if e == AT_HNT:
                            logits_less_max(k + 1)
                            took_if(1, 1)

                with dve.Fori(0, BLOCKS // 2 - 1) as kk:
                    for par in range(2):
                        experts(2 * kk + par, par, True, (kk + 1 + par) * 16)
                experts(BLOCKS - 3, 0, True, 3 * 16)
                experts(BLOCKS - 2, 1, True, 4 * 16, edges=False)
                experts(BLOCKS - 1, 0, False)
                assert place_in[0] == CHAIN2


_NAMES = ["x", "src", "dst", "edge_weight"] \
    + ["L0_gnn_" + n for n in ("W1", "b1", "ln_g1", "ln_b1", "W2", "b2", "ln_g2", "ln_b2")] \
    + ["L0_ffn_" + n for n in ("Wr", "br", "W1", "b1", "g1", "be1", "m1", "v1", "W2", "b2", "g2", "be2", "m2", "v2",
                               "Wo", "bo")]


def kernel(**inputs):
    import numpy as _np
    import concourse.bacc as _bacc
    from concourse import mybir as _mybir
    from concourse.bass_utils import run_bass_kernel_spmd as _run

    nc = _bacc.Bacc("TRN2", target_bir_lowering=False, num_devices=1, dynamic_dma_scratch_size=8192)
    arrays, a = {}, {}
    for name in _NAMES:
        host = _np.ascontiguousarray(inputs[name])
        arrays["in_" + name] = host
        a[name] = nc.dram_tensor("in_" + name, host.shape, _mybir.dt.from_np(host.dtype), kind="ExternalInput").ap()
    out = nc.dram_tensor("out_0", (N, D), F32, kind="ExternalOutput").ap()

    def g(n):
        return a["L0_gnn_" + n]

    def f(n):
        return a["L0_ffn_" + n]

    build_program(nc, a["x"], a["src"], a["dst"], a["edge_weight"], (g("W1"), g("W2")), (g("b1"), g("b2")),
                  (g("ln_g1"), g("ln_g2")), (g("ln_b1"), g("ln_b2")), f("Wr"), f("br"),
                  [f(n) for n in ("b1", "g1", "be1", "m1", "v1")], [f(n) for n in ("b2", "g2", "be2", "m2", "v2")],
                  f("W1"), f("W2"), f("Wo"), f("bo"), out)
    r = _run(nc, [arrays], core_ids=[0])
    return r.results[0]["out_0"]
```
